# Optimizing a Trainium2 kernel written in Bass

```python
import numpy as np
import jax
import jax.numpy as jnp

def _softmax(x, axis=-1):
    return jax.nn.softmax(x, axis=axis)

def _gelu(x):
    return jax.nn.gelu(x, approximate=True)

def _silu(x):
    return jax.nn.silu(x)

def _sigmoid(x):
    return jax.nn.sigmoid(x)

def _layernorm(x, axis=-1, eps=1e-05):
    m = jnp.mean(x, axis=axis, keepdims=True)
    v = jnp.var(x, axis=axis, keepdims=True)
    return (x - m) / jnp.sqrt(v + eps)

def _scatter_add(tgt, idx, src, axis=0):
    return tgt.at[idx].add(src)

def _segment_sum(src, seg, n):
    return jax.ops.segment_sum(src, seg, n)
kernel_name = 'mk_prb_d2_jaxref_r8_de883c'

def setup_inputs(seed: int=0):
    np.random.seed(seed)
    _w = jnp.asarray

    def _L0_attn_setup():
        import jax, jax.numpy as jnp
        import numpy as np
        DM = 128
        NH = 16
        key = jax.random.key(seed)
        ks = jax.random.split(key, 9)
        B, S = (8, 128)
        sc = 1.0 / np.sqrt(DM)
        return {'x': jax.random.normal(ks[0], (B, S, DM), jnp.float32), 'Wq': jax.random.normal(ks[1], (DM, DM), jnp.float32) * sc, 'bq': jax.random.normal(ks[2], (DM,), jnp.float32) * 0.02, 'Wk': jax.random.normal(ks[3], (DM, DM), jnp.float32) * sc, 'bk': jax.random.normal(ks[4], (DM,), jnp.float32) * 0.02, 'Wv': jax.random.normal(ks[5], (DM, DM), jnp.float32) * sc, 'bv': jax.random.normal(ks[6], (DM,), jnp.float32) * 0.02, 'Wo': jax.random.normal(ks[7], (DM, DM), jnp.float32) * sc, 'bo': jax.random.normal(ks[8], (DM,), jnp.float32) * 0.02}
    _L0_attn_in = _L0_attn_setup()

    def _L0_ffn_setup():
        import jax, jax.numpy as jnp
        import numpy as np
        B, S, D, H, E = (4, 256, 128, 512, 8)
        key = jax.random.key(seed)
        ks = jax.random.split(key, 8)
        s_d = 1.0 / np.sqrt(D)
        s_h = 1.0 / np.sqrt(H)
        return {'x': jax.random.normal(ks[0], (B, S, D), dtype=jnp.float32), 'gate_w': jax.random.uniform(ks[1], (E, D), jnp.float32, -s_d, s_d), 'gate_b': jax.random.uniform(ks[2], (E,), jnp.float32, -s_d, s_d), 'w1': jax.random.uniform(ks[3], (E, H, D), jnp.float32, -s_d, s_d), 'b1': jax.random.uniform(ks[4], (E, H), jnp.float32, -s_d, s_d), 'w2': jax.random.uniform(ks[5], (E, D, H), jnp.float32, -s_h, s_h), 'b2': jax.random.uniform(ks[6], (E, D), jnp.float32, -s_h, s_h)}
    _L0_ffn_in = _L0_ffn_setup()

    def _L1_attn_setup():
        import jax, jax.numpy as jnp
        import numpy as np
        N_EMBD = 128
        BLOCK_SIZE = 256
        ATTN_SPAN = 32
        LN_EPS = 1e-05

        def _band_mask(T, span, dtype):
            ones = jnp.ones((T, T), dtype=dtype)
            return jnp.tril(ones, 0) * (1.0 - jnp.tril(ones, -span))

        def _layer_norm(h, w, b):
            mu = jnp.mean(h, axis=-1, keepdims=True)
            var = jnp.var(h, axis=-1, keepdims=True)
            return (h - mu) * jax.lax.rsqrt(var + LN_EPS) * w + b
        key = jax.random.key(seed)
        k_x, k_w, k_b, k_lw = jax.random.split(key, 4)
        B, T, C = (4, BLOCK_SIZE, N_EMBD)
        x = jax.random.normal(k_x, (B, T, C), dtype=jnp.float32)
        lim = 1.0 / np.sqrt(C)
        W_qkv = jax.random.uniform(k_w, (C, 3 * C), minval=-lim, maxval=lim, dtype=jnp.float32)
        b_qkv = jax.random.uniform(k_b, (3 * C,), minval=-lim, maxval=lim, dtype=jnp.float32)
        ln_w = jnp.ones((C,), dtype=jnp.float32)
        ln_b = jnp.zeros((C,), dtype=jnp.float32)
        return {'x': x, 'W_qkv': W_qkv, 'b_qkv': b_qkv, 'ln_w': ln_w, 'ln_b': ln_b}
    _L1_attn_in = _L1_attn_setup()

    def _L1_ffn_setup():
        import jax, jax.numpy as jnp
        import numpy as np
        D_MODEL = 128
        N_EXPERTS = 8
        TOP_K = 2
        HIDDEN = 4 * D_MODEL
        key = jax.random.key(seed)
        ks = jax.random.split(key, 6)
        B, S = (2, 256)
        x = jax.random.normal(ks[0], (B, S, D_MODEL), dtype=jnp.float32)
        shared_w1 = jax.random.normal(ks[1], (HIDDEN, D_MODEL), dtype=jnp.float32) * 0.02
        shared_w2 = jax.random.normal(ks[2], (D_MODEL, HIDDEN), dtype=jnp.float32) * 0.02
        experts_w1 = jax.random.normal(ks[3], (N_EXPERTS, HIDDEN, D_MODEL), dtype=jnp.float32) * 0.02
        experts_w2 = jax.random.normal(ks[4], (N_EXPERTS, D_MODEL, HIDDEN), dtype=jnp.float32) * 0.02
        gate_w = jax.random.normal(ks[5], (N_EXPERTS, D_MODEL), dtype=jnp.float32) * 0.02
        return {'x': x, 'shared_w1': shared_w1, 'shared_w2': shared_w2, 'experts_w1': experts_w1, 'experts_w2': experts_w2, 'gate_w': gate_w}
    _L1_ffn_in = _L1_ffn_setup()
    _d = {'L0_attn_x': _L0_attn_in['x'], 'L0_attn_Wq': _L0_attn_in['Wq'], 'L0_attn_bq': _L0_attn_in['bq'], 'L0_attn_Wk': _L0_attn_in['Wk'], 'L0_attn_bk': _L0_attn_in['bk'], 'L0_attn_Wv': _L0_attn_in['Wv'], 'L0_attn_bv': _L0_attn_in['bv'], 'L0_attn_Wo': _L0_attn_in['Wo'], 'L0_attn_bo': _L0_attn_in['bo'], 'L0_ffn_gate_w': _L0_ffn_in['gate_w'], 'L0_ffn_gate_b': _L0_ffn_in['gate_b'], 'L0_ffn_w1': _L0_ffn_in['w1'], 'L0_ffn_b1': _L0_ffn_in['b1'], 'L0_ffn_w2': _L0_ffn_in['w2'], 'L0_ffn_b2': _L0_ffn_in['b2'], 'L1_attn_W_qkv': _L1_attn_in['W_qkv'], 'L1_attn_b_qkv': _L1_attn_in['b_qkv'], 'L1_attn_ln_w': _L1_attn_in['ln_w'], 'L1_attn_ln_b': _L1_attn_in['ln_b'], 'L1_ffn_shared_w1': _L1_ffn_in['shared_w1'], 'L1_ffn_shared_w2': _L1_ffn_in['shared_w2'], 'L1_ffn_experts_w1': _L1_ffn_in['experts_w1'], 'L1_ffn_experts_w2': _L1_ffn_in['experts_w2'], 'L1_ffn_gate_w': _L1_ffn_in['gate_w']}
    _x0 = _d['L0_attn_x']
    _d['L0_attn_x'] = jax.random.normal(jax.random.fold_in(jax.random.key(seed), 1), (32, 256, 128), dtype=_x0.dtype)
    del _x0
    return _d

def reference(L0_attn_x, L0_attn_Wq, L0_attn_bq, L0_attn_Wk, L0_attn_bk, L0_attn_Wv, L0_attn_bv, L0_attn_Wo, L0_attn_bo, L0_ffn_gate_w, L0_ffn_gate_b, L0_ffn_w1, L0_ffn_b1, L0_ffn_w2, L0_ffn_b2, L1_attn_W_qkv, L1_attn_b_qkv, L1_attn_ln_w, L1_attn_ln_b, L1_ffn_shared_w1, L1_ffn_shared_w2, L1_ffn_experts_w1, L1_ffn_experts_w2, L1_ffn_gate_w):

    def _L0_attn_ref(x, Wq, bq, Wk, bk, Wv, bv, Wo, bo):
        import jax, jax.numpy as jnp
        import numpy as np
        DM = 128
        NH = 16
        B, S, dm = x.shape
        H = NH
        dk = dm // H
        Q = (x @ Wq.T + bq).reshape(B, S, H, dk)
        K = (x @ Wk.T + bk).reshape(B, S, H, dk)
        V = (x @ Wv.T + bv).reshape(B, S, H, dk)
        scores = jnp.einsum('bqhd,bkhd->hbqk', Q, K)
        attn = jax.nn.softmax(scores, axis=1)
        heads = jnp.einsum('hbqk,bkhd->bqhd', attn, V).reshape(B, S, dm)
        return heads @ Wo.T + bo

    def _L0_ffn_ref(x, gate_w, gate_b, w1, b1, w2, b2):
        import jax, jax.numpy as jnp
        import numpy as np
        B, S, D, H, E = (4, 256, 128, 512, 8)
        b, s, d = x.shape
        xf = x.reshape(-1, d)
        logits = xf @ gate_w.T + gate_b
        top1 = jnp.argmax(logits, axis=-1)
        out = jnp.zeros_like(xf)
        n_experts = w1.shape[0]
        for e in range(n_experts):
            h = jax.nn.relu(xf @ w1[e].T + b1[e])
            y = h @ w2[e].T + b2[e]
            out = out + jnp.where((top1 == e)[:, None], y, jnp.zeros((), y.dtype))
        return out.reshape(b, s, d)

    def _L1_attn_ref(x, W_qkv, b_qkv, ln_w, ln_b):
        import jax, jax.numpy as jnp
        import numpy as np
        N_EMBD = 128
        BLOCK_SIZE = 256
        ATTN_SPAN = 32
        LN_EPS = 1e-05

        def _band_mask(T, span, dtype):
            ones = jnp.ones((T, T), dtype=dtype)
            return jnp.tril(ones, 0) * (1.0 - jnp.tril(ones, -span))

        def _layer_norm(h, w, b):
            mu = jnp.mean(h, axis=-1, keepdims=True)
            var = jnp.var(h, axis=-1, keepdims=True)
            return (h - mu) * jax.lax.rsqrt(var + LN_EPS) * w + b
        B, T, C = x.shape
        qkv = x @ W_qkv + b_qkv
        q, k, v = jnp.split(qkv, 3, axis=-1)
        scale = np.sqrt(C * ATTN_SPAN).astype(np.float32)
        scores = jnp.einsum('bid,bjd->bij', q, k) / scale
        scores = scores * _band_mask(T, ATTN_SPAN, x.dtype)[None, :, :]
        out = jnp.einsum('bij,bjd->bid', scores, v)
        return _layer_norm(out, ln_w, ln_b)

    def _L1_ffn_ref(x, shared_w1, shared_w2, experts_w1, experts_w2, gate_w):
        import jax, jax.numpy as jnp
        import numpy as np
        D_MODEL = 128
        N_EXPERTS = 8
        TOP_K = 2
        HIDDEN = 4 * D_MODEL
        B, S, D = x.shape
        T = B * S
        x_flat = x.reshape(T, D)
        shared = jnp.einsum('td,dh->th', x_flat, shared_w1.T)
        shared = jnp.einsum('th,hd->td', jax.nn.silu(shared), shared_w2.T)
        gate_logits = x_flat @ gate_w.T
        top_k_gates, top_k_idx = jax.lax.top_k(gate_logits, TOP_K)
        top_k_gates = jax.nn.softmax(top_k_gates, axis=1)
        gates = jnp.zeros((T, N_EXPERTS), dtype=x.dtype)
        gates = gates.at[jnp.arange(T)[:, None], top_k_idx].set(top_k_gates)
        h = jnp.einsum('td,ehd->teh', x_flat, experts_w1)
        expert_out = jnp.einsum('teh,edh->ted', jax.nn.silu(h), experts_w2)
        selected = jnp.einsum('ted,te->td', expert_out, gates)
        return (shared + selected).reshape(B, S, D)
    x = L0_attn_x
    xn = _layernorm(x, axis=-1)
    x = x + _L0_attn_ref(xn, L0_attn_Wq, L0_attn_bq, L0_attn_Wk, L0_attn_bk, L0_attn_Wv, L0_attn_bv, L0_attn_Wo, L0_attn_bo) + _L0_ffn_ref(xn, L0_ffn_gate_w, L0_ffn_gate_b, L0_ffn_w1, L0_ffn_b1, L0_ffn_w2, L0_ffn_b2)
    xn = _layernorm(x, axis=-1)
    x = x + _L1_attn_ref(xn, L1_attn_W_qkv, L1_attn_b_qkv, L1_attn_ln_w, L1_attn_ln_b) + _L1_ffn_ref(xn, L1_ffn_shared_w1, L1_ffn_shared_w2, L1_ffn_experts_w1, L1_ffn_experts_w2, L1_ffn_gate_w)
    return x

_drawn_inputs = setup_inputs


def setup_inputs(seed=0):
    import zlib

    import numpy as np

    out = dict(_drawn_inputs(seed))
    spreads = {'L1_attn_ln_w': (1.0, 0.2), 'L1_attn_ln_b': (0.0, 0.1)}
    factors = {'L0_attn_bo': 5.743,
     'L0_ffn_b1': 6.29,
     'L0_ffn_b2': 5.04,
     'L1_ffn_shared_w1': 3.068,
     'L1_ffn_shared_w2': 3.024,
     'L1_ffn_experts_w1': 4.308,
     'L1_ffn_experts_w2': 4.284,
     'L1_ffn_gate_w': 5.008}
    for name, (base, spread) in spreads.items():
        noise = np.random.default_rng([zlib.crc32(name.encode()), seed]).standard_normal(out[name].shape)
        drawn = base * np.exp(spread * noise) if base else spread * noise
        out[name] = jnp.asarray(drawn.astype(out[name].dtype))
    for name, factor in factors.items():
        out[name] = (out[name] * factor).astype(out[name].dtype)
    return out
```

```python
import concourse.bass as bass
from concourse import mybir
from contextlib import ExitStack

F32 = mybir.dt.float32
BF16 = mybir.dt.bfloat16
ALU = mybir.AluOpType
ACT = mybir.ActivationFunctionType
AX = mybir.AxisListType

P = 128
B, S, D = 32, 256, 128
T = B * S
TT = 512
NT = T // TT
SUB = TT // P
NS = T // P
H = 16
DK = D // H
E = 8
HID = 512
HC = HID // P
EPS = 1e-5
SPAN = 32
SCALE1 = 1.0 / float((D * SPAN) ** 0.5)
NPART = 3
KROWS = NPART * NPART * DK
BG = 4
NBG = B // BG
PRIO_NONE = -3.0e38


def sweep(eng, n, body):
    body(0, 0)
    body(1, 1)
    with eng.Fori(1, n // 2 - 1) as i:
        body(2 * i, 0)
        body(2 * i + 1, 1)
    body(n - 2, 0)
    body(n - 1, 1)


def is_last(t, n):
    return isinstance(t, int) and t == n - 1


def started(t, k):
    return not isinstance(t, int) or t >= k


def chain(eng, sem, base):
    state = [0]

    def link(ins):
        state[0] += 1
        ins.then_inc(sem, 1)
        eng.wait_ge(sem, base + state[0])
    return link


def norm_factors(pool, link, st, mean, rstd, tmp, half, share, eps, mhalf):
    (m_even, v_even), (m_odd, v_odd) = ((st[:, :, i + 1], st[:, :, i + 2]) for i in (0, 3))
    link(pool.tensor_tensor(mean, m_even, m_odd, ALU.add))
    link(pool.tensor_tensor(mean, mean, half, ALU.mult))
    link(pool.tensor_tensor(tmp, m_even, mean, ALU.subtract))
    link(pool.tensor_tensor(tmp, tmp, tmp, ALU.mult))
    link(pool.tensor_tensor(rstd, v_even, v_odd, ALU.add))
    link(pool.tensor_tensor(rstd, rstd, share, ALU.mult))
    link(pool.tensor_tensor(rstd, rstd, tmp, ALU.add))
    link(pool.tensor_tensor(rstd, rstd, eps, ALU.add))
    return pool.tensor_tensor(rstd, rstd, mhalf, ALU.pow)


NORM_LINKS = 8


def layer_kernel(nc, x, Wq, bq, Wk, bk, Wv, bv, Wo, bo, gate0_w, gate0_b, w1_0, b1_0, w2_0, b2_0,
                 W_qkv, b_qkv, ln_w, ln_b, sh_w1, sh_w2, w1_1, w2_1, gate1_w, out):
    x_v = x.rearrange("b (u p) d -> p (b u) d", p=P)
    out_v = out.rearrange("b (u p) d -> p (b u) d", p=P)

    xnT_d = nc.dram_tensor("xnT_d", [P, T], F32).ap()
    qs_d = nc.dram_tensor("qs_d", [NPART, D, T], BF16).ap()
    ks_d = nc.dram_tensor("ks_d", [NPART, D, T], BF16).ap()
    oT_d = nc.dram_tensor("oT_d", [D, T], F32).ap()
    x1_d = nc.dram_tensor("x1_d", [P, NS, D], F32).ap()
    xn1T_d = nc.dram_tensor("xn1T_d", [P, T], F32).ap()

    ctx = ExitStack()
    with ctx:
        def sb(name, shape, dt=F32, c=ctx):
            return c.enter_context(nc.sbuf_tensor(name, shape, dt))

        def pb(name, shape, c, dt=F32):
            return c.enter_context(nc.psum_tensor(name, shape, dt))

        def sem(name):
            return ctx.enter_context(nc.semaphore(name))

        ident = sb("ident", [P, P])
        identb = sb("identb", [P, P], BF16)
        wT = sb("wT", [P, 4, P])
        g0T = sb("g0T", [P, E])
        g1T = sb("g1T", [P, E])
        bqc = sb("bqc", [P, 1])
        bkc = sb("bkc", [P, 1])
        bv_bc = sb("bv_bc", [P, D])
        gb_bc = sb("gb_bc", [P, E])
        prio = sb("prio", [P, E])
        norm_c = [sb(f"norm_c{n}", [P, SUB]) for n in range(4)]
        V = sb("V", [P, NS, D])
        G0 = sb("G0", [P, NS, E])
        G1 = sb("G1", [P, NS, E])

        with ExitStack() as ph:
            wload = sb("wload", [P, 4, P], F32, ph)
            gload = sb("gload", [E, 2, P], F32, ph)
            xt = sb("xt", [P, 2, SUB, D], F32, ph)
            xn = sb("xn", [P, 2, SUB, D], F32, ph)
            xnT = sb("xnT", [P, 2, TT], F32, ph)
            st = sb("st", [P, 2, SUB, 6], F32, ph)
            mean = sb("mean", [P, 2, SUB], F32, ph)
            tmp = sb("tmp", [P, SUB], F32, ph)
            rs = sb("rs", [P, 2, SUB], F32, ph)
            qf = sb("qf", [P, 2, TT], F32, ph)
            rem = sb("rem", [P, 2, TT], F32, ph)
            parts = sb("parts", [P, 2, 2, NPART, TT], BF16, ph)
            pX = pb("pX", [P, TT], ph)
            pQ = pb("pQ", [P, TT], ph)
            pK = pb("pK", [P, TT], ph)
            pV = pb("pV", [P, SUB, D], ph)
            pL = pb("pL", [P, SUB, E], ph)
            pW = pb("pW", [P, 4, P], ph)
            pG = pb("pG", [P, 2, E], ph)

            a_w = sem("a_w")
            a_const = sem("a_const")
            a_wT = sem("a_wT")
            a_wTs = sem("a_wTs")
            a_x = [sem("a_x0"), sem("a_x1")]
            a_st = sem("a_st")
            a_ve = sem("a_ve")
            a_rs = sem("a_rs")
            a_xn = sem("a_xn")
            a_tr = sem("a_tr")
            a_xT = sem("a_xT")
            a_xTd = [sem("a_xTd0"), sem("a_xTd1")]
            a_q = sem("a_q")
            a_v = sem("a_v")
            a_qf = sem("a_qf")
            a_mid = sem("a_mid")
            a_rem = sem("a_rem")
            a_low = sem("a_low")
            a_vs = sem("a_vs")
            a_pd = [sem("a_pd0"), sem("a_pd1")]
            WLOADS = 10

            block = ph.enter_context(nc.Block())

            @block.sync
            def _(sp):
                for n, w in enumerate((Wq, Wk, Wv, Wo)):
                    sp.dma_start(wload[:, n, :], w).then_inc(a_w, 16)
                sp.dma_start(gload[:, 0, :], gate0_w).then_inc(a_w, 16)
                sp.dma_start(gload[:, 1, :], gate1_w).then_inc(a_w, 16)
                sp.dma_start(bqc[:], bq.rearrange("(p a) -> p a", a=1)).then_inc(a_w, 16)
                sp.dma_start(bkc[:], bk.rearrange("(p a) -> p a", a=1)).then_inc(a_w, 16)
                sp.dma_start(bv_bc[:], bv.partition_broadcast(P)).then_inc(a_w, 16)
                sp.dma_start(gb_bc[:], gate0_b.partition_broadcast(P)).then_inc(a_w, 16)

                def body(t, s):
                    if started(t, 2):
                        sp.wait_ge(a_xn, t - 1)
                    sp.dma_start(xt[:, s, :, :], x_v[:, bass.ds(t * SUB, SUB), :]).then_inc(a_x[s], 16)
                sweep(sp, NT, body)

            @block.gpsimd
            def _(pool):
                pool.memset(ident[:], 0.0).then_inc(a_const, 1)
                pool.memset(identb[:], 0.0).then_inc(a_const, 1)
                for c, value in zip(norm_c, (0.5, 1.0 / D, EPS, -0.5)):
                    pool.memset(c[:], value).then_inc(a_const, 1)
                for e in range(E):
                    pool.memset(prio[:, e:e + 1], float(E - e)).then_inc(a_const, 1)
                pool.wait_ge(a_const, 6 + E)
                for m in (ident, identb):
                    pool.affine_select(out=m[:], in_=m[:], compare_op=ALU.not_equal, fill=1.0, base=0,
                                       pattern=[[-1, P]], channel_multiplier=1).then_inc(a_const, 1)

                def norm(t, s):
                    pool.wait_ge(a_st, t + 1)
                    norm_factors(pool, chain(pool, a_ve, NORM_LINKS * t), st[:, s, :, :], mean[:, s, :],
                                 rs[:, s, :], tmp[:], *(c[:] for c in norm_c)).then_inc(a_rs, 1)

                def body(t, s):
                    if not is_last(t, NT):
                        norm(t + 1, 1 - s)
                    for n in range(2):
                        pool.wait_ge(a_qf, 4 * t + 2 * n + 2)
                        if started(t, 1):
                            pool.wait_ge(a_low, 2 * t + n)
                        pool.tensor_tensor(rem[:, n, :], qf[:, n, :], parts[:, s, n, 0, :],
                                           ALU.subtract).then_inc(a_rem, 1)
                        pool.wait_ge(a_rem, 2 * t + n + 1)
                        pool.wait_ge(a_mid, 2 * t + n + 1)
                        pool.tensor_tensor(parts[:, s, n, 2, :], rem[:, n, :], parts[:, s, n, 1, :],
                                           ALU.subtract).then_inc(a_low, 1)
                norm(0, 0)
                sweep(pool, NT, body)

            @block.vector
            def _(dve):
                dve.wait_ge(a_wT, 2)
                dve.tensor_copy(wT[:], pW[:]).then_inc(a_wTs, 1)
                dve.tensor_copy(g0T[:], pG[:, 0, :]).then_inc(a_wTs, 1)
                dve.tensor_copy(g1T[:], pG[:, 1, :]).then_inc(a_wTs, 1)
                dve.wait_ge(a_w, 16 * WLOADS)

                def norm(t, s, loads):
                    dve.wait_ge(a_x[s], loads)
                    for j in range(SUB):
                        ins = dve.bn_stats(st[:, s, j, :], xt[:, s, j, :])
                    ins.then_inc(a_st, 1)
                    dve.wait_ge(a_rs, t + 1)
                    if started(t, 2):
                        dve.wait_ge(a_tr, t - 1)
                    for j in range(SUB):
                        ins = dve.tensor_scalar(xn[:, s, j, :], xt[:, s, j, :], mean[:, s, j:j + 1],
                                                rs[:, s, j:j + 1], ALU.subtract, ALU.mult)
                    ins.then_inc(a_xn, 1)

                def body(t, s):
                    if not is_last(t, NT):
                        norm(t + 1, 1 - s, (8 * (t + 1 - (1 - s)) + 16))
                    for n in range(2):
                        dve.wait_ge(a_qf, 4 * t + 2 * n + 2)
                        dve.tensor_tensor(parts[:, s, n, 1, :], qf[:, n, :], parts[:, s, n, 0, :],
                                          ALU.subtract).then_inc(a_mid, 1)
                    dve.wait_ge(a_v, t + 1)
                    dve.tensor_tensor(V[:, bass.ds(t * SUB, SUB), :], pV[:],
                                      bv_bc[:].unsqueeze(1).broadcast_to([P, SUB, D]), ALU.add)
                    dve.tensor_tensor(G0[:, bass.ds(t * SUB, SUB), :], pL[:],
                                      gb_bc[:].unsqueeze(1).broadcast_to([P, SUB, E]), ALU.add)\
                       .then_inc(a_vs, 1)
                norm(0, 0, 16)
                sweep(dve, NT, body)

            @block.tensor
            def _(pe):
                pe.wait_ge(a_w, 16 * WLOADS)
                pe.wait_ge(a_const, 8 + E)
                for n in range(4):
                    ins = nc.tensor.transpose(pW[:, n, :], wload[:, n, :], ident[:])
                ins.then_inc(a_wT, 1)
                for n in range(2):
                    ins = nc.tensor.transpose(pG[:, n, :], gload[:, n, :], ident[0:E, 0:E])
                ins.then_inc(a_wT, 1)
                pe.wait_ge(a_wTs, 3)

                def transpose(t, s):
                    pe.wait_ge(a_xn, t + 1)
                    if started(t, 1):
                        pe.wait_ge(a_xT, t)
                    for j in range(SUB):
                        ins = nc.tensor.transpose(pX[:, j * P:(j + 1) * P], xn[:, s, j, :], ident[:])
                    ins.then_inc(a_tr, 1)

                def body(t, s):
                    if not is_last(t, NT):
                        transpose(t + 1, 1 - s)
                    pe.wait_ge(a_xT, t + 1)
                    if started(t, 1):
                        pe.wait_ge(a_qf, 4 * t)
                    nc.tensor.matmul(pQ[:], wT[:, 0, :], xnT[:, s, :], start=True, stop=True).then_inc(a_q, 1)
                    nc.tensor.matmul(pK[:], wT[:, 1, :], xnT[:, s, :], start=True, stop=True).then_inc(a_q, 1)
                    if started(t, 1):
                        pe.wait_ge(a_vs, t)
                    for j in range(SUB):
                        nc.tensor.matmul(pV[:, j, :], xnT[:, s, j * P:(j + 1) * P], wT[:, 2, :],
                                         start=True, stop=True)
                        ins = nc.tensor.matmul(pL[:, j, :], xnT[:, s, j * P:(j + 1) * P], g0T[:],
                                               start=True, stop=True)
                    ins.then_inc(a_v, 1)
                transpose(0, 0)
                sweep(pe, NT, body)

            @block.scalar
            def _(act):
                def copy_x(t, s):
                    act.wait_ge(a_tr, t + 1)
                    if started(t, 2):
                        act.wait_ge(a_v, t - 1)
                        act.wait_ge(a_xTd[s], 8 * (t - s))
                    act.copy(xnT[:, s, :], pX[:]).then_inc(a_xT, 1)
                    act.wait_ge(a_xT, t + 1)
                    act.dma_start(xnT_d[:, bass.ds(t * TT, TT)], xnT[:, s, :]).then_inc(a_xTd[s], 16)

                act.wait_ge(a_w, 16 * WLOADS)

                def body(t, s):
                    if not is_last(t, NT):
                        copy_x(t + 1, 1 - s)
                    if started(t, 1):
                        act.wait_ge(a_low, 2 * t)
                        act.wait_ge(a_mid, 2 * t)
                    if started(t, 2):
                        act.wait_ge(a_pd[s], 16 * (t - s))
                    for n, (ps, bias) in enumerate(((pQ, bqc), (pK, bkc))):
                        act.wait_ge(a_q, 2 * t + n + 1)
                        act.activation(qf[:, n, :], ps[:], ACT.Identity, bias=bias[:]).then_inc(a_qf, 1)
                        act.activation(parts[:, s, n, 0, :], ps[:], ACT.Identity, bias=bias[:])\
                           .then_inc(a_qf, 1)
                    for n, dst in enumerate((qs_d, ks_d)):
                        act.wait_ge(a_low, 2 * t + n + 1)
                        act.wait_ge(a_mid, 2 * t + n + 1)
                        act.dma_start(dst[:, :, bass.ds(t * TT, TT)].rearrange("a d t -> d a t"),
                                      parts[:, s, n, :, :]).then_inc(a_pd[s], 16)
                copy_x(0, 0)
                sweep(act, NT, body)
                for s in range(2):
                    act.wait_ge(a_pd[s], 16 * NT)
                    act.wait_ge(a_xTd[s], 8 * NT)

        with ExitStack() as ph:
            qk = sb("qk", [KROWS, 2, 2, T], BF16, ph)
            Ex = sb("Ex", [P, 4, B, P], F32, ph)
            Vh = sb("Vh", [P, 2, NS, DK], F32, ph)
            mg = sb("mg", [P, P, NBG], F32, ph)
            negm = sb("negm", [P, P], F32, ph)
            mh = sb("mh", [P, 2, P], BF16, ph)
            ml = sb("ml", [P, 2, P], BF16, ph)
            Z = sb("Z", [P, P], F32, ph)
            R = sb("R", [P, 2, P], F32, ph)
            Oev = sb("Oev", [P, 2, NBG, P], F32, ph)
            pA = pb("pA", [P, 2, BG, P], ph)
            pB = pb("pB", [P, 2, 2, BG, P], ph)
            pO = pb("pO", [P, NBG, P], ph)

            b_qk = [sem("b_qk0"), sem("b_qk1")]
            b_z = sem("b_z")
            b_s1 = sem("b_s1")
            b_red = sem("b_red")
            b_nm = sem("b_nm")
            b_mh = sem("b_mh")
            b_m = sem("b_m")
            b_s2 = sem("b_s2")
            b_exp = sem("b_exp")
            b_sum = sem("b_sum")
            b_r = sem("b_r")
            b_norm = sem("b_norm")
            b_vh = sem("b_vh")
            b_pv = sem("b_pv")
            b_oev = sem("b_oev")
            b_od = [sem("b_od0"), sem("b_od1")]
            LOADS = 12 * 16
            oT_v = oT_d.rearrange("(n d) (g c h q) -> n d g c h q", d=DK, g=NBG, c=BG, h=2)

            block = ph.enter_context(nc.Block())

            @block.sync
            def _(sp):
                def load(h, s):
                    for i in range(NPART):
                        for j in range(NPART):
                            r = (NPART * i + j) * DK
                            sp.dma_start(qk[r:r + DK, s, 0, :], qs_d[i, bass.ds(h * DK, DK), :])\
                              .then_inc(b_qk[s], 16)
                    for i in range(NPART):
                        r = NPART * i * DK
                        sp.dma_start(qk[r:r + NPART * DK, s, 1, :],
                                     ks_d[:, bass.ds(h * DK, DK), :]).then_inc(b_qk[s], 16)

                def store(h, w, qh):
                    sp.wait_ge(b_oev, w + 1)
                    for c in range(BG):
                        sp.dma_start(oT_v[bass.ds(h, 1), :, :, c, qh, :].squeeze(0),
                                     Oev[32 * c:32 * c + DK, qh, :, :]).then_inc(b_od[qh], 16)

                def body(h, s):
                    if started(h, 1):
                        sp.wait_ge(b_s2, 16 * h)
                    if not is_last(h, H):
                        load(h + 1, 1 - s)
                    if started(h, 1):
                        store(h - 1, 2 * h - 1, 1)
                    store(h, 2 * h, 0)
                load(0, 0)
                sweep(sp, H, body)
                store(H - 1, 2 * H - 1, 1)
                for qh in range(2):
                    sp.wait_ge(b_od[qh], 16 * BG * H)

            @block.tensor
            def _(pe):
                def s1_group(n, head_slot, qh, kc, g):
                    if not isinstance(n, int) or n >= 2:
                        pe.wait_ge(b_red, n - 1)
                    for c in range(BG):
                        tok = (BG * g + c) * S
                        ins = nc.tensor.matmul(pA[:, g % 2, c, :],
                                               qk[:, head_slot, 1, tok + kc * P:tok + kc * P + P],
                                               qk[:, head_slot, 0, tok + qh * P:tok + qh * P + P],
                                               start=True, stop=True)
                    ins.then_inc(b_s1, 1)

                def s2_group(n, u, s, j, g):
                    qh, kc = j // 2, j % 2
                    if not isinstance(n, int) or n >= 2:
                        pe.wait_ge(b_exp, n - 1)
                    for k in range(2):
                        for i, m in enumerate((mh, ml)):
                            nc.tensor.matmul(pB[:, g % 2, k, :, :], identb[:],
                                             m[:, j % 2, :].unsqueeze(1).broadcast_to([P, BG, P]),
                                             start=(i == 0), stop=False, skip_group_check=True)
                        for c in range(BG):
                            tok = (2 * BG * g + BG * k + c) * S
                            ins = nc.tensor.matmul(pB[:, g % 2, k, c, :],
                                                   qk[:, s, 1, tok + kc * P:tok + kc * P + P],
                                                   qk[:, s, 0, tok + qh * P:tok + qh * P + P],
                                                   start=False, stop=(c == BG - 1), skip_group_check=True)
                    ins.then_inc(b_s2, 1)

                def pv_group(v, s, j, g):
                    kc = j % 2
                    for k in range(2):
                        for c in range(BG):
                            b = 2 * BG * g + BG * k + c
                            ins = nc.tensor.matmul(pO[32 * c:32 * c + DK, b // BG, :],
                                                   Vh[:, s, 2 * b + kc, :], Ex[:, j, b, :],
                                                   start=(kc == 0 and (b // BG) % 4 == 0), stop=(kc == 1),
                                                   skip_group_check=True)
                    if g == 3:
                        ins.then_inc(b_pv, 1)

                def pv_waits(v, h, j):
                    pe.wait_ge(b_norm, v + 1)
                    if j == 0:
                        pe.wait_ge(b_vh, h + 1)
                    if j % 2 == 0:
                        if not isinstance(h, int) or 2 * h + j // 2 > 0:
                            pe.wait_ge(b_oev, 2 * h + j // 2)

                def body(h, s):
                    for j in range(4):
                        u = 4 * h + j
                        first_pv = started(h, 1) or j >= 2
                        lag_j, lag_s = (j - 2, s) if j >= 2 else (j + 2, 1 - s)
                        for g in range(NBG):
                            if j < 3:
                                s1_group(8 * (u + 1) + g, s, (j + 1) // 2, (j + 1) % 2, g)
                            elif not is_last(h, H):
                                if g == 0:
                                    pe.wait_ge(b_qk[1 - s], (h + 1 - (1 - s)) * (LOADS // 2) + LOADS)
                                s1_group(8 * (u + 1) + g, 1 - s, 0, 0, g)
                            if g % 2 == 1:
                                if g == 1:
                                    pe.wait_ge(b_m, u + 1)
                                s2_group(4 * u + g // 2, u, s, j, g // 2)
                                if first_pv:
                                    if g == 1:
                                        pv_waits(u - 2, h if j >= 2 else h - 1, lag_j)
                                    pv_group(u - 2, lag_s, lag_j, g // 2)

                pe.wait_ge(b_z, 1)
                pe.wait_ge(b_qk[0], LOADS)
                for g in range(NBG):
                    s1_group(g, 0, 0, 0, g)
                sweep(pe, H, body)
                for j in (2, 3):
                    pv_waits(4 * (H - 1) + j, H - 1, j)
                    for g in range(4):
                        pv_group(4 * (H - 1) + j, 1, j, g)

            @block.vector
            def _(dve):
                def maxima(u, m):
                    for g in range(NBG):
                        dve.wait_ge(b_s1, 8 * u + g + 1)
                        dve.tensor_reduce(mg[:, :, g], pA[:, g % 2, :, :].rearrange("p b q -> p q b"),
                                          AX.X, ALU.max).then_inc(b_red, 1)
                    dve.wait_ge(b_red, 8 * u + 8)
                    if not isinstance(u, int) or u >= 1:
                        dve.wait_ge(b_m, u)
                    dve.tensor_reduce(negm[:], mg[:], AX.X, ALU.max, negate=True).then_inc(b_nm, 1)
                    dve.wait_ge(b_nm, u + 1)
                    if not isinstance(u, int) or u >= 2:
                        dve.wait_ge(b_s2, 4 * (u - 1))
                    dve.tensor_copy(mh[:, m, :], negm[:]).then_inc(b_mh, 1)
                    dve.wait_ge(b_mh, u + 1)
                    dve.tensor_tensor(ml[:, m, :], negm[:], mh[:, m, :], ALU.subtract).then_inc(b_m, 1)

                def sums(u, j):
                    if not isinstance(u, int) or u >= 1:
                        dve.wait_ge(b_r, u)
                    dve.wait_ge(b_exp, 4 * u + 4)
                    dve.tensor_reduce(Z[:], Ex[:, j, :, :].rearrange("p b q -> p q b"), AX.X, ALU.add)\
                       .then_inc(b_sum, 1)
                    dve.wait_ge(b_sum, u + 1)
                    if not isinstance(u, int) or u >= 2:
                        dve.wait_ge(b_norm, u - 1)
                    dve.reciprocal(R[:, j % 2, :], Z[:]).then_inc(b_r, 1)

                def body(h, s):
                    for j in range(4):
                        u = 4 * h + j
                        if not (is_last(h, H) and j == 3):
                            maxima(u + 1, (j + 1) % 2)
                        sums(u, j)

                dve.memset(pO[:], 0.0).then_inc(b_z, 1)
                maxima(0, 0)
                sweep(dve, H, body)

            @block.scalar
            def _(act):
                def evac(h, qh):
                    w = 2 * h + qh
                    act.wait_ge(b_pv, 2 * w + 2)
                    if started(h, 1):
                        act.wait_ge(b_od[qh], 16 * BG * h)
                    act.copy(Oev[:, qh, :, :], pO[:]).then_inc(b_oev, 1)

                def body(h, s):
                    if started(h, 2):
                        act.wait_ge(b_pv, 4 * (h - 1))
                    act.copy(Vh[:, s, :, :], V[:, :, bass.ds(h * DK, DK)]).then_inc(b_vh, 1)
                    for j in range(4):
                        u = 4 * h + j
                        if started(h, 1):
                            act.wait_ge(b_pv, u - 3)
                        for g in range(4):
                            act.wait_ge(b_s2, 4 * u + g + 1)
                            act.activation(Ex[:, j, 2 * BG * g:2 * BG * (g + 1), :],
                                           pB[:, g % 2, :, :, :].rearrange("p k b q -> p (k b) q"),
                                           ACT.Exp).then_inc(b_exp, 1)
                        if j == 1 and started(h, 1):
                            evac(h - 1, 1)
                        if j == 3:
                            evac(h, 0)
                sweep(act, H, body)
                evac(H - 1, 1)

            @block.gpsimd
            def _(pool):
                def body(h, s):
                    for j in range(4):
                        u = 4 * h + j
                        pool.wait_ge(b_r, u + 1)
                        pool.tensor_tensor(Ex[:, j, :, :], Ex[:, j, :, :],
                                           R[:, j % 2, :].unsqueeze(1).broadcast_to([P, B, P]),
                                           ALU.mult).then_inc(b_norm, 1)
                sweep(pool, H, body)

        w1T = sb("w1T", [P, 2 * E + 1, HID])
        w2T = sb("w2T", [P, 2 * E + 1, HC, D])
        b1T = sb("b1T", [P, E, HC])
        b2x = sb("b2x", [E + 1, D])
        wqkv = sb("wqkv", [P, 3 * D])
        bqk1 = sb("bqk1", [P, 2])
        bv1 = sb("bv1", [P, D])
        lnw = sb("lnw", [P, D])
        lnb = sb("lnb", [P, D])
        mdiag = sb("mdiag", [P, P])
        mcross = sb("mcross", [P, P])

        with ExitStack() as ph:
            w1l = sb("w1l", [P, 2, HC, D], F32, ph)
            w2l = sb("w2l", [P, 2, HID], F32, ph)
            mx = sb("mx", [P, NS], F32, ph)
            cand = sb("cand", [P, NS, E], F32, ph)
            b1l = sb("b1l", [E * HC, P], F32, ph)
            pb1 = pb("pb1", [P, E * HC], ph)
            c_b1 = sem("c_b1")
            p1 = pb("p1", [P, 2, HID], ph)
            p2 = pb("p2", [P, 2, HC, D], ph)
            c_w = [sem("c_w0"), sem("c_w1")]
            c_s = sem("c_s")
            c_tr = sem("c_tr")
            c_ev1 = sem("c_ev1")
            c_ev2 = sem("c_ev2")
            c_g = sem("c_g")
            c_m = sem("c_m")
            NW = 2 * E + 1
            SMALL = 9

            block = ph.enter_context(nc.Block())

            def groups(eng, one):
                sweep(eng, E, lambda e, s: one(e, s, w1_0, w2_0, e))
                sweep(eng, E, lambda e, s: one(E + e, s, w1_1, w2_1, e))
                one(2 * E, 0, None, None, 0)

            @block.sync
            def _(sp):
                sp.dma_start(b1l[:], b1_0.rearrange("e (c p) -> (e c) p", p=P)).then_inc(c_s, 16)
                sp.dma_start(b2x[0:E, :], b2_0).then_inc(c_s, 16)
                sp.dma_start(b2x[E:E + 1, :], bo.rearrange("(a n) -> a n", a=1)).then_inc(c_s, 16)
                sp.dma_start(wqkv[:], W_qkv).then_inc(c_s, 16)
                sp.dma_start(bqk1[:, 0:1], b_qkv[0:D].rearrange("(p a) -> p a", a=1)).then_inc(c_s, 16)
                sp.dma_start(bqk1[:, 1:2], b_qkv[D:2 * D].rearrange("(p a) -> p a", a=1)).then_inc(c_s, 16)
                sp.dma_start(bv1[:], b_qkv[2 * D:3 * D].partition_broadcast(P)).then_inc(c_s, 16)
                sp.dma_start(lnw[:], ln_w.partition_broadcast(P)).then_inc(c_s, 16)
                sp.dma_start(lnb[:], ln_b.partition_broadcast(P)).then_inc(c_s, 16)

                def one(k, s, w1, w2, e):
                    if started(k, 2):
                        sp.wait_ge(c_tr, k - 1)
                    a = sh_w1 if w1 is None else w1[e, :, :]
                    b = sh_w2 if w2 is None else w2[e, :, :]
                    sp.dma_start(w1l[:, s, :, :], a.rearrange("(c p) d -> p c d", p=P)).then_inc(c_w[s], 16)
                    sp.dma_start(w2l[:, s, :], b).then_inc(c_w[s], 16)
                groups(sp, one)
                sp.wait_ge(c_s, 16 * SMALL)

            @block.tensor
            def _(pe):
                def one(k, s, w1, w2, e):
                    pe.wait_ge(c_w[s], 16 * (k - s) + 32)
                    if started(k, 2):
                        pe.wait_ge(c_ev1, k - 1)
                        pe.wait_ge(c_ev2, k - 1)
                    for c in range(HC):
                        nc.tensor.transpose(p1[:, s, c * P:(c + 1) * P], w1l[:, s, c, :], ident[:])
                        ins = nc.tensor.transpose(p2[:, s, c, :], w2l[:, s, c * P:(c + 1) * P], ident[:])
                    ins.then_inc(c_tr, 1)
                pe.wait_ge(c_s, 16 * SMALL)
                nc.tensor.transpose(pb1[:], b1l[:], ident[0:E * HC, 0:E * HC]).then_inc(c_b1, 1)
                groups(pe, one)

            @block.scalar
            def _(act):
                def one(k, s, w1, w2, e):
                    act.wait_ge(c_tr, k + 1)
                    act.copy(w1T[:, bass.ds(k, 1), :], p1[:, s, :].unsqueeze(1)).then_inc(c_ev1, 1)
                act.wait_ge(c_b1, 1)
                act.copy(b1T[:].rearrange("p e c -> p (e c)"), pb1[:])
                groups(act, one)

            @block.vector
            def _(dve):
                def one(k, s, w1, w2, e):
                    dve.wait_ge(c_tr, k + 1)
                    dve.tensor_copy(w2T[:, bass.ds(k, 1), :, :], p2[:, s, :, :].unsqueeze(1)).then_inc(c_ev2, 1)
                groups(dve, one)
                link = chain(dve, c_g, 0)
                link(dve.tensor_reduce(mx[:], G0[:], AX.X, ALU.max))
                link(dve.tensor_tensor(cand[:], G0[:], mx[:].unsqueeze(2).broadcast_to([P, NS, E]), ALU.is_equal))
                link(dve.tensor_tensor(cand[:], cand[:], prio[:].unsqueeze(1).broadcast_to([P, NS, E]), ALU.mult))
                link(dve.tensor_reduce(mx[:], cand[:], AX.X, ALU.max))
                link(dve.tensor_tensor(G0[:], cand[:], mx[:].unsqueeze(2).broadcast_to([P, NS, E]), ALU.is_equal))

            @block.gpsimd
            def _(pool):
                link = chain(pool, c_m, 0)
                link(pool.memset(mdiag[:], 1.0))
                link(pool.memset(mcross[:], 1.0))
                link(pool.affine_select(out=mdiag[:], in_=mdiag[:], compare_op=ALU.is_ge, fill=0.0, base=0,
                                        pattern=[[1, P]], channel_multiplier=-1))
                link(pool.affine_select(out=mdiag[:], in_=mdiag[:], compare_op=ALU.is_ge, fill=0.0,
                                        base=SPAN - 1, pattern=[[-1, P]], channel_multiplier=1))
                link(pool.affine_select(out=mcross[:], in_=mcross[:], compare_op=ALU.is_ge, fill=0.0,
                                        base=SPAN - 1 - P, pattern=[[-1, P]], channel_multiplier=1))

        with ExitStack() as ph:
            xnT = sb("d_xnT", [P, 2, TT], F32, ph)
            oT = sb("d_oT", [P, 2, TT], F32, ph)
            acc = sb("d_acc", [P, 2, SUB, D], F32, ph)
            gt = sb("d_gt", [P, 2, SUB, E], F32, ph)
            gT = sb("d_gT", [E + 1, 2, TT], F32, ph)
            hT = sb("d_hT", [P, 2, HC, TT], F32, ph)
            st = sb("d_st", [P, SUB, 6], F32, ph)
            mean = sb("d_mean", [P, SUB], F32, ph)
            tmp = sb("d_tmp", [P, SUB], F32, ph)
            rs = sb("d_rs", [P, SUB], F32, ph)
            xn = sb("d_xn", [P, SUB, D], F32, ph)
            xn1T = sb("d_xn1T", [P, TT], F32, ph)
            pH = pb("d_pH", [P, HC, TT], ph)
            pY = pb("d_pY", [P, 2, SUB, D], ph)
            pC = pb("d_pC", [P, SUB, D], ph)
            pL = pb("d_pL", [P, SUB, E], ph)

            d_x = [sem("d_x0"), sem("d_x1")]
            d_ones = sem("d_ones")
            d_gt = sem("d_gt")
            d_gTp = sem("d_gTp")
            d_gT = sem("d_gT")
            d_c = sem("d_c")
            d_up = sem("d_up")
            d_h = sem("d_h")
            d_y = sem("d_y")
            d_acc = sem("d_acc")
            d_ln = sem("d_ln")
            d_ve = sem("d_ve")
            d_rs = sem("d_rs")
            d_xn = sem("d_xn")
            d_tr = sem("d_tr")
            d_xT = sem("d_xT")
            d_lg = sem("d_lg")
            d_lgs = sem("d_lgs")
            d_x1d = [sem("d_x1d0"), sem("d_x1d1")]
            d_xTd = sem("d_xTd")
            TPT = 1 + E

            block = ph.enter_context(nc.Block())

            @block.sync
            def _(sp):
                def body(t, s):
                    if started(t, 2):
                        sp.wait_ge(d_x1d[s], 8 * (t - s))
                        sp.wait_ge(d_y, E * (t - 1))
                        sp.wait_ge(d_xn, t - 1)
                    sp.dma_start(xnT[:, s, :], xnT_d[:, bass.ds(t * TT, TT)]).then_inc(d_x[s], 16)
                    sp.dma_start(oT[:, s, :], oT_d[:, bass.ds(t * TT, TT)]).then_inc(d_x[s], 16)
                    sp.dma_start(acc[:, s, :, :], x_v[:, bass.ds(t * SUB, SUB), :]).then_inc(d_x[s], 16)
                sweep(sp, NT, body)

            @block.tensor
            def _(pe):
                def up(t, s, e):
                    if e == 0:
                        pe.wait_ge(d_x[s], 24 * (t - s) + 48)
                    for c in range(HC):
                        if started(t, 1) or e > 0:
                            pe.wait_ge(d_h, HC * (E * t + e - 1) + c + 1)
                        nc.tensor.matmul(pH[:, c, :], w1T[:, e, c * P:(c + 1) * P], xnT[:, s, :],
                                         start=True, stop=True).then_inc(d_up, 1)

                def down(t, s, e):
                    n = E * t + e
                    pe.wait_ge(d_h, HC * (n + 1))
                    if started(t, 1) or e >= 2:
                        pe.wait_ge(d_acc, TPT * t + e - (0 if e >= 2 else 1))
                    for j in range(SUB):
                        for c in range(HC):
                            ins = nc.tensor.matmul(pY[:, e % 2, j, :], hT[:, e % 2, c, j * P:(j + 1) * P],
                                                   w2T[:, e, c, :], start=(c == 0), stop=(c == HC - 1))
                    ins.then_inc(d_y, 1)

                def choice(t, s):
                    pe.wait_ge(d_gt, t + 1)
                    if started(t, 1):
                        pe.wait_ge(d_xT, t)
                    for j in range(SUB):
                        ins = nc.tensor.transpose(pC[0:E, j, :], gt[:, s, j, :], ident[:])
                    ins.then_inc(d_gTp, 1)

                def project(t, s):
                    pe.wait_ge(d_gT, t + 1)
                    for j in range(SUB):
                        nc.tensor.matmul(pC[:, j, :], oT[:, s, j * P:(j + 1) * P], wT[:, 3, :],
                                         start=True, stop=False)
                        ins = nc.tensor.matmul(pC[:, j, :], gT[:, s, j * P:(j + 1) * P], b2x[:],
                                               start=False, stop=True)
                    ins.then_inc(d_c, 1)

                def next_norm(t, s):
                    pe.wait_ge(d_xn, t + 1)
                    for j in range(SUB):
                        ins = nc.tensor.transpose(pC[:, j, :], xn[:, j, :], ident[:])
                    ins.then_inc(d_tr, 1)

                def next_logits(t):
                    pe.wait_ge(d_xT, t + 1)
                    if started(t, 1):
                        pe.wait_ge(d_lgs, t)
                    for j in range(SUB):
                        ins = nc.tensor.matmul(pL[:, j, :], xn1T[:, j * P:(j + 1) * P], g1T[:],
                                               start=True, stop=True)
                    ins.then_inc(d_lg, 1)

                def body(t, s):
                    for e in range(E):
                        if e < E - 1:
                            up(t, s, e + 1)
                        elif not is_last(t, NT):
                            up(t + 1, 1 - s, 0)
                        if started(t, 1) and e == 1:
                            next_norm(t - 1, 1 - s)
                        if started(t, 1) and e == 2:
                            next_logits(t - 1)
                        if e == 3:
                            choice(t, s)
                        if e == 4:
                            project(t, s)
                        down(t, s, e)
                pe.wait_ge(d_ones, 1)
                up(0, 0, 0)
                sweep(pe, NT, body)
                next_norm(NT - 1, 1)
                next_logits(NT - 1)

            @block.scalar
            def _(act):
                def body(t, s):
                    for e in range(E):
                        n = E * t + e
                        if started(t, 1) or e >= 2:
                            act.wait_ge(d_y, n - 1)
                        for c in range(HC):
                            act.wait_ge(d_up, HC * n + c + 1)
                            act.activation(hT[:, e % 2, c, :], pH[:, c, :], ACT.Relu,
                                           bias=b1T[:, e, c:c + 1]).then_inc(d_h, 1)
                        if e == 1 and started(t, 1):
                            copy_xn(t - 1)
                        if e == 3:
                            act.wait_ge(d_gTp, t + 1)
                            act.copy(gT[0:E, s, :], pC[0:E, :, :].rearrange("p j n -> p (j n)"))\
                               .then_inc(d_gT, 1)

                def copy_xn(t):
                    act.wait_ge(d_tr, t + 1)
                    if started(t, 1):
                        act.wait_ge(d_xTd, 16 * t)
                        act.wait_ge(d_lg, t)
                    act.copy(xn1T[:], pC[:].rearrange("p j n -> p (j n)")).then_inc(d_xT, 1)
                    act.wait_ge(d_xT, t + 1)
                    act.dma_start(xn1T_d[:, bass.ds(t * TT, TT)], xn1T[:]).then_inc(d_xTd, 16)
                act.wait_ge(d_ones, 1)
                sweep(act, NT, body)
                copy_xn(NT - 1)
                act.wait_ge(d_xTd, 16 * NT)

            @block.vector
            def _(dve):
                def stats(t, s):
                    dve.wait_ge(d_acc, TPT * (t + 1))
                    for j in range(SUB):
                        ins = dve.bn_stats(st[:, j, :], acc[:, s, j, :])
                    ins.then_inc(d_ln, 1)

                def norm(t, s):
                    dve.wait_ge(d_rs, t + 1)
                    if started(t, 1):
                        dve.wait_ge(d_tr, t)
                    for j in range(SUB):
                        ins = dve.tensor_scalar(xn[:, j, :], acc[:, s, j, :], mean[:, j:j + 1], rs[:, j:j + 1],
                                                ALU.subtract, ALU.mult)
                    ins.then_inc(d_xn, 1)

                def logits(t):
                    dve.wait_ge(d_lg, t + 1)
                    dve.tensor_copy(G1[:, bass.ds(t * SUB, SUB), :], pL[:]).then_inc(d_lgs, 1)

                def body(t, s):
                    if started(t, 2):
                        dve.wait_ge(d_y, E * (t - 1))
                    dve.tensor_copy(gt[:, s, :, :], G0[:, bass.ds(t * SUB, SUB), :]).then_inc(d_gt, 1)
                    dve.wait_ge(d_gt, t + 1)
                    dve.wait_ge(d_x[s], 24 * (t - s) + 48)
                    k = 0
                    for e in range(E):
                        if started(t, 1) and e == 0:
                            norm(t - 1, 1 - s)
                        dve.wait_ge(d_y, E * t + e + 1)
                        if k:
                            dve.wait_ge(d_acc, TPT * t + k)
                        for j in range(SUB):
                            ins = dve.scalar_tensor_tensor(acc[:, s, j, :], pY[:, e % 2, j, :],
                                                           gt[:, s, j, e:e + 1], acc[:, s, j, :],
                                                           ALU.mult, ALU.add)
                        ins.then_inc(d_acc, 1)
                        k += 1
                        if started(t, 1) and e == 2:
                            logits(t - 1)
                        if e == E - 1:
                            dve.wait_ge(d_c, t + 1)
                            dve.wait_ge(d_acc, TPT * t + k)
                            dve.tensor_tensor(acc[:, s, :, :], pC[:], acc[:, s, :, :], ALU.add)\
                               .then_inc(d_acc, 1)
                    stats(t, s)

                dve.memset(gT[:], 1.0).then_inc(d_ones, 1)
                sweep(dve, NT, body)
                norm(NT - 1, 1)
                logits(NT - 1)

            @block.gpsimd
            def _(pool):
                def body(t, s):
                    pool.wait_ge(d_acc, TPT * (t + 1))
                    pool.dma_start(x1_d[:, bass.ds(t * SUB, SUB), :], acc[:, s, :, :]).then_inc(d_x1d[s], 16)
                    pool.wait_ge(d_ln, t + 1)
                    norm_factors(pool, chain(pool, d_ve, NORM_LINKS * t), st[:], mean[:], rs[:], tmp[:],
                                 *(c[:] for c in norm_c)).then_inc(d_rs, 1)
                sweep(pool, NT, body)
                for s in range(2):
                    pool.wait_ge(d_x1d[s], 8 * NT)

        with ExitStack() as ph:
            m1 = sb("g_m1", [P, NS], F32, ph)
            m2 = sb("g_m2", [P, NS], F32, ph)
            c1 = sb("g_c1", [P, NS], F32, ph)
            oh1 = sb("g_oh1", [P, NS, E], F32, ph)
            oh2 = sb("g_oh2", [P, NS, E], F32, ph)
            lg2 = sb("g_lg2", [P, NS, E], F32, ph)
            g_c = sem("g_c")
            g_d = sem("g_d")
            g_e = sem("g_e")
            block = ph.enter_context(nc.Block())

            @block.vector
            def _(dve):
                link = chain(dve, g_c, 0)

                def bc(a):
                    return a[:].unsqueeze(2).broadcast_to([P, NS, E])
                pr = prio[:].unsqueeze(1).broadcast_to([P, NS, E])
                for m, oh, lg in ((m1, oh1, G1), (m2, oh2, lg2)):
                    link(dve.tensor_reduce(m[:], lg[:], AX.X, ALU.max))
                    link(dve.tensor_tensor(oh[:], lg[:], bc(m), ALU.is_equal))
                    link(dve.tensor_tensor(oh[:], oh[:], pr, ALU.mult))
                    link(dve.tensor_reduce(c1[:], oh[:], AX.X, ALU.max))
                    link(dve.tensor_tensor(oh[:], oh[:], bc(c1), ALU.is_equal))
                    if m is m1:
                        link(dve.tensor_scalar(lg2[:], oh1[:], PRIO_NONE, None, ALU.mult))
                        link(dve.tensor_tensor(lg2[:], lg2[:], G1[:], ALU.add))
                dve.tensor_tensor(m2[:], m2[:], m1[:], ALU.subtract).then_inc(g_d, 1)
                dve.wait_ge(g_e, 1)
                link(dve.tensor_scalar(c1[:], m2[:], 1.0, None, ALU.add))
                link(dve.reciprocal(m1[:], c1[:]))
                link(dve.tensor_tensor(m2[:], m2[:], m1[:], ALU.mult))
                link(dve.tensor_tensor(oh1[:], oh1[:], bc(m1), ALU.mult))
                link(dve.tensor_tensor(oh2[:], oh2[:], bc(m2), ALU.mult))
                link(dve.tensor_tensor(G1[:], oh1[:], oh2[:], ALU.add))

            @block.scalar
            def _(act):
                act.wait_ge(g_d, 1)
                act.activation(m2[:], m2[:], ACT.Exp).then_inc(g_e, 1)

        with ExitStack() as ph:
            xnT = sb("f_xnT", [P, 2, TT], F32, ph)
            acc = sb("f_acc", [P, 2, SUB, D], F32, ph)
            qkT = sb("f_qkT", [P, 2, TT], F32, ph)
            v = sb("f_v", [P, SUB, D], F32, ph)
            sm = sb("f_sm", [P, 2, 3, P], F32, ph)
            o = sb("f_o", [P, SUB, D], F32, ph)
            hT = sb("f_hT", [P, 2, HC, TT], F32, ph)
            st = sb("f_st", [P, SUB, 6], F32, ph)
            mean = sb("f_mean", [P, SUB], F32, ph)
            tmp = sb("f_tmp", [P, SUB], F32, ph)
            rs = sb("f_rs", [P, SUB], F32, ph)
            pH = pb("f_pH", [P, HC, TT], ph)
            pY = pb("f_pY", [P, 2, SUB, D], ph)
            pM = pb("f_pM", [P, 2, TT], ph)
            NE = E + 1

            f_x = [sem("f_x0"), sem("f_x1")]
            f_up = sem("f_up")
            f_h = sem("f_h")
            f_y = sem("f_y")
            f_acc = sem("f_acc")
            f_qk = sem("f_qk")
            f_qks = sem("f_qks")
            f_v = sem("f_v")
            f_vs = sem("f_vs")
            f_s = sem("f_s")
            f_sm = sem("f_sm")
            f_o = sem("f_o")
            f_os = sem("f_os")
            f_ln = sem("f_ln")
            f_ve = sem("f_ve")
            f_rs = sem("f_rs")
            f_out = [sem("f_out0"), sem("f_out1")]
            TPT = NE + 1
            weight = [2 * E] + list(range(E, 2 * E))

            block = ph.enter_context(nc.Block())

            @block.sync
            def _(sp):
                def body(t, s):
                    if started(t, 2):
                        sp.wait_ge(f_out[s], 8 * (t - s))
                        sp.wait_ge(f_y, NE * t - NE)
                    sp.dma_start(xnT[:, s, :], xn1T_d[:, bass.ds(t * TT, TT)]).then_inc(f_x[s], 16)
                    sp.dma_start(acc[:, s, :, :], x1_d[:, bass.ds(t * SUB, SUB), :]).then_inc(f_x[s], 16)
                sweep(sp, NT, body)

            @block.tensor
            def _(pe):
                def up(t, s, e):
                    k = (s + e) % 2
                    if e == 0:
                        pe.wait_ge(f_x[s], 16 * (t - s) + 32)
                    for c in range(HC):
                        if started(t, 1) or e > 0:
                            pe.wait_ge(f_h, HC * (NE * t + e - 1) + c + 1)
                        nc.tensor.matmul(pH[:, c, :], w1T[:, weight[e], c * P:(c + 1) * P], xnT[:, s, :],
                                         start=True, stop=True).then_inc(f_up, 1)

                def down(t, s, e):
                    k = (s + e) % 2
                    pe.wait_ge(f_h, HC * (NE * t + e + 1))
                    if started(t, 1) or e >= 2:
                        pe.wait_ge(f_acc, TPT * t + e - (1 if e >= 2 else 2))
                    for j in range(SUB):
                        for c in range(HC):
                            ins = nc.tensor.matmul(pY[:, k, j, :], hT[:, k, c, j * P:(j + 1) * P],
                                                   w2T[:, weight[e], c, :], start=(c == 0), stop=(c == HC - 1))
                    ins.then_inc(f_y, 1)

                def project_qk(t, s):
                    if started(t, 1):
                        pe.wait_ge(f_os, t)
                    for n in range(2):
                        nc.tensor.matmul(pM[:, n, :], wqkv[:, n * D:(n + 1) * D], xnT[:, s, :],
                                         start=True, stop=True).then_inc(f_qk, 1)

                def project_v(t, s):
                    pe.wait_ge(f_qks, 2 * t + 1)
                    for j in range(SUB):
                        ins = nc.tensor.matmul(pM[:, 0, j * P:(j + 1) * P], xnT[:, s, j * P:(j + 1) * P],
                                               wqkv[:, 2 * D:3 * D], start=True, stop=True)
                    ins.then_inc(f_v, 1)

                def scores(t, b):
                    pe.wait_ge(f_qks, 2 * t + 2)
                    if b == 0:
                        pe.wait_ge(f_vs, t + 1)
                    for n, (key, query) in enumerate(((0, 0), (1, 1), (0, 1))):
                        ins = nc.tensor.matmul(pM[:, b, n * P:(n + 1) * P],
                                               qkT[:, 1, (2 * b + key) * P:(2 * b + key + 1) * P],
                                               qkT[:, 0, (2 * b + query) * P:(2 * b + query + 1) * P],
                                               start=True, stop=True)
                    ins.then_inc(f_s, 1)

                def attend(t):
                    pe.wait_ge(f_sm, 4 * t + 4)
                    for b in range(2):
                        nc.tensor.matmul(pM[:, 0, 2 * b * P:(2 * b + 1) * P], sm[:, b, 0, :],
                                         v[:, 2 * b, :], start=True, stop=True)
                        nc.tensor.matmul(pM[:, 0, (2 * b + 1) * P:(2 * b + 2) * P], sm[:, b, 1, :],
                                         v[:, 2 * b + 1, :], start=True, stop=False)
                        ins = nc.tensor.matmul(pM[:, 0, (2 * b + 1) * P:(2 * b + 2) * P], sm[:, b, 2, :],
                                               v[:, 2 * b, :], start=False, stop=True)
                    ins.then_inc(f_o, 1)

                def body(t, s):
                    for e in range(NE):
                        if e < NE - 1:
                            up(t, s, e + 1)
                        elif not is_last(t, NT):
                            up(t + 1, 1 - s, 0)
                        if e == 1:
                            project_qk(t, s)
                        if e == 2:
                            project_v(t, s)
                        if e == 3:
                            scores(t, 0)
                            scores(t, 1)
                        if e == 5:
                            attend(t)
                        down(t, s, e)
                up(0, 0, 0)
                sweep(pe, NT, body)

            @block.scalar
            def _(act):
                def body(t, s):
                    for e in range(NE):
                        n = NE * t + e
                        k = (s + e) % 2
                        if started(t, 1) or e >= 2:
                            act.wait_ge(f_y, n - 1)
                        for c in range(HC):
                            act.wait_ge(f_up, HC * n + c + 1)
                            act.activation(hT[:, k, c, :], pH[:, c, :], ACT.Silu).then_inc(f_h, 1)
                        if e == 1:
                            if started(t, 1):
                                act.wait_ge(f_s, 2 * t)
                            for i in range(2):
                                act.wait_ge(f_qk, 2 * t + i + 1)
                                act.activation(qkT[:, i, :], pM[:, i, :], ACT.Identity,
                                               bias=bqk1[:, i:i + 1]).then_inc(f_qks, 1)
                sweep(act, NT, body)

            @block.vector
            def _(dve):
                def add_expert(t, s, e):
                    k = (s + e) % 2
                    dve.wait_ge(f_y, NE * t + e + 1)
                    if e:
                        dve.wait_ge(f_acc, TPT * t + e)
                        for j in range(SUB):
                            ins = dve.scalar_tensor_tensor(
                                acc[:, s, j, :], pY[:, k, j, :], gt[:, j, e - 1:e], acc[:, s, j, :],
                                ALU.mult, ALU.add)
                    else:
                        ins = dve.tensor_tensor(acc[:, s, :, :], pY[:, k, :, :], acc[:, s, :, :], ALU.add)
                    ins.then_inc(f_acc, 1)

                def body(t, s):
                    dve.wait_ge(f_x[s], 16 * (t - s) + 32)
                    dve.tensor_copy(gt[:], G1[:, bass.ds(t * SUB, SUB), :]).then_inc(f_gt, 1)
                    dve.wait_ge(f_gt, t + 1)
                    link = chain(dve, f_ln, t * LINKS)
                    for e in range(NE):
                        add_expert(t, s, e)
                        if e == 1:
                            dve.wait_ge(f_v, t + 1)
                            if started(t, 1):
                                dve.wait_ge(f_o, t)
                            dve.tensor_tensor(v[:], pM[:, 0, :].rearrange("p (j d) -> p j d", d=D),
                                              bv1[:].unsqueeze(1).broadcast_to([P, SUB, D]),
                                              ALU.add).then_inc(f_vs, 1)
                        if e == 3:
                            for b in range(2):
                                dve.wait_ge(f_s, 2 * t + b + 1)
                                sc = pM[:, b, :].rearrange("p (n q) -> p n q", q=P)
                                dve.scalar_tensor_tensor(
                                    sm[:, b, 0:2, :], sc[:, 0:2, :], SCALE1,
                                    mdiag[:].unsqueeze(1).broadcast_to([P, 2, P]),
                                    ALU.mult, ALU.mult).then_inc(f_sm, 1)
                                dve.scalar_tensor_tensor(sm[:, b, 2, :], sc[:, 2, :], SCALE1, mcross[:],
                                                         ALU.mult, ALU.mult).then_inc(f_sm, 1)
                        if e == 5:
                            dve.wait_ge(f_o, t + 1)
                            link(dve.tensor_copy(o[:], pM[:, 0, :].rearrange("p (j d) -> p j d", d=D)))
                            for j in range(SUB):
                                ins = dve.bn_stats(st[:, j, :], o[:, j, :])
                            ins.then_inc(f_os, 1)
                        if e == 7:
                            dve.wait_ge(f_rs, t + 1)
                            for j in range(SUB):
                                ins = dve.tensor_scalar(o[:, j, :], o[:, j, :], mean[:, j:j + 1], rs[:, j:j + 1],
                                                        ALU.subtract, ALU.mult)
                            link(ins)
                            link(dve.tensor_tensor(o[:], o[:], lnw[:].unsqueeze(1).broadcast_to([P, SUB, D]),
                                                   ALU.mult))
                            link(dve.tensor_tensor(o[:], o[:], lnb[:].unsqueeze(1).broadcast_to([P, SUB, D]),
                                                   ALU.add))
                    dve.wait_ge(f_acc, TPT * t + NE)
                    dve.tensor_tensor(acc[:, s, :, :], acc[:, s, :, :], o[:], ALU.add).then_inc(f_acc, 1)
                LINKS = 4
                gt = sb("f_gt", [P, SUB, E], F32, ph)
                f_gt = sem("f_gt")
                sweep(dve, NT, body)

            @block.gpsimd
            def _(pool):
                def body(t, s):
                    pool.wait_ge(f_os, t + 1)
                    norm_factors(pool, chain(pool, f_ve, NORM_LINKS * t), st[:], mean[:], rs[:], tmp[:],
                                 *(c[:] for c in norm_c)).then_inc(f_rs, 1)
                    pool.wait_ge(f_acc, TPT * (t + 1))
                    pool.dma_start(out_v[:, bass.ds(t * SUB, SUB), :], acc[:, s, :, :]).then_inc(f_out[s], 16)
                sweep(pool, NT, body)
                for s in range(2):
                    pool.wait_ge(f_out[s], 8 * NT)


_INS = ['L0_attn_x', 'L0_attn_Wq', 'L0_attn_bq', 'L0_attn_Wk', 'L0_attn_bk', 'L0_attn_Wv', 'L0_attn_bv',
        'L0_attn_Wo', 'L0_attn_bo', 'L0_ffn_gate_w', 'L0_ffn_gate_b', 'L0_ffn_w1', 'L0_ffn_b1', 'L0_ffn_w2',
        'L0_ffn_b2', 'L1_attn_W_qkv', 'L1_attn_b_qkv', 'L1_attn_ln_w', 'L1_attn_ln_b', 'L1_ffn_shared_w1',
        'L1_ffn_shared_w2', 'L1_ffn_experts_w1', 'L1_ffn_experts_w2', 'L1_ffn_gate_w']


def kernel(**inputs):
    import numpy as _np
    import concourse.bacc as _bacc
    from concourse import mybir as _mybir
    from concourse.bass_utils import run_bass_kernel_spmd as _run

    nc = _bacc.Bacc("TRN2", target_bir_lowering=False, num_devices=1)
    arrays, args = {}, []
    for name in _INS:
        a = _np.ascontiguousarray(inputs[name])
        arrays[f"in_{name}_dram"] = a
        args.append(nc.dram_tensor(f"in_{name}_dram", a.shape, _mybir.dt.from_np(a.dtype),
                                   kind="ExternalInput").ap())
    args.append(nc.dram_tensor("out_0_dram", (B, S, D), _mybir.dt.float32, kind="ExternalOutput").ap())
    layer_kernel(nc, *args)
    r = _run(nc, [arrays], core_ids=[0])
    return r.results[0]["out_0_dram"]
```

```python
import concourse.bass as bass
from concourse import mybir
from contextlib import ExitStack

F32 = mybir.dt.float32
BF16 = mybir.dt.bfloat16
U32 = mybir.dt.uint32
I32 = mybir.dt.int32
ALU = mybir.AluOpType
ACT = mybir.ActivationFunctionType
AX = mybir.AxisListType

P = 128
B, S, D = 32, 256, 128
T = B * S
TT = 512
NT = T // TT
SUB = TT // P
NS = T // P
H = 16
DK = D // H
E = 8
HID = 512
HC = HID // P
EPS = 1e-5
SPAN = 32
SCALE1 = 1.0 / float((D * SPAN) ** 0.5)
NPART = 3
KROWS = NPART * NPART * DK
BG = 4
NBG = B // BG
PRIO_NONE = -3.0e38
TOPK = 2
NB0 = -(-(NS + E - 1) // 4) * 4
NB1 = -(-(TOPK * NS + E - 1) // 4) * 4


def sweep(eng, n, body, unroll=2):
    assert n % unroll == 0 and n // unroll > 2
    for t in range(unroll):
        body(t, t)
    with eng.Fori(1, n // unroll - 1) as i:
        for k in range(unroll):
            body(unroll * i + k, k)
    for t in range(n - unroll, n):
        body(t, t % unroll)


def is_last(t, n):
    return isinstance(t, int) and t == n - 1


def beyond(t, ahead, n):
    return isinstance(t, int) and t + ahead >= n


def started(t, k):
    return not isinstance(t, int) or t >= k


def chain(eng, sem, base):
    state = [0]

    def link(ins):
        state[0] += 1
        ins.then_inc(sem, 1)
        eng.wait_ge(sem, base + state[0])
    return link


def settle(eng, settled):
    eng.sem_inc(settled, 1)


def row_statistics(dve, st, mv, rows, stats_done, count, settled):
    for j in range(SUB):
        ins = dve.bn_stats(st[:, j, :], rows[:, j, :])
    ins.then_inc(stats_done, 1)
    dve.wait_ge(stats_done, count + 1)
    settle(dve, settled)
    for j in range(SUB):
        ins = dve.bn_aggr(mv[:, j, :], st[:, j, :])
    return ins


def inverse_deviation(pool, mv, rstd, eps, mhalf, added, count):
    pool.tensor_tensor(rstd, mv[:, :, 1], eps[:], ALU.add).then_inc(added, 1)
    pool.wait_ge(added, count + 1)
    return pool.tensor_tensor(rstd, rstd, mhalf[:], ALU.pow)


def layer_kernel(nc, x, Wq, bq, Wk, bk, Wv, bv, Wo, bo, gate0_w, gate0_b, w1_0, b1_0, w2_0, b2_0,
                 W_qkv, b_qkv, ln_w, ln_b, sh_w1, sh_w2, w1_1, w2_1, gate1_w, out):
    x_v = x.rearrange("b (u p) d -> p (b u) d", p=P)
    out_v = out.rearrange("b (u p) d -> p (b u) d", p=P)

    xn0_d = nc.dram_tensor("xn0_d", [P, NS, D], F32).ap()
    qs_d = nc.dram_tensor("qs_d", [NPART, D, T], BF16).ap()
    ks_d = nc.dram_tensor("ks_d", [NPART, D, T], BF16).ap()
    oT_d = nc.dram_tensor("oT_d", [D, T], F32).ap()
    x2_d = nc.dram_tensor("x2_d", [P, NS, D], F32).ap()
    xn1_d = nc.dram_tensor("xn1_d", [P, NS, D], F32).ap()
    xs0_d = nc.dram_tensor("xs0_d", [NB0 * P, D], F32).ap()
    ys0_d = nc.dram_tensor("ys0_d", [NB0 * P, D], F32).ap()
    xs1_d = nc.dram_tensor("xs1_d", [NB1 * P, D], F32).ap()
    ys1_d = nc.dram_tensor("ys1_d", [NB1 * P, D], F32).ap()

    ctx = ExitStack()
    with ctx:
        def sb(name, shape, dt=F32, c=ctx):
            return c.enter_context(nc.sbuf_tensor(name, shape, dt))

        def pb(name, shape, c, dt=F32):
            return c.enter_context(nc.psum_tensor(name, shape, dt))

        def sem(name):
            return ctx.enter_context(nc.semaphore(name))

        settled = sem("settled")
        ident = sb("ident", [P, P])
        identb = sb("identb", [P, P], BF16)
        wT = sb("wT", [P, 4, P])
        g0T = sb("g0T", [P, E])
        g1T = sb("g1T", [P, E])
        bqc = sb("bqc", [P, 1])
        bkc = sb("bkc", [P, 1])
        bv_bc = sb("bv_bc", [P, D])
        gb_bc = sb("gb_bc", [P, E])
        prio = sb("prio", [P, E])
        eps = sb("eps", [P, SUB])
        mhalf = sb("mhalf", [P, SUB])
        G0 = sb("G0", [P, NS, E])
        G1 = sb("G1", [P, NS, E])
        below = sb("below", [P, P])
        ones = sb("ones", [P, P])
        thr = sb("thr", [P, E, NS * TOPK])
        blk = sb("blk", [P, NB1, E])
        row0 = sb("row0", [P, NS], U32)
        row1 = sb("row1", [P, TOPK, NS], U32)
        gate1 = sb("gate1", [P, TOPK, NS])
        eb0 = sb("eb0", [P, NB0], I32)
        eb1 = sb("eb1", [P, NB1], I32)
        vstack = ExitStack()
        V = sb("V", [P, NS, D], F32, vstack)

        with ExitStack() as ph:
            wload = sb("wload", [P, 4, P], F32, ph)
            gload = sb("gload", [E, 2, P], F32, ph)
            xt = sb("xt", [P, 4, SUB, D], F32, ph)
            xn = sb("xn", [P, 2, SUB, D], F32, ph)
            xnT = sb("xnT", [P, 2, TT], F32, ph)
            st = sb("st", [P, 2, SUB, 6], F32, ph)
            mv = sb("mv", [P, 2, SUB, 2], F32, ph)
            rs = sb("rs", [P, 2, SUB], F32, ph)
            qf = sb("qf", [P, 2, TT], F32, ph)
            rem = sb("rem", [P, 2, TT], F32, ph)
            parts = sb("parts", [P, 2, 2, NPART, TT], BF16, ph)
            pX = pb("pX", [P, TT], ph)
            pQ = pb("pQ", [P, TT], ph)
            pK = pb("pK", [P, TT], ph)
            pV = pb("pV", [P, SUB, D], ph)
            pL = pb("pL", [P, SUB, E], ph)
            pW = pb("pW", [P, 4, P], ph)
            pG = pb("pG", [P, 2, E], ph)

            a_w = sem("a_w")
            a_const = sem("a_const")
            a_wT = sem("a_wT")
            a_wTs = sem("a_wTs")
            a_x = [sem(f"a_x{i}") for i in range(4)]
            a_agg = sem("a_agg")
            a_st = sem("a_st")
            a_ve = sem("a_ve")
            a_rs = sem("a_rs")
            a_xn = sem("a_xn")
            a_tr = sem("a_tr")
            a_xT = sem("a_xT")
            a_xnd = [sem("a_xnd0"), sem("a_xnd1")]
            a_zero = sem("a_zero")
            a_fill = sem("a_fill")
            a_q = sem("a_q")
            a_v = sem("a_v")
            a_qf = sem("a_qf")
            a_mid = sem("a_mid")
            a_rem = sem("a_rem")
            a_low = sem("a_low")
            a_vs = sem("a_vs")
            a_pd = [sem("a_pd0"), sem("a_pd1")]
            WLOADS = 10
            FILL = 2048
            FILLS = sum(-(-nb * D // FILL) for nb in (NB0, NB1))
            zero = sb("zero", [P, FILL], F32, ph)

            block = ph.enter_context(nc.Block())

            @block.sync
            def _(sp):
                for n, w in enumerate((Wq, Wk, Wv, Wo)):
                    sp.dma_start(wload[:, n, :], w).then_inc(a_w, 16)
                sp.dma_start(gload[:, 0, :], gate0_w).then_inc(a_w, 16)
                sp.dma_start(gload[:, 1, :], gate1_w).then_inc(a_w, 16)
                sp.dma_start(bqc[:], bq.rearrange("(p a) -> p a", a=1)).then_inc(a_w, 16)
                sp.dma_start(bkc[:], bk.rearrange("(p a) -> p a", a=1)).then_inc(a_w, 16)
                sp.dma_start(bv_bc[:], bv.partition_broadcast(P)).then_inc(a_w, 16)
                sp.dma_start(gb_bc[:], gate0_b.partition_broadcast(P)).then_inc(a_w, 16)

                def store_norm(t, s):
                    sp.dma_start(xn0_d[:, bass.ds(t * SUB, SUB), :], xn[:, s, :, :]).then_inc(a_xnd[s], 16)

                def body(t, q):
                    if started(t, 4):
                        sp.wait_ge(a_xn, t - 3)
                        settle(sp, settled)
                    sp.dma_start(xt[:, q, :, :], x_v[:, bass.ds(t * SUB, SUB), :]).then_inc(a_x[q], 16)
                    if started(t, 4):
                        store_norm(t - 4, q % 2)
                sp.wait_ge(a_zero, 1)
                for rows, nb in ((xs0_d, NB0), (xs1_d, NB1)):
                    v = rows.rearrange("(p n) d -> p (n d)", p=P)
                    for c in range(0, nb * D, FILL):
                        w = min(FILL, nb * D - c)
                        sp.dma_start(v[:, c:c + w], zero[:, 0:w]).then_inc(a_fill, 16)
                sweep(sp, NT, body, 4)
                for t in range(NT - 4, NT):
                    sp.wait_ge(a_xn, t + 1)
                    store_norm(t, t % 2)

            @block.gpsimd
            def _(pool):
                pool.memset(ones[:], 1.0).then_inc(a_const, 1)
                pool.memset(zero[:], 0.0).then_inc(a_zero, 1)
                pool.memset(ident[:], 0.0).then_inc(a_const, 1)
                pool.memset(identb[:], 0.0).then_inc(a_const, 1)
                for c, value in ((eps, EPS), (mhalf, -0.5)):
                    pool.memset(c[:], value).then_inc(a_const, 1)
                for e in range(E):
                    pool.memset(prio[:, e:e + 1], float(E - e)).then_inc(a_const, 1)
                pool.wait_ge(a_const, 5 + E)
                for m in (ident, identb):
                    pool.affine_select(out=m[:], in_=m[:], compare_op=ALU.not_equal, fill=1.0, base=0,
                                       pattern=[[-1, P]], channel_multiplier=1).then_inc(a_const, 1)
                pool.memset(below[:], 1.0).then_inc(a_const, 1)
                pool.wait_ge(a_const, 8 + E)
                pool.affine_select(out=below[:], in_=below[:], compare_op=ALU.is_gt, fill=0.0, base=0,
                                   pattern=[[1, P]], channel_multiplier=-1)
                pool.iota(thr[:], [[0, E], [P, NS * TOPK]], base=0, channel_multiplier=0,
                          allow_small_or_imprecise_dtypes=True)
                pool.iota(blk[:], [[1, NB1], [0, E]], base=0, channel_multiplier=0,
                          allow_small_or_imprecise_dtypes=True)

                def deviation(t, s):
                    pool.wait_ge(a_agg, t + 1)
                    if started(t, 2):
                        pool.wait_ge(a_xn, t - 1)
                    inverse_deviation(pool, mv[:, s, :, :], rs[:, s, :], eps, mhalf, a_ve, t).then_inc(a_rs, 1)

                def third_part(t, s, n):
                    pool.wait_ge(a_qf, 4 * t + 2 * n + 2)
                    if started(t, 1):
                        pool.wait_ge(a_low, 2 * t + n)
                    pool.tensor_tensor(rem[:, n, :], qf[:, n, :], parts[:, s, n, 0, :],
                                       ALU.subtract).then_inc(a_rem, 1)
                    pool.wait_ge(a_rem, 2 * t + n + 1)
                    pool.wait_ge(a_mid, 2 * t + n + 1)
                    pool.tensor_tensor(parts[:, s, n, 2, :], rem[:, n, :], parts[:, s, n, 1, :],
                                       ALU.subtract).then_inc(a_low, 1)

                def body(t, s):
                    third_part(t, s, 0)
                    third_part(t, s, 1)
                    if not beyond(t, 3, NT):
                        deviation(t + 3, 1 - s)
                for t in range(3):
                    deviation(t, t % 2)
                sweep(pool, NT, lambda t, q: body(t, q % 2), 4)

            @block.vector
            def _(dve):
                dve.wait_ge(a_wT, 2)
                dve.tensor_copy(wT[:], pW[:]).then_inc(a_wTs, 1)
                dve.tensor_copy(g0T[:], pG[:, 0, :]).then_inc(a_wTs, 1)
                dve.tensor_copy(g1T[:], pG[:, 1, :]).then_inc(a_wTs, 1)
                dve.wait_ge(a_w, 16 * WLOADS)

                def statistics(t, q):
                    s = q % 2
                    dve.wait_ge(a_x[q], 4 * (t - q) + 16)
                    if started(t, 2):
                        dve.wait_ge(a_rs, t - 1)
                    row_statistics(dve, st[:, s, :, :], mv[:, s, :, :], xt[:, q, :, :], a_st, t, settled)\
                        .then_inc(a_agg, 1)

                def norm(t, q):
                    s = q % 2
                    dve.wait_ge(a_rs, t + 1)
                    if started(t, 2):
                        dve.wait_ge(a_tr, t - 1)
                        dve.wait_ge(a_xnd[s], 8 * (t - s))
                    for j in range(SUB):
                        ins = dve.tensor_scalar(xn[:, s, j, :], xt[:, q, j, :], mv[:, s, j, 0:1],
                                                rs[:, s, j:j + 1], ALU.subtract, ALU.mult)
                    ins.then_inc(a_xn, 1)

                def body(t, q):
                    s = q % 2
                    for n in range(2):
                        dve.wait_ge(a_qf, 4 * t + 2 * n + 2)
                        dve.tensor_tensor(parts[:, s, n, 1, :], qf[:, n, :], parts[:, s, n, 0, :],
                                          ALU.subtract).then_inc(a_mid, 1)
                    dve.wait_ge(a_v, t + 1)
                    dve.tensor_tensor(V[:, bass.ds(t * SUB, SUB), :], pV[:],
                                      bv_bc[:].unsqueeze(1).broadcast_to([P, SUB, D]), ALU.add)
                    dve.tensor_tensor(G0[:, bass.ds(t * SUB, SUB), :], pL[:],
                                      gb_bc[:].unsqueeze(1).broadcast_to([P, SUB, E]), ALU.add)\
                       .then_inc(a_vs, 1)
                    if not beyond(t, 2, NT):
                        norm(t + 2, (q + 2) % 4)
                    if not beyond(t, 3, NT):
                        statistics(t + 3, (q + 3) % 4)
                statistics(0, 0)
                statistics(1, 1)
                norm(0, 0)
                norm(1, 1)
                statistics(2, 2)
                sweep(dve, NT, body, 4)

            @block.tensor
            def _(pe):
                pe.wait_ge(a_w, 16 * WLOADS)
                pe.wait_ge(a_const, 7 + E)
                for n in range(4):
                    ins = nc.tensor.transpose(pW[:, n, :], wload[:, n, :], ident[:])
                ins.then_inc(a_wT, 1)
                for n in range(2):
                    ins = nc.tensor.transpose(pG[:, n, :], gload[:, n, :], ident[0:E, 0:E])
                ins.then_inc(a_wT, 1)
                pe.wait_ge(a_wTs, 3)

                def transpose(t, s):
                    pe.wait_ge(a_xn, t + 1)
                    if started(t, 1):
                        pe.wait_ge(a_xT, t)
                    for j in range(SUB):
                        ins = nc.tensor.transpose(pX[:, j * P:(j + 1) * P], xn[:, s, j, :], ident[:])
                    ins.then_inc(a_tr, 1)

                def body(t, s):
                    if not is_last(t, NT):
                        transpose(t + 1, 1 - s)
                    pe.wait_ge(a_xT, t + 1)
                    if started(t, 1):
                        pe.wait_ge(a_qf, 4 * t)
                    nc.tensor.matmul(pQ[:], wT[:, 0, :], xnT[:, s, :], start=True, stop=True).then_inc(a_q, 1)
                    nc.tensor.matmul(pK[:], wT[:, 1, :], xnT[:, s, :], start=True, stop=True).then_inc(a_q, 1)
                    if started(t, 1):
                        pe.wait_ge(a_vs, t)
                    for j in range(SUB):
                        nc.tensor.matmul(pV[:, j, :], xnT[:, s, j * P:(j + 1) * P], wT[:, 2, :],
                                         start=True, stop=True)
                        ins = nc.tensor.matmul(pL[:, j, :], xnT[:, s, j * P:(j + 1) * P], g0T[:],
                                               start=True, stop=True)
                    ins.then_inc(a_v, 1)
                transpose(0, 0)
                sweep(pe, NT, body)

            @block.scalar
            def _(act):
                def copy_x(t, s):
                    act.wait_ge(a_tr, t + 1)
                    if started(t, 2):
                        act.wait_ge(a_v, t - 1)
                    act.copy(xnT[:, s, :], pX[:]).then_inc(a_xT, 1)

                act.wait_ge(a_w, 16 * WLOADS)

                def body(t, s):
                    if not is_last(t, NT):
                        copy_x(t + 1, 1 - s)
                    if started(t, 1):
                        act.wait_ge(a_low, 2 * t)
                        act.wait_ge(a_mid, 2 * t)
                    if started(t, 2):
                        act.wait_ge(a_pd[s], 16 * (t - s))
                    for n, (ps, bias) in enumerate(((pQ, bqc), (pK, bkc))):
                        act.wait_ge(a_q, 2 * t + n + 1)
                        act.activation(qf[:, n, :], ps[:], ACT.Identity, bias=bias[:]).then_inc(a_qf, 1)
                        act.activation(parts[:, s, n, 0, :], ps[:], ACT.Identity, bias=bias[:])\
                           .then_inc(a_qf, 1)
                    if started(t, 1):
                        store(t - 1, 1 - s)

                def store(t, s):
                    for n, dst in enumerate((qs_d, ks_d)):
                        act.wait_ge(a_low, 2 * t + n + 1)
                        act.wait_ge(a_mid, 2 * t + n + 1)
                        act.dma_start(dst[:, :, bass.ds(t * TT, TT)].rearrange("a d t -> d a t"),
                                      parts[:, s, n, :, :]).then_inc(a_pd[s], 16)
                copy_x(0, 0)
                sweep(act, NT, body)
                store(NT - 1, 1)
                for s in range(2):
                    act.wait_ge(a_pd[s], 16 * NT)
                    act.wait_ge(a_xnd[s], 8 * NT)
                act.wait_ge(a_fill, 16 * FILLS)

        def first_of_largest(dve, link, lg, oh, m, c):
            link(dve.tensor_reduce(m[:], lg[:], AX.X, ALU.max))
            link(dve.tensor_tensor(oh[:], lg[:], m[:].unsqueeze(2).broadcast_to([P, NS, E]), ALU.is_equal))
            link(dve.tensor_tensor(oh[:], oh[:], prio[:].unsqueeze(1).broadcast_to([P, NS, E]), ALU.mult))
            link(dve.tensor_reduce(c[:], oh[:], AX.X, ALU.max))
            link(dve.tensor_tensor(oh[:], oh[:], c[:].unsqueeze(2).broadcast_to([P, NS, E]), ALU.is_equal))

        def route(pre, chosen, hits, rows, eb, nb, first_weight):
            with ExitStack() as ph:
                within = pb(pre + "within", [P, NS, E], ph)
                total = pb(pre + "total", [P, NS, E], ph)
                upto = [sb(f"{pre}upto{i}", [P, NS, E], F32, ph) for i in range(2)]
                rk = sb(pre + "rk", [P, NS, E], F32, ph)
                pick = sb(pre + "pick", [P, NS, E], F32, ph)
                rowf = sb(pre + "rowf", [P, NS], F32, ph)
                need = sb(pre + "need", [P, E, NS * TOPK], F32, ph)
                nblk = sb(pre + "nblk", [P, E], F32, ph)
                end = [sb(f"{pre}end{i}", [P, E], F32, ph) for i in range(2)]
                past = sb(pre + "past", [P, nb, E], F32, ph)
                ebf = sb(pre + "ebf", [P, nb], F32, ph)
                r_link = sem(pre + "r_link")
                r_hits = sem(pre + "r_hits")
                r_cnt = sem(pre + "r_cnt")
                r_top = sem(pre + "r_top")
                r_exp = sem(pre + "r_exp")
                block = ph.enter_context(nc.Block())

                @block.tensor
                def _(pe):
                    pe.wait_ge(r_hits, 1)
                    C = hits[-1][:].rearrange("p n e -> p (n e)")
                    nc.tensor.matmul(within[:].rearrange("p n e -> p (n e)"), below[:], C,
                                     start=True, stop=True)
                    nc.tensor.matmul(total[:].rearrange("p n e -> p (n e)"), ones[:], C,
                                     start=True, stop=True).then_inc(r_cnt, 1)

                if pre == "r1":
                    @block.scalar
                    def _(act):
                        act.wait_ge(r_top, 1)
                        act.activation(gate1[:, 1, :], gate1[:, 0, :], ACT.Exp).then_inc(r_exp, 1)

                @block.vector
                def _(dve):
                    link = chain(dve, r_link, 0)
                    chosen(dve, link, r_top, r_exp)
                    dve.sem_inc(r_hits, 1)
                    dve.wait_ge(r_cnt, 1)
                    link(dve.tensor_copy(upto[0][:], total[:]))
                    cur, step = 0, 1
                    while step < NS:
                        a, b = upto[cur], upto[1 - cur]
                        dve.tensor_copy(b[:, 0:step, :], a[:, 0:step, :])
                        link(dve.tensor_tensor(b[:, step:, :], a[:, step:, :], a[:, 0:NS - step, :], ALU.add))
                        cur, step = 1 - cur, 2 * step
                    A = upto[cur]
                    link(dve.tensor_tensor(rk[:], A[:], total[:], ALU.subtract))
                    link(dve.tensor_tensor(rk[:], rk[:], within[:], ALU.add))
                    link(dve.tensor_tensor(need[:], A[:, NS - 1, :].unsqueeze(2).broadcast_to([P, E, NS * TOPK]),
                                           thr[:], ALU.is_gt))
                    link(dve.tensor_reduce(nblk[:], need[:], AX.X, ALU.add))
                    link(dve.tensor_copy(end[0][:], nblk[:]))
                    cur, step = 0, 1
                    while step < E:
                        a, b = end[cur], end[1 - cur]
                        dve.tensor_copy(b[:, 0:step], a[:, 0:step])
                        link(dve.tensor_tensor(b[:, step:], a[:, step:], a[:, 0:E - step], ALU.add))
                        cur, step = 1 - cur, 2 * step
                    last = end[cur]
                    link(dve.tensor_tensor(nblk[:], last[:], nblk[:], ALU.subtract))
                    link(dve.tensor_scalar(nblk[:], nblk[:], float(P), None, ALU.mult))
                    link(dve.tensor_tensor(rk[:], rk[:], nblk[:].unsqueeze(1).broadcast_to([P, NS, E]), ALU.add))
                    for oh, row in zip(hits, rows):
                        link(dve.tensor_tensor(pick[:], oh[:], rk[:], ALU.mult))
                        link(dve.tensor_reduce(rowf[:], pick[:], AX.X, ALU.add))
                        link(dve.tensor_copy(row, rowf[:]))
                    link(dve.tensor_tensor(past[:], blk[:, 0:nb, :],
                                           last[:].unsqueeze(1).broadcast_to([P, nb, E]), ALU.is_ge))
                    link(dve.tensor_reduce(ebf[:], past[:], AX.X, ALU.add))
                    link(dve.tensor_scalar(eb[:], ebf[:], float(E - 1), float(first_weight), ALU.min, ALU.add))

        def scatter(pre, src, rows, dst):
            with ExitStack() as ph:
                xr = sb(pre + "xr", [P, 2, SUB, D], F32, ph)
                idx = sb(pre + "idx", [P, 2, len(rows), SUB], U32, ph)
                t_x = [sem(pre + "t_x0"), sem(pre + "t_x1")]
                t_i = sem(pre + "t_i")
                t_d = [sem(pre + "t_d0"), sem(pre + "t_d1")]
                PER = 16 * SUB * len(rows)
                block = ph.enter_context(nc.Block())

                @block.sync
                def _(sp):
                    def body(t, s):
                        if started(t, 2):
                            sp.wait_ge(t_d[s], (t - s) * (PER // 2))
                        settle(sp, settled)
                        sp.dma_start(xr[:, s, :, :], src[:, bass.ds(t * SUB, SUB), :]).then_inc(t_x[s], 16)
                    sweep(sp, NT, body)

                @block.vector
                def _(dve):
                    def body(t, s):
                        if started(t, 2):
                            dve.wait_ge(t_d[s], (t - s) * (PER // 2))
                        for i, row in enumerate(rows):
                            ins = dve.tensor_copy(idx[:, s, i, :], row[:, bass.ds(t * SUB, SUB)])
                        ins.then_inc(t_i, 1)
                    sweep(dve, NT, body)

                @block.gpsimd
                def _(pool):
                    def body(t, s):
                        pool.wait_ge(t_x[s], 8 * (t - s) + 16)
                        pool.wait_ge(t_i, t + 1)
                        settle(pool, settled)
                        for i in range(len(rows)):
                            for j in range(SUB):
                                pool.indirect_dma_start(
                                    out=dst, out_offset=bass.IndirectOffsetOnAxis(idx[:, s, i, j:j + 1], 0),
                                    in_=xr[:, s, j, :], in_offset=None).then_inc(t_d[s], 16)
                    sweep(pool, NT, body)
                    for s in range(2):
                        pool.wait_ge(t_d[s], PER * NT // 2)

        with ExitStack() as rs0:
            oh = sb("oh0", [P, NS, E], F32, rs0)
            m0 = sb("m0", [P, NS], F32, rs0)
            c0 = sb("c0", [P, NS], F32, rs0)
            route("r0", lambda dve, link, top, ex: first_of_largest(dve, link, G0, oh, m0, c0),
                  [oh, oh], [row0[:]], eb0, NB0, 0)
        scatter("s0", xn0_d, [row0[:]], xs0_d)

        with ExitStack() as ph:
            qk = sb("qk", [KROWS, 2, 2, T], BF16, ph)
            Ex = sb("Ex", [P, 4, B, P], F32, ph)
            Vh = sb("Vh", [P, 2, NS, DK], F32, ph)
            mg = sb("mg", [P, P, NBG], F32, ph)
            negm = sb("negm", [P, P], F32, ph)
            mh = sb("mh", [P, 2, P], BF16, ph)
            ml = sb("ml", [P, 2, P], BF16, ph)
            Zg = sb("Zg", [P, P, 4], F32, ph)
            Z = sb("Z", [P, P], F32, ph)
            R = sb("R", [P, 2, P], F32, ph)
            Oev = sb("Oev", [P, 2, NBG, P], F32, ph)
            pA = pb("pA", [P, 2, BG, P], ph)
            pB = pb("pB", [P, 2, 2, BG, P], ph)
            pO = pb("pO", [P, NBG, P], ph)

            b_qk = [sem("b_qk0"), sem("b_qk1")]
            b_z = sem("b_z")
            b_s1 = sem("b_s1")
            b_red = sem("b_red")
            b_nm = sem("b_nm")
            b_mh = sem("b_mh")
            b_m = sem("b_m")
            b_s2 = sem("b_s2")
            b_exp = sem("b_exp")
            b_part = sem("b_part")
            b_sum = sem("b_sum")
            b_r = sem("b_r")
            b_norm = sem("b_norm")
            b_vh = sem("b_vh")
            b_pv = sem("b_pv")
            b_oev = sem("b_oev")
            b_od = [sem("b_od0"), sem("b_od1")]
            LOADS = 12 * 16
            oT_v = oT_d.rearrange("(n d) (g c h q) -> n d g c h q", d=DK, g=NBG, c=BG, h=2)

            block = ph.enter_context(nc.Block())

            @block.sync
            def _(sp):
                def load(h, s):
                    for i in range(NPART):
                        for j in range(NPART):
                            r = (NPART * i + j) * DK
                            sp.dma_start(qk[r:r + DK, s, 0, :], qs_d[i, bass.ds(h * DK, DK), :])\
                              .then_inc(b_qk[s], 16)
                    for i in range(NPART):
                        r = NPART * i * DK
                        sp.dma_start(qk[r:r + NPART * DK, s, 1, :],
                                     ks_d[:, bass.ds(h * DK, DK), :]).then_inc(b_qk[s], 16)

                def store(h, w, qh):
                    sp.wait_ge(b_oev, w + 1)
                    settle(sp, settled)
                    for c in range(BG):
                        sp.dma_start(oT_v[bass.ds(h, 1), :, :, c, qh, :].squeeze(0),
                                     Oev[32 * c:32 * c + DK, qh, :, :]).then_inc(b_od[qh], 16)

                def body(h, s):
                    if started(h, 1):
                        sp.wait_ge(b_s2, 16 * h)
                    if not is_last(h, H):
                        load(h + 1, 1 - s)
                    if started(h, 1):
                        store(h - 1, 2 * h - 1, 1)
                    store(h, 2 * h, 0)
                load(0, 0)
                sweep(sp, H, body)
                store(H - 1, 2 * H - 1, 1)
                for qh in range(2):
                    sp.wait_ge(b_od[qh], 16 * BG * H)

            @block.tensor
            def _(pe):
                def s1_group(n, head_slot, qh, kc, g):
                    if not isinstance(n, int) or n >= 2:
                        pe.wait_ge(b_red, n - 1)
                    for c in range(BG):
                        tok = (BG * g + c) * S
                        ins = nc.tensor.matmul(pA[:, g % 2, c, :],
                                               qk[:, head_slot, 1, tok + kc * P:tok + kc * P + P],
                                               qk[:, head_slot, 0, tok + qh * P:tok + qh * P + P],
                                               start=True, stop=True)
                    ins.then_inc(b_s1, 1)

                def s2_group(n, u, s, j, g):
                    qh, kc = j // 2, j % 2
                    if not isinstance(n, int) or n >= 2:
                        pe.wait_ge(b_exp, n - 1)
                    for k in range(2):
                        for i, m in enumerate((mh, ml)):
                            nc.tensor.matmul(pB[:, g % 2, k, :, :], identb[:],
                                             m[:, j % 2, :].unsqueeze(1).broadcast_to([P, BG, P]),
                                             start=(i == 0), stop=False, skip_group_check=True)
                        for c in range(BG):
                            tok = (2 * BG * g + BG * k + c) * S
                            ins = nc.tensor.matmul(pB[:, g % 2, k, c, :],
                                                   qk[:, s, 1, tok + kc * P:tok + kc * P + P],
                                                   qk[:, s, 0, tok + qh * P:tok + qh * P + P],
                                                   start=False, stop=(c == BG - 1), skip_group_check=True)
                    ins.then_inc(b_s2, 1)

                def pv_group(v, s, j, g):
                    kc = j % 2
                    for k in range(2):
                        for c in range(BG):
                            b = 2 * BG * g + BG * k + c
                            ins = nc.tensor.matmul(pO[32 * c:32 * c + DK, b // BG, :],
                                                   Vh[:, s, 2 * b + kc, :], Ex[:, j, b, :],
                                                   start=(kc == 0 and (b // BG) % 4 == 0), stop=(kc == 1),
                                                   skip_group_check=True)
                    if g == 3:
                        ins.then_inc(b_pv, 1)

                def pv_waits(v, h, j):
                    pe.wait_ge(b_norm, v + 1)
                    if j == 0:
                        pe.wait_ge(b_vh, h + 1)
                    if j % 2 == 0:
                        if not isinstance(h, int) or 2 * h + j // 2 > 0:
                            pe.wait_ge(b_oev, 2 * h + j // 2)

                def body(h, s):
                    for j in range(4):
                        u = 4 * h + j
                        first_pv = started(h, 1) or j >= 2
                        lag_j, lag_s = (j - 2, s) if j >= 2 else (j + 2, 1 - s)
                        for g in range(NBG):
                            if j < 3:
                                s1_group(8 * (u + 1) + g, s, (j + 1) // 2, (j + 1) % 2, g)
                            elif not is_last(h, H):
                                if g == 0:
                                    pe.wait_ge(b_qk[1 - s], (h + 1 - (1 - s)) * (LOADS // 2) + LOADS)
                                s1_group(8 * (u + 1) + g, 1 - s, 0, 0, g)
                            if g % 2 == 1:
                                if g == 1:
                                    pe.wait_ge(b_m, u + 1)
                                s2_group(4 * u + g // 2, u, s, j, g // 2)
                                if first_pv:
                                    if g == 1:
                                        pv_waits(u - 2, h if j >= 2 else h - 1, lag_j)
                                    pv_group(u - 2, lag_s, lag_j, g // 2)

                pe.wait_ge(b_z, 1)
                pe.wait_ge(b_qk[0], LOADS)
                for g in range(NBG):
                    s1_group(g, 0, 0, 0, g)
                sweep(pe, H, body)
                for j in (2, 3):
                    pv_waits(4 * (H - 1) + j, H - 1, j)
                    for g in range(4):
                        pv_group(4 * (H - 1) + j, 1, j, g)

            @block.vector
            def _(dve):
                def group_max(u, g):
                    dve.wait_ge(b_s1, 8 * u + g + 1)
                    dve.tensor_reduce(mg[:, :, g], pA[:, g % 2, :, :].rearrange("p b q -> p q b"),
                                      AX.X, ALU.max).then_inc(b_red, 1)

                def unit_max(u, m):
                    dve.wait_ge(b_red, 8 * u + 8)
                    if not isinstance(u, int) or u >= 1:
                        dve.wait_ge(b_m, u)
                    dve.tensor_reduce(negm[:], mg[:], AX.X, ALU.max, negate=True).then_inc(b_nm, 1)
                    dve.wait_ge(b_nm, u + 1)
                    if not isinstance(u, int) or u >= 2:
                        dve.wait_ge(b_s2, 4 * (u - 1))
                    dve.tensor_copy(mh[:, m, :], negm[:]).then_inc(b_mh, 1)
                    dve.wait_ge(b_mh, u + 1)
                    dve.tensor_tensor(ml[:, m, :], negm[:], mh[:, m, :], ALU.subtract).then_inc(b_m, 1)

                def group_sum(u, j, g):
                    if g == 0 and (not isinstance(u, int) or u >= 1):
                        dve.wait_ge(b_sum, u)
                    dve.wait_ge(b_exp, 4 * u + g + 1)
                    dve.tensor_reduce(Zg[:, :, g],
                                      Ex[:, j, 2 * BG * g:2 * BG * (g + 1), :].rearrange("p b q -> p q b"),
                                      AX.X, ALU.add).then_inc(b_part, 1)

                def unit_sum(u, j):
                    dve.wait_ge(b_part, 4 * u + 4)
                    if not isinstance(u, int) or u >= 1:
                        dve.wait_ge(b_r, u)
                    dve.tensor_reduce(Z[:], Zg[:], AX.X, ALU.add).then_inc(b_sum, 1)
                    dve.wait_ge(b_sum, u + 1)
                    if not isinstance(u, int) or u >= 2:
                        dve.wait_ge(b_norm, u - 1)
                    dve.reciprocal(R[:, j % 2, :], Z[:]).then_inc(b_r, 1)

                def body(h, s):
                    for j in range(4):
                        u = 4 * h + j
                        more = not (is_last(h, H) and j == 3)
                        for g in range(4):
                            if more:
                                group_max(u + 1, 2 * g)
                                group_max(u + 1, 2 * g + 1)
                            if g:
                                group_sum(u, j, g - 1)
                        if more:
                            unit_max(u + 1, (j + 1) % 2)
                        group_sum(u, j, 3)
                        unit_sum(u, j)

                dve.memset(pO[:], 0.0).then_inc(b_z, 1)
                for g in range(NBG):
                    group_max(0, g)
                unit_max(0, 0)
                sweep(dve, H, body)

            @block.scalar
            def _(act):
                def evac(h, qh):
                    w = 2 * h + qh
                    act.wait_ge(b_pv, 2 * w + 2)
                    if started(h, 1):
                        act.wait_ge(b_od[qh], 16 * BG * h)
                    act.copy(Oev[:, qh, :, :], pO[:]).then_inc(b_oev, 1)

                def body(h, s):
                    if started(h, 2):
                        act.wait_ge(b_pv, 4 * (h - 1))
                    act.copy(Vh[:, s, :, :], V[:, :, bass.ds(h * DK, DK)]).then_inc(b_vh, 1)
                    for j in range(4):
                        u = 4 * h + j
                        if started(h, 1):
                            act.wait_ge(b_pv, u - 3)
                        for g in range(4):
                            act.wait_ge(b_s2, 4 * u + g + 1)
                            act.activation(Ex[:, j, 2 * BG * g:2 * BG * (g + 1), :],
                                           pB[:, g % 2, :, :, :].rearrange("p k b q -> p (k b) q"),
                                           ACT.Exp).then_inc(b_exp, 1)
                        if j == 1 and started(h, 1):
                            evac(h - 1, 1)
                        if j == 3:
                            evac(h, 0)
                sweep(act, H, body)
                evac(H - 1, 1)

            @block.gpsimd
            def _(pool):
                def body(h, s):
                    for j in range(4):
                        u = 4 * h + j
                        pool.wait_ge(b_r, u + 1)
                        pool.tensor_tensor(Ex[:, j, :, :], Ex[:, j, :, :],
                                           R[:, j % 2, :].unsqueeze(1).broadcast_to([P, B, P]),
                                           ALU.mult).then_inc(b_norm, 1)
                sweep(pool, H, body)

        vstack.close()

        w1T = sb("w1T", [P, 2 * E + 1, HID])
        w2T = sb("w2T", [P, 2 * E + 1, HC, D])
        b1x = sb("b1x", [P, E, HID])
        b2x = sb("b2x", [P, E, D])
        wqkv = sb("wqkv", [P, 3 * D])
        bqk1 = sb("bqk1", [P, 2])
        bv1 = sb("bv1", [P, D])
        lnw = sb("lnw", [P, D])
        lnb = sb("lnb", [P, D])
        mdiag = sb("mdiag", [P, P])
        mcross = sb("mcross", [P, P])

        with ExitStack() as ph:
            bo_bc = sb("bo_bc", [P, D], F32, ph)
            w1l = sb("w1l", [P, 2, HC, D], F32, ph)
            w2l = sb("w2l", [P, 2, HID], F32, ph)
            p1 = pb("p1", [P, 2, HID], ph)
            p2 = pb("p2", [P, 2, HC, D], ph)
            c_w = [sem("c_w0"), sem("c_w1")]
            c_s = sem("c_s")
            c_tr = sem("c_tr")
            c_ev1 = sem("c_ev1")
            c_ev2 = sem("c_ev2")
            c_m = sem("c_m")
            SMALL = 9

            block = ph.enter_context(nc.Block())

            def groups(eng, one):
                sweep(eng, E, lambda e, s: one(e, s, w1_0, w2_0, e))
                sweep(eng, E, lambda e, s: one(E + e, s, w1_1, w2_1, e))
                one(2 * E, 0, None, None, 0)

            @block.sync
            def _(sp):
                sp.dma_start(b1x[:], b1_0.partition_broadcast(P)).then_inc(c_s, 16)
                sp.dma_start(b2x[:], b2_0.partition_broadcast(P)).then_inc(c_s, 16)
                sp.dma_start(bo_bc[:], bo.partition_broadcast(P)).then_inc(c_s, 16)
                sp.dma_start(wqkv[:], W_qkv).then_inc(c_s, 16)
                sp.dma_start(bqk1[:, 0:1], b_qkv[0:D].rearrange("(p a) -> p a", a=1)).then_inc(c_s, 16)
                sp.dma_start(bqk1[:, 1:2], b_qkv[D:2 * D].rearrange("(p a) -> p a", a=1)).then_inc(c_s, 16)
                sp.dma_start(bv1[:], b_qkv[2 * D:3 * D].partition_broadcast(P)).then_inc(c_s, 16)
                sp.dma_start(lnw[:], ln_w.partition_broadcast(P)).then_inc(c_s, 16)
                sp.dma_start(lnb[:], ln_b.partition_broadcast(P)).then_inc(c_s, 16)

                def one(k, s, w1, w2, e):
                    if started(k, 2):
                        sp.wait_ge(c_tr, k - 1)
                    a = sh_w1 if w1 is None else w1[e, :, :]
                    b = sh_w2 if w2 is None else w2[e, :, :]
                    sp.dma_start(w1l[:, s, :, :], a.rearrange("(c p) d -> p c d", p=P)).then_inc(c_w[s], 16)
                    sp.dma_start(w2l[:, s, :], b).then_inc(c_w[s], 16)
                groups(sp, one)
                sp.wait_ge(c_s, 16 * SMALL)

            @block.tensor
            def _(pe):
                def one(k, s, w1, w2, e):
                    pe.wait_ge(c_w[s], 16 * (k - s) + 32)
                    if started(k, 2):
                        pe.wait_ge(c_ev1, k - 1)
                        pe.wait_ge(c_ev2, k - 1)
                    for c in range(HC):
                        nc.tensor.transpose(p1[:, s, c * P:(c + 1) * P], w1l[:, s, c, :], ident[:])
                        ins = nc.tensor.transpose(p2[:, s, c, :], w2l[:, s, c * P:(c + 1) * P], ident[:])
                    ins.then_inc(c_tr, 1)
                groups(pe, one)

            @block.scalar
            def _(act):
                def one(k, s, w1, w2, e):
                    act.wait_ge(c_tr, k + 1)
                    act.copy(w1T[:, bass.ds(k, 1), :], p1[:, s, :].unsqueeze(1)).then_inc(c_ev1, 1)
                groups(act, one)

            @block.vector
            def _(dve):
                def one(k, s, w1, w2, e):
                    dve.wait_ge(c_tr, k + 1)
                    dve.tensor_copy(w2T[:, bass.ds(k, 1), :, :], p2[:, s, :, :].unsqueeze(1)).then_inc(c_ev2, 1)
                groups(dve, one)
                dve.wait_ge(c_s, 16 * SMALL)
                dve.tensor_tensor(b2x[:], b2x[:], bo_bc[:].unsqueeze(1).broadcast_to([P, E, D]), ALU.add)

            @block.gpsimd
            def _(pool):
                link = chain(pool, c_m, 0)
                link(pool.memset(mdiag[:], 1.0))
                link(pool.memset(mcross[:], 1.0))
                link(pool.affine_select(out=mdiag[:], in_=mdiag[:], compare_op=ALU.is_ge, fill=0.0, base=0,
                                        pattern=[[1, P]], channel_multiplier=-1))
                link(pool.affine_select(out=mdiag[:], in_=mdiag[:], compare_op=ALU.is_ge, fill=0.0,
                                        base=SPAN - 1, pattern=[[-1, P]], channel_multiplier=1))
                link(pool.affine_select(out=mcross[:], in_=mcross[:], compare_op=ALU.is_ge, fill=0.0,
                                        base=SPAN - 1 - P, pattern=[[-1, P]], channel_multiplier=1))

        e_x = [sem(f"e_x{i}") for i in range(4)]
        e_xp = sem("e_xp")
        e_xT = sem("e_xT")
        e_u = sem("e_u")
        e_hb = sem("e_hb")
        e_hp = sem("e_hp")
        e_hT = sem("e_hT")
        e_y = sem("e_y")
        e_yb = sem("e_yb")
        e_st = [sem(f"e_st{i}") for i in range(4)]

        def experts(pre, layer, xs, ys, eb, nb, k0):
            with ExitStack() as ph:
                xb = sb(pre + "xb", [P, 4, D], F32, ph)
                xT = sb(pre + "xT", [P, 2, P], F32, ph)
                hb = sb(pre + "hb", [P, 2, HID], F32, ph)
                hT = sb(pre + "hT", [P, 2, HC, P], F32, ph)
                yb = sb(pre + "yb", [P, 4, D], F32, ph)
                pX = [pb(f"{pre}pX{i}", [P, P], ph) for i in range(2)]
                pU = [pb(f"{pre}pU{i}", [P, HID], ph) for i in range(2)]
                pT = [pb(f"{pre}pT{i}", [P, HC, P], ph) for i in range(2)]
                pY = [pb(f"{pre}pY{i}", [P, D], ph) for i in range(2)]
                lo, hi = (0, E - 1) if layer == 0 else (E, 2 * E - 1)
                block = ph.enter_context(nc.Block())

                def expert_of(eng, k):
                    return eng.value_load(eb[0:1, bass.ds(k, 1)], min_val=lo, max_val=hi)

                @block.sync
                def _(sp):
                    def load(k, q):
                        sp.dma_start(xb[:, q, :], xs[bass.ds(k * P, P), :]).then_inc(e_x[q], 16)

                    def body(k, q):
                        sp.wait_ge(e_yb, k0 + k + 1)
                        settle(sp, settled)
                        sp.dma_start(ys[bass.ds(k * P, P), :], yb[:, q, :]).then_inc(e_st[q], 16)
                        if not beyond(k, 4, nb):
                            load(k + 4, q)
                    for k in range(4):
                        load(k, k)
                    sweep(sp, nb, body, 4)
                    for q in range(4):
                        sp.wait_ge(e_st[q], 4 * (k0 + nb))

                @block.tensor
                def _(pe):
                    def transpose_x(k, q):
                        pe.wait_ge(e_x[q], 4 * (k0 + k - q) + 16)
                        if started(k, 2):
                            pe.wait_ge(e_xT, k0 + k - 1)
                        nc.tensor.transpose(pX[q % 2][:], xb[:, q, :], ident[:]).then_inc(e_xp, 1)

                    def up(k, q):
                        e = expert_of(pe, k)
                        pe.wait_ge(e_xT, k0 + k + 1)
                        if started(k, 2):
                            pe.wait_ge(e_hb, k0 + k - 1)
                        nc.tensor.matmul(pU[q % 2][:].unsqueeze(1), xT[:, q % 2, :], w1T[:, bass.ds(e, 1), :],
                                         start=True, stop=True).then_inc(e_u, 1)

                    def transpose_h(k, q):
                        pe.wait_ge(e_hb, k0 + k + 1)
                        if started(k, 2):
                            pe.wait_ge(e_hT, k0 + k - 1)
                        for c in range(HC):
                            ins = nc.tensor.transpose(pT[q % 2][:, c, :], hb[:, q % 2, c * P:(c + 1) * P],
                                                      ident[:])
                        ins.then_inc(e_hp, 1)

                    def down(k, q):
                        e = expert_of(pe, k)
                        pe.wait_ge(e_hT, k0 + k + 1)
                        if started(k, 2):
                            pe.wait_ge(e_yb, k0 + k - 1)
                        for c in range(HC):
                            ins = nc.tensor.matmul(pY[q % 2][:].unsqueeze(1), hT[:, q % 2, c, :],
                                                   w2T[:, bass.ds(e, 1), c, :],
                                                   start=(c == 0), stop=(c == HC - 1))
                        ins.then_inc(e_y, 1)

                    def body(k, q):
                        transpose_h(k, q)
                        if not beyond(k, 1, nb):
                            up(k + 1, (q + 1) % 4)
                        down(k, q)
                        if not beyond(k, 2, nb):
                            transpose_x(k + 2, (q + 2) % 4)
                    transpose_x(0, 0)
                    transpose_x(1, 1)
                    up(0, 0)
                    sweep(pe, nb, body, 4)

                @block.scalar
                def _(act):
                    def copy_x(k, q):
                        act.wait_ge(e_xp, k0 + k + 1)
                        if started(k, 2):
                            act.wait_ge(e_u, k0 + k - 1)
                        act.copy(xT[:, q % 2, :], pX[q % 2][:]).then_inc(e_xT, 1)

                    def silu(k, q):
                        act.wait_ge(e_u, k0 + k + 1)
                        if started(k, 2):
                            act.wait_ge(e_hp, k0 + k - 1)
                        act.activation(hb[:, q % 2, :], pU[q % 2][:], ACT.Silu).then_inc(e_hb, 1)

                    def relu(k, q):
                        act.wait_ge(e_hp, k0 + k + 1)
                        if started(k, 2):
                            act.wait_ge(e_y, k0 + k - 1)
                        act.activation(hT[:, q % 2, :, :], pT[q % 2][:], ACT.Relu).then_inc(e_hT, 1)

                    def body(k, q):
                        if layer == 0:
                            relu(k, q)
                        elif not beyond(k, 1, nb):
                            silu(k + 1, (q + 1) % 4)
                        if not beyond(k, 2, nb):
                            copy_x(k + 2, (q + 2) % 4)
                    copy_x(0, 0)
                    copy_x(1, 1)
                    if layer == 1:
                        silu(0, 0)
                    sweep(act, nb, body, 4)

                @block.vector
                def _(dve):
                    def add_b1(k, q):
                        e = expert_of(dve, k)
                        dve.wait_ge(e_u, k0 + k + 1)
                        if started(k, 2):
                            dve.wait_ge(e_hp, k0 + k - 1)
                        dve.tensor_tensor(hb[:, q % 2, :].unsqueeze(1), pU[q % 2][:].unsqueeze(1),
                                          b1x[:, bass.ds(e, 1), :], ALU.add).then_inc(e_hb, 1)

                    def copy_h(k, q):
                        dve.wait_ge(e_hp, k0 + k + 1)
                        if started(k, 2):
                            dve.wait_ge(e_y, k0 + k - 1)
                        dve.tensor_copy(hT[:, q % 2, :, :], pT[q % 2][:]).then_inc(e_hT, 1)

                    def finish(k, q):
                        if layer == 0:
                            e = expert_of(dve, k)
                        dve.wait_ge(e_y, k0 + k + 1)
                        if started(k, 4):
                            dve.wait_ge(e_st[q], 4 * (k0 + k - q))
                        if layer == 0:
                            ins = dve.tensor_tensor(yb[:, q, :].unsqueeze(1), pY[q % 2][:].unsqueeze(1),
                                                    b2x[:, bass.ds(e, 1), :], ALU.add)
                        else:
                            ins = dve.tensor_copy(yb[:, q, :], pY[q % 2][:])
                        ins.then_inc(e_yb, 1)

                    def body(k, q):
                        if layer == 1:
                            copy_h(k, q)
                        elif not beyond(k, 1, nb):
                            add_b1(k + 1, (q + 1) % 4)
                        finish(k, q)
                    if layer == 0:
                        add_b1(0, 0)
                    sweep(dve, nb, body, 4)

        experts("x0", 0, xs0_d, ys0_d, eb0, NB0, 0)

        with ExitStack() as ph:
            idx = sb("d_idx", [P, 2, SUB], U32, ph)
            oT = sb("d_oT", [P, 2, TT], F32, ph)
            ye = sb("d_ye", [P, 2, SUB, D], F32, ph)
            acc = sb("d_acc", [P, 4, SUB, D], F32, ph)
            xn = sb("d_xn", [P, 2, SUB, D], F32, ph)
            xnT = sb("d_xnT", [P, 2, TT], F32, ph)
            st = sb("d_st", [P, SUB, 6], F32, ph)
            mv = sb("d_mv", [P, SUB, 2], F32, ph)
            rs = sb("d_rs", [P, SUB], F32, ph)
            st2 = sb("d_st2", [P, SUB, 6], F32, ph)
            mv2 = sb("d_mv2", [P, SUB, 2], F32, ph)
            rs2 = sb("d_rs2", [P, SUB], F32, ph)
            qkT = sb("d_qkT", [P, 2, TT], F32, ph)
            v = sb("d_v", [P, SUB, D], F32, ph)
            sm = sb("d_sm", [P, 2, 3, P], F32, ph)
            o = sb("d_o", [P, SUB, D], F32, ph)
            hT = sb("d_hT", [P, HC, TT], F32, ph)
            pC = pb("d_pC", [P, SUB, D], ph)
            pL = pb("d_pL", [P, SUB, E], ph)
            pH = pb("d_pH", [P, 2, TT], ph)
            pM = pb("d_pM", [P, 2, TT], ph)
            pV = pb("d_pV", [P, SUB, D], ph)
            pY = pb("d_pY", [P, SUB, D], ph)

            d_x = [sem(f"d_x{i}") for i in range(4)]
            d_agg = sem("d_agg")
            d_agg2 = sem("d_agg2")
            d_st2 = sem("d_st2s")
            d_idx = sem("d_idx_s")
            d_g = [sem("d_g0"), sem("d_g1")]
            d_wo = sem("d_wo")
            d_sum = sem("d_sum")
            d_x1 = sem("d_x1s")
            d_st = sem("d_sts")
            d_ve = sem("d_ve")
            d_rs = sem("d_rss")
            d_xn = sem("d_xns")
            d_xnd = [sem("d_xnd0"), sem("d_xnd1")]
            d_tr = sem("d_tr")
            d_xT = sem("d_xTs")
            d_lg = sem("d_lg")
            d_lgs = sem("d_lgs")
            d_up = sem("d_up")
            d_h = sem("d_h")
            d_y = sem("d_y")
            d_qk = sem("d_qk")
            d_qks = sem("d_qks")
            d_v = sem("d_vp")
            d_vs = sem("d_vs")
            d_s = sem("d_s")
            d_sm = sem("d_sms")
            d_o = sem("d_op")
            d_os = sem("d_os")
            d_ve2 = sem("d_ve2")
            d_rs2 = sem("d_rs2s")
            d_ln = sem("d_ln")
            d_ys = sem("d_ys")
            d_acc = sem("d_accs")
            d_x2 = [sem(f"d_x2{i}") for i in range(4)]
            WS = 2 * E
            LINKS = 3

            block = ph.enter_context(nc.Block())

            @block.sync
            def _(sp):
                def body(t, q):
                    if started(t, 4):
                        sp.wait_ge(d_x2[q], 4 * (t - q))
                        settle(sp, settled)
                    if started(t, 2):
                        sp.wait_ge(d_wo, t - 1)
                        settle(sp, settled)
                    sp.dma_start(oT[:, q % 2, :], oT_d[:, bass.ds(t * TT, TT)]).then_inc(d_x[q], 16)
                    sp.dma_start(acc[:, q, :, :], x_v[:, bass.ds(t * SUB, SUB), :]).then_inc(d_x[q], 16)
                sweep(sp, NT, body, 4)

            @block.tensor
            def _(pe):
                def project(t, q):
                    s = q % 2
                    pe.wait_ge(d_x[q], 8 * (t - q) + 32)
                    if started(t, 1):
                        pe.wait_ge(d_xT, t)
                    for j in range(SUB):
                        ins = nc.tensor.matmul(pC[:, j, :], oT[:, s, j * P:(j + 1) * P], wT[:, 3, :],
                                               start=True, stop=True)
                    ins.then_inc(d_wo, 1)

                def transpose(t, s):
                    pe.wait_ge(d_xn, t + 1)
                    for j in range(SUB):
                        ins = nc.tensor.transpose(pC[:, j, :], xn[:, s, j, :], ident[:])
                    ins.then_inc(d_tr, 1)

                def logits(t, s):
                    pe.wait_ge(d_xT, t + 1)
                    if started(t, 1):
                        pe.wait_ge(d_lgs, t)
                    for j in range(SUB):
                        ins = nc.tensor.matmul(pL[:, j, :], xnT[:, s, j * P:(j + 1) * P], g1T[:],
                                               start=True, stop=True)
                    ins.then_inc(d_lg, 1)

                def up(t, s, c):
                    if c >= 2:
                        pe.wait_ge(d_h, HC * t + c - 1)
                    elif started(t, 1):
                        pe.wait_ge(d_h, HC * t)
                    nc.tensor.matmul(pH[:, c % 2, :], w1T[:, WS, c * P:(c + 1) * P], xnT[:, s, :],
                                     start=True, stop=True).then_inc(d_up, 1)

                def body(t, q):
                    s = q % 2
                    if not is_last(t, NT):
                        project(t + 1, (q + 1) % 4)
                    up(t, s, 0)
                    up(t, s, 1)
                    if started(t, 1):
                        pe.wait_ge(d_os, t)
                    for n in range(2):
                        nc.tensor.matmul(pM[:, n, :], wqkv[:, n * D:(n + 1) * D], xnT[:, s, :],
                                         start=True, stop=True).then_inc(d_qk, 1)
                    up(t, s, 2)
                    up(t, s, 3)
                    if started(t, 1):
                        pe.wait_ge(d_vs, t)
                    for j in range(SUB):
                        ins = nc.tensor.matmul(pV[:, j, :], xnT[:, s, j * P:(j + 1) * P],
                                               wqkv[:, 2 * D:3 * D], start=True, stop=True)
                    ins.then_inc(d_v, 1)
                    pe.wait_ge(d_qks, 2 * t + 2)
                    for b in range(2):
                        for n, (key, query) in enumerate(((0, 0), (1, 1), (0, 1))):
                            ins = nc.tensor.matmul(pM[:, b, n * P:(n + 1) * P],
                                                   qkT[:, 1, (2 * b + key) * P:(2 * b + key + 1) * P],
                                                   qkT[:, 0, (2 * b + query) * P:(2 * b + query + 1) * P],
                                                   start=True, stop=True)
                        ins.then_inc(d_s, 1)
                    pe.wait_ge(d_h, HC * (t + 1))
                    if started(t, 1):
                        pe.wait_ge(d_ys, t)
                    for j in range(SUB):
                        for c in range(HC):
                            ins = nc.tensor.matmul(pY[:, j, :], hT[:, c, j * P:(j + 1) * P],
                                                   w2T[:, WS, c, :], start=(c == 0), stop=(c == HC - 1))
                    ins.then_inc(d_y, 1)
                    if not is_last(t, NT):
                        transpose(t + 1, 1 - s)
                    pe.wait_ge(d_sm, 4 * t + 4)
                    for b in range(2):
                        nc.tensor.matmul(pM[:, 0, 2 * b * P:(2 * b + 1) * P], sm[:, b, 0, :],
                                         v[:, 2 * b, :], start=True, stop=True)
                        nc.tensor.matmul(pM[:, 0, (2 * b + 1) * P:(2 * b + 2) * P], sm[:, b, 1, :],
                                         v[:, 2 * b + 1, :], start=True, stop=False)
                        ins = nc.tensor.matmul(pM[:, 0, (2 * b + 1) * P:(2 * b + 2) * P], sm[:, b, 2, :],
                                               v[:, 2 * b, :], start=False, stop=True)
                    ins.then_inc(d_o, 1)
                    if not is_last(t, NT):
                        logits(t + 1, 1 - s)
                project(0, 0)
                transpose(0, 0)
                logits(0, 0)
                sweep(pe, NT, body, 4)

            @block.scalar
            def _(act):
                def copy_xT(t, s):
                    act.wait_ge(d_tr, t + 1)
                    if started(t, 2):
                        act.wait_ge(d_v, t - 1)
                        act.wait_ge(d_lg, t - 1)
                    act.copy(xnT[:, s, :], pC[:].rearrange("p j n -> p (j n)")).then_inc(d_xT, 1)

                def silu(t, c):
                    if started(t, 1) and c == 0:
                        act.wait_ge(d_y, t)
                    act.wait_ge(d_up, HC * t + c + 1)
                    act.activation(hT[:, c, :], pH[:, c % 2, :], ACT.Silu).then_inc(d_h, 1)

                def body(t, s):
                    silu(t, 0)
                    silu(t, 1)
                    if started(t, 1):
                        act.wait_ge(d_s, 2 * t)
                    for i in range(2):
                        act.wait_ge(d_qk, 2 * t + i + 1)
                        act.activation(qkT[:, i, :], pM[:, i, :], ACT.Identity,
                                       bias=bqk1[:, i:i + 1]).then_inc(d_qks, 1)
                    silu(t, 2)
                    silu(t, 3)
                    if not is_last(t, NT):
                        copy_xT(t + 1, 1 - s)
                copy_xT(0, 0)
                sweep(act, NT, lambda t, q: body(t, q % 2), 4)

            @block.vector
            def _(dve):
                def index(t, s):
                    if started(t, 2):
                        dve.wait_ge(d_g[s], 32 * (t - s))
                    dve.tensor_copy(idx[:, s, :], row0[:, bass.ds(t * SUB, SUB)]).then_inc(d_idx, 1)

                def first_sum(t, q):
                    s = q % 2
                    dve.wait_ge(d_x[q], 8 * (t - q) + 32)
                    dve.wait_ge(d_g[s], 32 * (t - s) + 64)
                    dve.tensor_tensor(acc[:, q, :, :], acc[:, q, :, :], ye[:, s, :, :], ALU.add).then_inc(d_sum, 1)
                    dve.wait_ge(d_wo, t + 1)
                    dve.wait_ge(d_sum, t + 1)
                    dve.tensor_tensor(acc[:, q, :, :], pC[:], acc[:, q, :, :], ALU.add).then_inc(d_x1, 1)
                    dve.wait_ge(d_x1, t + 1)
                    row_statistics(dve, st[:], mv[:], acc[:, q, :, :], d_st, t, settled).then_inc(d_agg, 1)

                def norm(t, q):
                    s = q % 2
                    dve.wait_ge(d_rs, t + 1)
                    if started(t, 2):
                        dve.wait_ge(d_tr, t - 1)
                        dve.wait_ge(d_xnd[s], 8 * (t - s))
                    for j in range(SUB):
                        ins = dve.tensor_scalar(xn[:, s, j, :], acc[:, q, j, :], mv[:, j, 0:1], rs[:, j:j + 1],
                                                ALU.subtract, ALU.mult)
                    ins.then_inc(d_xn, 1)

                def keep_logits(t):
                    dve.wait_ge(d_lg, t + 1)
                    dve.tensor_copy(G1[:, bass.ds(t * SUB, SUB), :], pL[:]).then_inc(d_lgs, 1)

                def finish(t, q):
                    link = chain(dve, d_ln, t * LINKS)
                    dve.wait_ge(d_rs2, t + 1)
                    for j in range(SUB):
                        ins = dve.tensor_scalar(o[:, j, :], o[:, j, :], mv2[:, j, 0:1], rs2[:, j:j + 1],
                                                ALU.subtract, ALU.mult)
                    link(ins)
                    link(dve.tensor_tensor(o[:], o[:], lnw[:].unsqueeze(1).broadcast_to([P, SUB, D]), ALU.mult))
                    link(dve.tensor_tensor(o[:], o[:], lnb[:].unsqueeze(1).broadcast_to([P, SUB, D]), ALU.add))
                    dve.wait_ge(d_ys, t + 1)
                    dve.tensor_tensor(acc[:, q, :, :], acc[:, q, :, :], o[:], ALU.add).then_inc(d_acc, 1)

                def body(t, q):
                    s = q % 2
                    if not beyond(t, 2, NT):
                        index(t + 2, s)
                    if not is_last(t, NT):
                        first_sum(t + 1, (q + 1) % 4)
                    if started(t, 1):
                        finish(t - 1, (q + 3) % 4)
                    if not is_last(t, NT):
                        norm(t + 1, (q + 1) % 4)
                    dve.wait_ge(d_v, t + 1)
                    if started(t, 1):
                        dve.wait_ge(d_o, t)
                    dve.tensor_tensor(v[:], pV[:], bv1[:].unsqueeze(1).broadcast_to([P, SUB, D]),
                                      ALU.add).then_inc(d_vs, 1)
                    for b in range(2):
                        dve.wait_ge(d_s, 2 * t + b + 1)
                        sc = pM[:, b, :].rearrange("p (n q) -> p n q", q=P)
                        dve.scalar_tensor_tensor(
                            sm[:, b, 0:2, :], sc[:, 0:2, :], SCALE1,
                            mdiag[:].unsqueeze(1).broadcast_to([P, 2, P]),
                            ALU.mult, ALU.mult).then_inc(d_sm, 1)
                        dve.scalar_tensor_tensor(sm[:, b, 2, :], sc[:, 2, :], SCALE1, mcross[:],
                                                 ALU.mult, ALU.mult).then_inc(d_sm, 1)
                    dve.wait_ge(d_y, t + 1)
                    dve.tensor_tensor(acc[:, q, :, :], pY[:], acc[:, q, :, :], ALU.add).then_inc(d_ys, 1)
                    dve.wait_ge(d_o, t + 1)
                    if started(t, 1):
                        dve.wait_ge(d_acc, t)
                    dve.tensor_copy(o[:], pM[:, 0, :].rearrange("p (j d) -> p j d", d=D)).then_inc(d_os, 1)
                    dve.wait_ge(d_os, t + 1)
                    row_statistics(dve, st2[:], mv2[:], o[:], d_st2, t, settled).then_inc(d_agg2, 1)
                    if not is_last(t, NT):
                        keep_logits(t + 1)

                index(0, 0)
                index(1, 1)
                first_sum(0, 0)
                norm(0, 0)
                keep_logits(0)
                sweep(dve, NT, body, 4)
                finish(NT - 1, 3)

            @block.gpsimd
            def _(pool):
                def gather(t, s):
                    pool.wait_ge(d_idx, t + 1)
                    if started(t, 2):
                        pool.wait_ge(d_sum, t - 1)
                    settle(pool, settled)
                    for j in range(SUB):
                        pool.indirect_dma_start(
                            out=ye[:, s, j, :], out_offset=None, in_=ys0_d,
                            in_offset=bass.IndirectOffsetOnAxis(idx[:, s, j:j + 1], 0)).then_inc(d_g[s], 16)

                def first_norm(t):
                    pool.wait_ge(d_agg, t + 1)
                    inverse_deviation(pool, mv[:], rs[:], eps, mhalf, d_ve, t).then_inc(d_rs, 1)

                def store_norm(t, s):
                    pool.wait_ge(d_xn, t + 1)
                    settle(pool, settled)
                    pool.dma_start(xn1_d[:, bass.ds(t * SUB, SUB), :], xn[:, s, :, :]).then_inc(d_xnd[s], 16)

                def store(t, q):
                    pool.wait_ge(d_acc, t + 1)
                    settle(pool, settled)
                    pool.dma_start(x2_d[:, bass.ds(t * SUB, SUB), :], acc[:, q, :, :]).then_inc(d_x2[q], 16)

                def body(t, q):
                    s = q % 2
                    if not is_last(t, NT):
                        first_norm(t + 1)
                    if not beyond(t, 2, NT):
                        gather(t + 2, s)
                    if started(t, 1):
                        store(t - 1, (q + 3) % 4)
                    if not is_last(t, NT):
                        store_norm(t + 1, 1 - s)
                    pool.wait_ge(d_agg2, t + 1)
                    inverse_deviation(pool, mv2[:], rs2[:], eps, mhalf, d_ve2, t).then_inc(d_rs2, 1)
                gather(0, 0)
                gather(1, 1)
                first_norm(0)
                store_norm(0, 0)
                sweep(pool, NT, body, 4)
                store(NT - 1, 3)
                for q in range(4):
                    pool.wait_ge(d_x2[q], 4 * NT)
                for s in range(2):
                    pool.wait_ge(d_xnd[s], 8 * NT)

        with ExitStack() as rs1:
            oh1 = sb("oh1", [P, NS, E], F32, rs1)
            oh2 = sb("oh2", [P, NS, E], F32, rs1)
            both = sb("both", [P, NS, E], F32, rs1)
            lg2 = sb("lg2", [P, NS, E], F32, rs1)
            m1 = sb("m1", [P, NS], F32, rs1)
            m2 = sb("m2", [P, NS], F32, rs1)
            c1 = sb("c1", [P, NS], F32, rs1)

            def two_largest(dve, link, top, ex):
                first_of_largest(dve, link, G1, oh1, m1, c1)
                link(dve.tensor_scalar(lg2[:], oh1[:], PRIO_NONE, None, ALU.mult))
                link(dve.tensor_tensor(lg2[:], lg2[:], G1[:], ALU.add))
                first_of_largest(dve, link, lg2, oh2, m2, c1)
                link(dve.tensor_tensor(both[:], oh1[:], oh2[:], ALU.add))
                dve.tensor_tensor(gate1[:, 0, :], m2[:], m1[:], ALU.subtract).then_inc(top, 1)
                dve.wait_ge(ex, 1)
                link(dve.tensor_scalar(c1[:], gate1[:, 1, :], 1.0, None, ALU.add))
                link(dve.reciprocal(gate1[:, 0, :], c1[:]))
                link(dve.tensor_tensor(gate1[:, 1, :], gate1[:, 1, :], gate1[:, 0, :], ALU.mult))
            route("r1", two_largest, [oh1, oh2, both], [row1[:, 0, :], row1[:, 1, :]], eb1, NB1, E)
        scatter("s1", xn1_d, [row1[:, 0, :], row1[:, 1, :]], xs1_d)
        experts("x1", 1, xs1_d, ys1_d, eb1, NB1, NB0)

        with ExitStack() as ph:
            idx = sb("f_idx", [P, 2, TOPK, SUB], U32, ph)
            gt = sb("f_gt", [P, 2, TOPK, SUB], F32, ph)
            ye = sb("f_ye", [P, 2, TOPK, SUB, D], F32, ph)
            acc = sb("f_acc", [P, 2, SUB, D], F32, ph)
            f_x = [sem("f_x0"), sem("f_x1")]
            f_i = sem("f_i")
            f_g = [sem("f_g0"), sem("f_g1")]
            f_1 = sem("f_1")
            f_2 = sem("f_2")
            f_out = [sem("f_out0"), sem("f_out1")]
            PER = 16 * TOPK * SUB

            block = ph.enter_context(nc.Block())

            @block.sync
            def _(sp):
                def body(t, s):
                    if started(t, 2):
                        sp.wait_ge(f_out[s], 8 * (t - s))
                    settle(sp, settled)
                    sp.dma_start(acc[:, s, :, :], x2_d[:, bass.ds(t * SUB, SUB), :]).then_inc(f_x[s], 16)
                sweep(sp, NT, body)

            @block.gpsimd
            def _(pool):
                def body(t, s):
                    pool.wait_ge(f_i, t + 1)
                    if started(t, 2):
                        pool.wait_ge(f_2, t - 1)
                    settle(pool, settled)
                    for i in range(TOPK):
                        for j in range(SUB):
                            pool.indirect_dma_start(
                                out=ye[:, s, i, j, :], out_offset=None, in_=ys1_d,
                                in_offset=bass.IndirectOffsetOnAxis(idx[:, s, i, j:j + 1], 0))\
                                .then_inc(f_g[s], 16)
                sweep(pool, NT, body)

            @block.vector
            def _(dve):
                def index(t, s):
                    if started(t, 2):
                        dve.wait_ge(f_g[s], (t - s) * (PER // 2))
                        dve.wait_ge(f_2, t - 1)
                    for i in range(TOPK):
                        dve.tensor_copy(idx[:, s, i, :], row1[:, i, bass.ds(t * SUB, SUB)])
                        ins = dve.tensor_copy(gt[:, s, i, :], gate1[:, i, bass.ds(t * SUB, SUB)])
                    ins.then_inc(f_i, 1)

                def body(t, s):
                    dve.wait_ge(f_i, t + 1)
                    dve.wait_ge(f_x[s], 8 * (t - s) + 16)
                    dve.wait_ge(f_g[s], (t - s) * (PER // 2) + PER)
                    for i, done in enumerate((f_1, f_2)):
                        for j in range(SUB):
                            ins = dve.scalar_tensor_tensor(acc[:, s, j, :], ye[:, s, i, j, :],
                                                           gt[:, s, i, j:j + 1], acc[:, s, j, :],
                                                           ALU.mult, ALU.add)
                        ins.then_inc(done, 1)
                        if i == 0:
                            dve.wait_ge(f_1, t + 1)
                    if not beyond(t, 2, NT):
                        index(t + 2, s)
                index(0, 0)
                index(1, 1)
                sweep(dve, NT, body)

            @block.scalar
            def _(act):
                def body(t, s):
                    act.wait_ge(f_2, t + 1)
                    act.dma_start(out_v[:, bass.ds(t * SUB, SUB), :], acc[:, s, :, :]).then_inc(f_out[s], 16)
                sweep(act, NT, body)
                for s in range(2):
                    act.wait_ge(f_out[s], 8 * NT)


_INS = ['L0_attn_x', 'L0_attn_Wq', 'L0_attn_bq', 'L0_attn_Wk', 'L0_attn_bk', 'L0_attn_Wv', 'L0_attn_bv',
        'L0_attn_Wo', 'L0_attn_bo', 'L0_ffn_gate_w', 'L0_ffn_gate_b', 'L0_ffn_w1', 'L0_ffn_b1', 'L0_ffn_w2',
        'L0_ffn_b2', 'L1_attn_W_qkv', 'L1_attn_b_qkv', 'L1_attn_ln_w', 'L1_attn_ln_b', 'L1_ffn_shared_w1',
        'L1_ffn_shared_w2', 'L1_ffn_experts_w1', 'L1_ffn_experts_w2', 'L1_ffn_gate_w']


def kernel(**inputs):
    import numpy as _np
    import concourse.bacc as _bacc
    from concourse import mybir as _mybir
    from concourse.bass_utils import run_bass_kernel_spmd as _run

    nc = _bacc.Bacc("TRN2", target_bir_lowering=False, num_devices=1)
    arrays, args = {}, []
    for name in _INS:
        a = _np.ascontiguousarray(inputs[name])
        arrays[f"in_{name}_dram"] = a
        args.append(nc.dram_tensor(f"in_{name}_dram", a.shape, _mybir.dt.from_np(a.dtype),
                                   kind="ExternalInput").ap())
    args.append(nc.dram_tensor("out_0_dram", (B, S, D), _mybir.dt.float32, kind="ExternalOutput").ap())
    layer_kernel(nc, *args)
    r = _run(nc, [arrays], core_ids=[0])
    return r.results[0]["out_0_dram"]
```

```python
import concourse.bass as bass
from concourse import mybir
from contextlib import ExitStack

F32 = mybir.dt.float32
BF16 = mybir.dt.bfloat16
U32 = mybir.dt.uint32
I32 = mybir.dt.int32
ALU = mybir.AluOpType
ACT = mybir.ActivationFunctionType
AX = mybir.AxisListType

P = 128
B, S, D = 32, 256, 128
T = B * S
TT = 512
NT = T // TT
SUB = TT // P
NS = T // P
H = 16
DK = D // H
E = 8
HID = 512
HC = HID // P
EPS = 1e-5
SPAN = 32
SCALE1 = 1.0 / float((D * SPAN) ** 0.5)
NPART = 3
KROWS = NPART * NPART * DK
BG = 4
NBG = B // BG
PRIO_NONE = -3.0e38
TOPK = 2
DR = D + 1
REG = T + P
RND = 8
NB0 = -(-(NS + E - 1) // RND) * RND
NB1 = -(-(TOPK * NS + E - 1) // RND) * RND
SPARE = max(NB0 - NS, NB1 - TOPK * NS)


def sweep(eng, n, body, unroll=2):
    assert n % unroll == 0 and n // unroll > 2
    for t in range(unroll):
        body(t, t)
    with eng.Fori(1, n // unroll - 1) as i:
        for k in range(unroll):
            body(unroll * i + k, k)
    for t in range(n - unroll, n):
        body(t, t % unroll)


def is_last(t, n):
    return isinstance(t, int) and t == n - 1


def beyond(t, ahead, n):
    return isinstance(t, int) and t + ahead >= n


def started(t, k):
    return not isinstance(t, int) or t >= k


def chain(eng, sem, base):
    state = [0]

    def link(ins):
        state[0] += 1
        ins.then_inc(sem, 1)
        eng.wait_ge(sem, base + state[0])
    return link


def settle(eng, settled):
    eng.sem_inc(settled, 1)


def row_statistics(dve, st, mv, rows, stats_done, count, settled):
    for j in range(SUB):
        ins = dve.bn_stats(st[:, j, :], rows[:, j, :])
    ins.then_inc(stats_done, 1)
    dve.wait_ge(stats_done, count + 1)
    settle(dve, settled)
    for j in range(SUB):
        ins = dve.bn_aggr(mv[:, j, :], st[:, j, :])
    return ins


def inverse_deviation(pool, mv, rstd, eps, mhalf, added, count):
    pool.tensor_tensor(rstd, mv[:, :, 1], eps[:], ALU.add).then_inc(added, 1)
    pool.wait_ge(added, count + 1)
    return pool.tensor_tensor(rstd, rstd, mhalf[:], ALU.pow)


def layer_kernel(nc, x, Wq, bq, Wk, bk, Wv, bv, Wo, bo, gate0_w, gate0_b, w1_0, b1_0, w2_0, b2_0,
                 W_qkv, b_qkv, ln_w, ln_b, sh_w1, sh_w2, w1_1, w2_1, gate1_w, out):
    x_v = x.rearrange("b (u p) d -> p (b u) d", p=P)
    out_v = out.rearrange("b (u p) d -> p (b u) d", p=P)

    xn0_d = nc.dram_tensor("xn0_d", [P, NS, DR], F32).ap()
    qs_d = nc.dram_tensor("qs_d", [NPART, D, T], BF16).ap()
    ks_d = nc.dram_tensor("ks_d", [NPART, D, T], BF16).ap()
    oT_d = nc.dram_tensor("oT_d", [D, T], F32).ap()
    x2_d = nc.dram_tensor("x2_d", [P, NS, D], F32).ap()
    xs0_d = nc.dram_tensor("xs0_d", [E * REG + SPARE * P, DR], F32).ap()
    xs1_d = nc.dram_tensor("xs1_d", [E * REG + SPARE * P, DR], F32).ap()
    y0_d = nc.dram_tensor("y0_d", [T + (E + SPARE) * P, D], F32).ap()
    y1_d = nc.dram_tensor("y1_d", [TOPK * T + (E + SPARE) * P, D], F32).ap()
    y0_v = y0_d[0:T, :].rearrange("(p n) d -> p n d", p=P)
    y1_v = y1_d[0:TOPK * T, :].rearrange("(p n i) d -> p n i d", p=P, i=TOPK)

    ctx = ExitStack()
    with ctx:
        def sb(name, shape, dt=F32, c=ctx):
            return c.enter_context(nc.sbuf_tensor(name, shape, dt))

        def pb(name, shape, c, dt=F32):
            return c.enter_context(nc.psum_tensor(name, shape, dt))

        def sem(name):
            return ctx.enter_context(nc.semaphore(name))

        settled = sem("settled")
        ident = sb("ident", [P, P])
        identb = sb("identb", [P, P], BF16)
        wT = sb("wT", [P, 4, P])
        g0T = sb("g0T", [P, E])
        g1T = sb("g1T", [P, E])
        bqc = sb("bqc", [P, 1])
        bkc = sb("bkc", [P, 1])
        bv_bc = sb("bv_bc", [P, D])
        gb_bc = sb("gb_bc", [P, E])
        prio = sb("prio", [P, E])
        eps = sb("eps", [P, SUB])
        mhalf = sb("mhalf", [P, SUB])
        below = sb("below", [P, P])
        ones = sb("ones", [P, P])
        thr = sb("thr", [P, E, NS * TOPK])
        blk = sb("blk", [P, NB1, E])
        row0 = sb("row0", [P, NS], U32)
        dest0 = sb("dest0", [P, NS], U32)
        dest1 = sb("dest1", [P, TOPK, NS], U32)
        region = sb("region", [P, E])
        rows0 = sb("rows0", [P, E])
        rows1 = sb("rows1", [P, E])
        top1 = sb("top1", [P, TOPK, NS])
        eb0 = sb("eb0", [P, NB0 + RND], I32)
        eb1 = sb("eb1", [P, NB1 + RND], I32)
        bs0 = sb("bs0", [P, NB0], I32)
        bs1 = sb("bs1", [P, NB1], I32)
        vstack = ExitStack()
        V = sb("V", [P, NS, D], F32, vstack)

        class Routing:
            pass

        def routing_tiles(pre, stack, top):
            r = Routing()
            r.lg = sb(pre + "_lg", [P, SUB, E], F32, stack)
            r.oh = [sb(f"{pre}_oh{i}", [P, SUB, E], F32, stack) for i in range(top)]
            r.hit = sb(pre + "_hit", [P, SUB, E], F32, stack) if top > 1 else r.oh[0]
            r.lg2 = sb(pre + "_lg2", [P, SUB, E], F32, stack) if top > 1 else None
            r.m = [sb(f"{pre}_m{i}", [P, SUB], F32, stack) for i in range(top)]
            r.c = [sb(f"{pre}_c{i}", [P, SUB], F32, stack) for i in range(top)]
            r.rowf = sb(pre + "_rowf", [P, SUB], F32, stack)
            r.rk = sb(pre + "_rk", [P, SUB, E], F32, stack)
            r.pick = sb(pre + "_pick", [P, SUB, E], F32, stack)
            return r

        def first_of_largest(dve, link, lg, oh, m, c, n):
            link(dve.tensor_reduce(m, lg[:], AX.X, ALU.max))
            link(dve.tensor_tensor(oh[:], lg[:], m.unsqueeze(2).broadcast_to([P, n, E]), ALU.is_equal))
            link(dve.tensor_tensor(oh[:], oh[:], prio[:].unsqueeze(1).broadcast_to([P, n, E]), ALU.mult))
            link(dve.tensor_reduce(c[:], oh[:], AX.X, ALU.max))
            link(dve.tensor_tensor(oh[:], oh[:], c[:].unsqueeze(2).broadcast_to([P, n, E]), ALU.is_equal))

        def count_rows(pe, hit_done, counted, routed, links, t, rt, pG):
            pe.wait_ge(hit_done, t + 1)
            if started(t, 1):
                pe.wait_ge(routed, links * t)
            hit = rt.hit[:].rearrange("p n e -> p (n e)")
            nc.tensor.matmul(pG[:, 0, 0, :], below[:], hit, start=True, stop=True)
            nc.tensor.matmul(pG[:, 1, 0, :], ones[:], hit, start=True, stop=True).then_inc(counted, 1)

        def assign_rows(dve, link, rt, pG, free, rows):
            for j in range(SUB):
                link(dve.tensor_copy(rt.rk[:, j, :], free[:]))
                link(dve.tensor_tensor(free[:], free[:], pG[:, 1, 0, j * E:(j + 1) * E], ALU.add))
            link(dve.tensor_tensor(rt.rk[:], rt.rk[:], pG[:, 0, 0, :].rearrange("p (n e) -> p n e", e=E), ALU.add))
            for oh, row in zip(rt.oh, rows):
                link(dve.tensor_tensor(rt.pick[:], oh[:], rt.rk[:], ALU.mult))
                link(dve.tensor_reduce(rt.rowf[:], rt.pick[:], AX.X, ALU.add))
                link(dve.tensor_copy(row, rt.rowf[:]))

        LINKS0 = 5 + 2 * SUB + 1 + 3

        with ExitStack() as ph:
            wload = sb("wload", [P, 4, P], F32, ph)
            gload = sb("gload", [E, 2, P], F32, ph)
            xt = sb("xt", [P, 4, SUB, D], F32, ph)
            xn = sb("xn", [P, 2, SUB, DR], F32, ph)
            rt = routing_tiles("a", ph, 1)
            xnT = sb("xnT", [P, 2, TT], F32, ph)
            st = sb("st", [P, 2, SUB, 6], F32, ph)
            mv = sb("mv", [P, 2, SUB, 2], F32, ph)
            rs = sb("rs", [P, 2, SUB], F32, ph)
            qf = sb("qf", [P, 2, TT], F32, ph)
            rem = sb("rem", [P, 2, TT], F32, ph)
            parts = sb("parts", [P, 2, 2, NPART, TT], BF16, ph)
            pX = pb("pX", [P, TT], ph)
            pQ = pb("pQ", [P, TT], ph)
            pK = pb("pK", [P, TT], ph)
            pV = pb("pV", [P, SUB, D], ph)
            pL = pb("pL", [P, SUB, E], ph)
            pW = pb("pW", [P, 4, P], ph)
            pG = pb("pG", [P, 2, 2, SUB * E], ph)

            a_w = sem("a_w")
            a_const = sem("a_const")
            a_wT = sem("a_wT")
            a_wTs = sem("a_wTs")
            a_x = [sem(f"a_x{i}") for i in range(4)]
            a_agg = sem("a_agg")
            a_st = sem("a_st")
            a_ve = sem("a_ve")
            a_rs = sem("a_rs")
            a_xn = sem("a_xn")
            a_tr = sem("a_tr")
            a_xT = sem("a_xT")
            a_xnd = [sem("a_xnd0"), sem("a_xnd1")]
            a_dest = sem("a_dest")
            a_hit = sem("a_hit")
            a_cnt = sem("a_cnt")
            a_route = sem("a_route")
            a_q = sem("a_q")
            a_v = sem("a_v")
            a_qf = sem("a_qf")
            a_mid = sem("a_mid")
            a_rem = sem("a_rem")
            a_low = sem("a_low")
            a_vs = sem("a_vs")
            a_pd = [sem("a_pd0"), sem("a_pd1")]
            WLOADS = 10

            block = ph.enter_context(nc.Block())

            @block.sync
            def _(sp):
                for n, w in enumerate((Wq, Wk, Wv, Wo)):
                    sp.dma_start(wload[:, n, :], w).then_inc(a_w, 16)
                sp.dma_start(gload[:, 0, :], gate0_w).then_inc(a_w, 16)
                sp.dma_start(gload[:, 1, :], gate1_w).then_inc(a_w, 16)
                sp.dma_start(bqc[:], bq.rearrange("(p a) -> p a", a=1)).then_inc(a_w, 16)
                sp.dma_start(bkc[:], bk.rearrange("(p a) -> p a", a=1)).then_inc(a_w, 16)
                sp.dma_start(bv_bc[:], bv.partition_broadcast(P)).then_inc(a_w, 16)
                sp.dma_start(gb_bc[:], gate0_b.partition_broadcast(P)).then_inc(a_w, 16)

                def store_norm(t, s):
                    sp.dma_start(xn0_d[:, bass.ds(t * SUB, SUB), :], xn[:, s, :, :]).then_inc(a_xnd[s], 16)

                def body(t, q):
                    if started(t, 4):
                        sp.wait_ge(a_xn, t - 3)
                        settle(sp, settled)
                    sp.dma_start(xt[:, q, :, :], x_v[:, bass.ds(t * SUB, SUB), :]).then_inc(a_x[q], 16)
                    if started(t, 4):
                        store_norm(t - 4, q % 2)
                sweep(sp, NT, body, 4)
                for t in range(NT - 4, NT):
                    sp.wait_ge(a_xn, t + 1)
                    store_norm(t, t % 2)

            @block.gpsimd
            def _(pool):
                pool.memset(ones[:], 1.0).then_inc(a_const, 1)
                pool.memset(ident[:], 0.0).then_inc(a_const, 1)
                pool.memset(identb[:], 0.0).then_inc(a_const, 1)
                for c, value in ((eps, EPS), (mhalf, -0.5)):
                    pool.memset(c[:], value).then_inc(a_const, 1)
                for e in range(E):
                    pool.memset(prio[:, e:e + 1], float(E - e)).then_inc(a_const, 1)
                pool.wait_ge(a_const, 5 + E)
                for m in (ident, identb):
                    pool.affine_select(out=m[:], in_=m[:], compare_op=ALU.not_equal, fill=1.0, base=0,
                                       pattern=[[-1, P]], channel_multiplier=1).then_inc(a_const, 1)
                pool.memset(below[:], 1.0).then_inc(a_const, 1)
                pool.wait_ge(a_const, 8 + E)
                pool.affine_select(out=below[:], in_=below[:], compare_op=ALU.is_gt, fill=0.0, base=0,
                                   pattern=[[1, P]], channel_multiplier=-1)
                pool.iota(thr[:], [[0, E], [P, NS * TOPK]], base=0, channel_multiplier=0,
                          allow_small_or_imprecise_dtypes=True)
                pool.iota(blk[:], [[1, NB1], [0, E]], base=0, channel_multiplier=0,
                          allow_small_or_imprecise_dtypes=True)
                pool.iota(dest0[:], [[1, NS]], base=0, channel_multiplier=NS)
                for i in range(TOPK):
                    pool.iota(dest1[:, i, :], [[TOPK, NS]], base=i, channel_multiplier=TOPK * NS)
                for n in (region, rows0, rows1):
                    ins = pool.iota(n[:], [[REG, E]], base=0, channel_multiplier=0,
                                    allow_small_or_imprecise_dtypes=True)
                ins.then_inc(a_dest, 1)

                def deviation(t, s):
                    pool.wait_ge(a_agg, t + 1)
                    if started(t, 2):
                        pool.wait_ge(a_xn, t - 1)
                    inverse_deviation(pool, mv[:, s, :, :], rs[:, s, :], eps, mhalf, a_ve, t).then_inc(a_rs, 1)

                def third_part(t, s, n):
                    pool.wait_ge(a_qf, 4 * t + 2 * n + 2)
                    if started(t, 1):
                        pool.wait_ge(a_low, 2 * t + n)
                    pool.tensor_tensor(rem[:, n, :], qf[:, n, :], parts[:, s, n, 0, :],
                                       ALU.subtract).then_inc(a_rem, 1)
                    pool.wait_ge(a_rem, 2 * t + n + 1)
                    pool.wait_ge(a_mid, 2 * t + n + 1)
                    pool.tensor_tensor(parts[:, s, n, 2, :], rem[:, n, :], parts[:, s, n, 1, :],
                                       ALU.subtract).then_inc(a_low, 1)

                def body(t, s):
                    third_part(t, s, 0)
                    third_part(t, s, 1)
                    if not beyond(t, 3, NT):
                        deviation(t + 3, 1 - s)
                for t in range(3):
                    deviation(t, t % 2)
                sweep(pool, NT, lambda t, q: body(t, q % 2), 4)

            @block.vector
            def _(dve):
                dve.wait_ge(a_wT, 2)
                dve.tensor_copy(wT[:], pW[:]).then_inc(a_wTs, 1)
                dve.tensor_copy(g0T[:], pG[:, 0, 0, 0:E]).then_inc(a_wTs, 1)
                dve.tensor_copy(g1T[:], pG[:, 0, 1, 0:E]).then_inc(a_wTs, 1)
                dve.wait_ge(a_w, 16 * WLOADS)

                def statistics(t, q):
                    s = q % 2
                    dve.wait_ge(a_x[q], 4 * (t - q) + 16)
                    if started(t, 2):
                        dve.wait_ge(a_rs, t - 1)
                    row_statistics(dve, st[:, s, :, :], mv[:, s, :, :], xt[:, q, :, :], a_st, t, settled)\
                        .then_inc(a_agg, 1)

                def norm(t, q):
                    s = q % 2
                    dve.wait_ge(a_rs, t + 1)
                    if started(t, 2):
                        dve.wait_ge(a_tr, t - 1)
                        dve.wait_ge(a_xnd[s], 8 * (t - s))
                    dve.tensor_copy(xn[:, s, :, D:DR].bitcast(U32),
                                    dest0[:, bass.ds(t * SUB, SUB)].unsqueeze(2))
                    for j in range(SUB):
                        ins = dve.tensor_scalar(xn[:, s, j, 0:D], xt[:, q, j, :], mv[:, s, j, 0:1],
                                                rs[:, s, j:j + 1], ALU.subtract, ALU.mult)
                    ins.then_inc(a_xn, 1)

                def body(t, q):
                    s = q % 2
                    for n in range(2):
                        dve.wait_ge(a_qf, 4 * t + 2 * n + 2)
                        dve.tensor_tensor(parts[:, s, n, 1, :], qf[:, n, :], parts[:, s, n, 0, :],
                                          ALU.subtract).then_inc(a_mid, 1)
                    if not beyond(t, 2, NT):
                        norm(t + 2, (q + 2) % 4)
                    dve.wait_ge(a_v, t + 1)
                    dve.tensor_tensor(V[:, bass.ds(t * SUB, SUB), :], pV[:],
                                      bv_bc[:].unsqueeze(1).broadcast_to([P, SUB, D]), ALU.add)
                    dve.tensor_tensor(rt.lg[:], pL[:],
                                      gb_bc[:].unsqueeze(1).broadcast_to([P, SUB, E]), ALU.add)\
                       .then_inc(a_vs, 1)
                    if started(t, 1):
                        assign(t - 1)
                    link = chain(dve, a_route, LINKS0 * t)
                    dve.wait_ge(a_vs, t + 1)
                    first_of_largest(dve, link, rt.lg, rt.oh[0], rt.m[0][:], rt.c[0], SUB)
                    dve.sem_inc(a_hit, 1)
                    if not beyond(t, 3, NT):
                        statistics(t + 3, (q + 3) % 4)

                def assign(t):
                    dve.wait_ge(a_cnt, t + 1)
                    assign_rows(dve, chain(dve, a_route, LINKS0 * t + 5), rt, pG, rows0,
                                [row0[:, bass.ds(t * SUB, SUB)]])
                dve.wait_ge(a_dest, 1)
                statistics(0, 0)
                statistics(1, 1)
                norm(0, 0)
                norm(1, 1)
                statistics(2, 2)
                sweep(dve, NT, body, 4)
                assign(NT - 1)

            @block.tensor
            def _(pe):
                pe.wait_ge(a_w, 16 * WLOADS)
                pe.wait_ge(a_const, 7 + E)
                for n in range(4):
                    ins = nc.tensor.transpose(pW[:, n, :], wload[:, n, :], ident[:])
                ins.then_inc(a_wT, 1)
                for n in range(2):
                    ins = nc.tensor.transpose(pG[:, 0, n, 0:E], gload[:, n, :], ident[0:E, 0:E])
                ins.then_inc(a_wT, 1)
                pe.wait_ge(a_wTs, 3)

                def transpose(t, s):
                    pe.wait_ge(a_xn, t + 1)
                    if started(t, 1):
                        pe.wait_ge(a_xT, t)
                    for j in range(SUB):
                        ins = nc.tensor.transpose(pX[:, j * P:(j + 1) * P], xn[:, s, j, 0:D], ident[:])
                    ins.then_inc(a_tr, 1)

                def body(t, s):
                    if not is_last(t, NT):
                        transpose(t + 1, 1 - s)
                    pe.wait_ge(a_xT, t + 1)
                    if started(t, 1):
                        pe.wait_ge(a_qf, 4 * t)
                    nc.tensor.matmul(pQ[:], wT[:, 0, :], xnT[:, s, :], start=True, stop=True).then_inc(a_q, 1)
                    nc.tensor.matmul(pK[:], wT[:, 1, :], xnT[:, s, :], start=True, stop=True).then_inc(a_q, 1)
                    if started(t, 1):
                        pe.wait_ge(a_vs, t)
                    for j in range(SUB):
                        nc.tensor.matmul(pV[:, j, :], xnT[:, s, j * P:(j + 1) * P], wT[:, 2, :],
                                         start=True, stop=True)
                        ins = nc.tensor.matmul(pL[:, j, :], xnT[:, s, j * P:(j + 1) * P], g0T[:],
                                               start=True, stop=True)
                    ins.then_inc(a_v, 1)
                    if started(t, 1):
                        count_rows(pe, a_hit, a_cnt, a_route, LINKS0, t - 1, rt, pG)
                transpose(0, 0)
                sweep(pe, NT, body)
                count_rows(pe, a_hit, a_cnt, a_route, LINKS0, NT - 1, rt, pG)

            @block.scalar
            def _(act):
                def copy_x(t, s):
                    act.wait_ge(a_tr, t + 1)
                    if started(t, 2):
                        act.wait_ge(a_v, t - 1)
                    act.copy(xnT[:, s, :], pX[:]).then_inc(a_xT, 1)

                act.wait_ge(a_w, 16 * WLOADS)

                def body(t, s):
                    if not is_last(t, NT):
                        copy_x(t + 1, 1 - s)
                    if started(t, 1):
                        act.wait_ge(a_low, 2 * t)
                        act.wait_ge(a_mid, 2 * t)
                    if started(t, 2):
                        act.wait_ge(a_pd[s], 16 * (t - s))
                    for n, (ps, bias) in enumerate(((pQ, bqc), (pK, bkc))):
                        act.wait_ge(a_q, 2 * t + n + 1)
                        act.activation(qf[:, n, :], ps[:], ACT.Identity, bias=bias[:]).then_inc(a_qf, 1)
                        act.activation(parts[:, s, n, 0, :], ps[:], ACT.Identity, bias=bias[:])\
                           .then_inc(a_qf, 1)
                    if started(t, 1):
                        store(t - 1, 1 - s)

                def store(t, s):
                    for n, dst in enumerate((qs_d, ks_d)):
                        act.wait_ge(a_low, 2 * t + n + 1)
                        act.wait_ge(a_mid, 2 * t + n + 1)
                        act.dma_start(dst[:, :, bass.ds(t * TT, TT)].rearrange("a d t -> d a t"),
                                      parts[:, s, n, :, :]).then_inc(a_pd[s], 16)
                copy_x(0, 0)
                sweep(act, NT, body)
                store(NT - 1, 1)
                for s in range(2):
                    act.wait_ge(a_pd[s], 16 * NT)
                    act.wait_ge(a_xnd[s], 8 * NT)

        r_link = sem("r_link")
        r_lane = sem("r_lane")
        r_fill = sem("r_fill")
        r_pad = sem("r_pad")
        r_dma = sem("r_dma")
        BLOCK_LINKS = 22

        def blocks(pre, calls, free, start, xs, eb, bs, nb, ph):
            fill = sb(pre + "fill", [P, E + SPARE, DR], F32, ph)
            cnt = sb(pre + "cnt", [P, E], F32, ph)
            need = sb(pre + "need", [P, E, NS * TOPK], F32, ph)
            nblk = sb(pre + "nblk", [P, E], F32, ph)
            end = [sb(f"{pre}end{i}", [P, E], F32, ph) for i in range(2)]
            past = sb(pre + "past", [P, nb, E], F32, ph)
            mine = sb(pre + "mine", [P, nb, E], F32, ph)
            first = sb(pre + "first", [P, nb, E], F32, ph)
            ebf = sb(pre + "ebf", [P, nb], F32, ph)
            bsf = sb(pre + "bsf", [P, nb], F32, ph)
            lanes = sb(pre + "lanes", [P, 1], F32, ph)
            padf = sb(pre + "padf", [P, E], F32, ph)
            pad = sb(pre + "pad", [P, E], U32, ph)

            def pad_steps(pool):
                pool.iota(lanes[:], [[0, 1]], base=0, channel_multiplier=1,
                          allow_small_or_imprecise_dtypes=True).then_inc(r_lane, 1)
                pool.memset(fill[:, :, 0:D], 0.0).then_inc(r_fill, 1)
                pool.iota(fill[:, :, D:DR].bitcast(U32), [[P, E + SPARE], [0, 1]], base=start,
                          channel_multiplier=1).then_inc(r_fill, 1)
                pool.wait_ge(r_fill, 2 * calls + 2)
                pool.dma_start(xs[E * REG:E * REG + SPARE * P, :].rearrange("(j p) d -> p j d", p=P),
                               fill[:, E:E + SPARE, :]).then_inc(r_dma, 16)
                pool.wait_ge(r_pad, calls + 1)
                for e in range(E):
                    pool.indirect_dma_start(
                        out=xs, out_offset=bass.IndirectOffsetOnAxis(pad[:, e:e + 1], 0),
                        in_=fill[:, e, :], in_offset=None).then_inc(r_dma, 16)
                pool.wait_ge(r_dma, 16 * (E + 1) * (calls + 1))

            def table_steps(dve):
                link = chain(dve, r_link, calls * BLOCK_LINKS)
                dve.wait_ge(r_lane, calls + 1)
                link(dve.tensor_scalar(padf[:], free[:], lanes[:], None, ALU.add))
                dve.tensor_copy(pad[:], padf[:]).then_inc(r_pad, 1)
                link(dve.tensor_tensor(cnt[:], free[:], region[:], ALU.subtract))
                link(dve.tensor_tensor(need[:], cnt[:].unsqueeze(2).broadcast_to([P, E, NS * TOPK]),
                                       thr[:], ALU.is_gt))
                link(dve.tensor_reduce(nblk[:], need[:], AX.X, ALU.add))
                link(dve.tensor_copy(end[0][:], nblk[:]))
                cur, step = 0, 1
                while step < E:
                    a, b = end[cur], end[1 - cur]
                    dve.tensor_copy(b[:, 0:step], a[:, 0:step])
                    link(dve.tensor_tensor(b[:, step:], a[:, step:], a[:, 0:E - step], ALU.add))
                    cur, step = 1 - cur, 2 * step
                last = end[cur]
                link(dve.tensor_tensor(past[:], blk[:, 0:nb, :],
                                       last[:].unsqueeze(1).broadcast_to([P, nb, E]), ALU.is_ge))
                link(dve.tensor_reduce(ebf[:], past[:], AX.X, ALU.add))
                dve.memset(eb[:, nb:], 0)
                link(dve.tensor_scalar(eb[:, 0:nb], ebf[:], float(E - 1), None, ALU.min))
                dve.tensor_scalar(mine[:, :, 0:1], past[:, :, 0:1], -1.0, 1.0, ALU.mult, ALU.add)
                link(dve.tensor_tensor(mine[:, :, 1:E], past[:, :, 0:E - 1], past[:, :, 1:E], ALU.subtract))
                link(dve.tensor_tensor(nblk[:], last[:], nblk[:], ALU.subtract))
                link(dve.tensor_tensor(first[:], blk[:, 0:nb, :],
                                       nblk[:].unsqueeze(1).broadcast_to([P, nb, E]), ALU.subtract))
                link(dve.tensor_scalar(first[:], first[:], float(P), None, ALU.mult))
                link(dve.tensor_tensor(first[:], first[:], region[:].unsqueeze(1).broadcast_to([P, nb, E]),
                                       ALU.add))
                link(dve.tensor_tensor(first[:], first[:], mine[:], ALU.mult))
                link(dve.tensor_reduce(bsf[:], first[:], AX.X, ALU.add))
                link(dve.tensor_tensor(ebf[:], blk[:, 0:nb, 0], last[:, E - 1:E].broadcast_to([P, nb]),
                                       ALU.subtract))
                link(dve.tensor_scalar(ebf[:], ebf[:], float(P), float(E * REG), ALU.mult, ALU.add))
                link(dve.tensor_tensor(ebf[:], ebf[:], past[:, :, E - 1], ALU.mult))
                link(dve.tensor_tensor(bs[:], bsf[:], ebf[:], ALU.add))
            return pad_steps, table_steps

        with ExitStack() as ph:
            qk = sb("qk", [KROWS, 2, 2, T], BF16, ph)
            PAIRS = BG
            Ex = sb("Ex", [P, 4, B, P], F32, ph)
            Vh = sb("Vh", [P, 2, NS, DK], F32, ph)
            mg = sb("mg", [P, P, NBG], F32, ph)
            negm = sb("negm", [P, P], F32, ph)
            mh = sb("mh", [P, 2, P], BF16, ph)
            ml = sb("ml", [P, 2, P], BF16, ph)
            pairs = sb("pairs", [P, PAIRS, P], F32, ph)
            Zg = sb("Zg", [P, P, 4], F32, ph)
            Z = sb("Z", [P, P], F32, ph)
            R = sb("R", [P, 2, P], F32, ph)
            Oev = sb("Oev", [P, 2, NBG, P], F32, ph)
            xr = sb("xr", [P, 2, SUB, DR], F32, ph)
            idx = sb("idx", [P, 2, SUB], U32, ph)
            pA = pb("pA", [P, 2, BG, P], ph)
            pB = pb("pB", [P, 2, 2, BG, P], ph)
            pO = pb("pO", [P, NBG, P], ph)

            b_qk = [sem("b_qk0"), sem("b_qk1")]
            b_z = sem("b_z")
            b_s1 = sem("b_s1")
            b_red = sem("b_red")
            b_nm = sem("b_nm")
            b_mh = sem("b_mh")
            b_m = sem("b_m")
            b_s2 = sem("b_s2")
            b_exp = sem("b_exp")
            b_pair = sem("b_pair")
            b_part = sem("b_part")
            b_sum = sem("b_sum")
            b_r = sem("b_r")
            b_norm = sem("b_norm")
            b_vh = sem("b_vh")
            b_pv = sem("b_pv")
            b_oev = sem("b_oev")
            b_od = [sem("b_od0"), sem("b_od1")]
            b_xr = [sem("b_xr0"), sem("b_xr1")]
            b_idx = sem("b_idx")
            b_sc = [sem("b_sc0"), sem("b_sc1")]
            LOADS = 12 * 16
            oT_v = oT_d.rearrange("(n d) (g c h q) -> n d g c h q", d=DK, g=NBG, c=BG, h=2)

            block = ph.enter_context(nc.Block())

            @block.sync
            def _(sp):
                def load(h, s):
                    for i in range(NPART):
                        for j in range(NPART):
                            r = (NPART * i + j) * DK
                            sp.dma_start(qk[r:r + DK, s, 0, :], qs_d[i, bass.ds(h * DK, DK), :])\
                              .then_inc(b_qk[s], 16)
                    for i in range(NPART):
                        r = NPART * i * DK
                        sp.dma_start(qk[r:r + NPART * DK, s, 1, :],
                                     ks_d[:, bass.ds(h * DK, DK), :]).then_inc(b_qk[s], 16)

                def store(h, w, qh):
                    sp.wait_ge(b_oev, w + 1)
                    settle(sp, settled)
                    for c in range(BG):
                        sp.dma_start(oT_v[bass.ds(h, 1), :, :, c, qh, :].squeeze(0),
                                     Oev[32 * c:32 * c + DK, qh, :, :]).then_inc(b_od[qh], 16)

                def body(h, s):
                    if started(h, 2):
                        sp.wait_ge(b_sc[s], 32 * (h - s))
                        settle(sp, settled)
                    sp.dma_start(xr[:, s, :, :], xn0_d[:, bass.ds(h * SUB, SUB), :]).then_inc(b_xr[s], 16)
                    if started(h, 1):
                        sp.wait_ge(b_s2, 16 * h)
                    if not is_last(h, H):
                        load(h + 1, 1 - s)
                    if started(h, 1):
                        store(h - 1, 2 * h - 1, 1)
                    store(h, 2 * h, 0)
                load(0, 0)
                sweep(sp, H, body)
                store(H - 1, 2 * H - 1, 1)
                for qh in range(2):
                    sp.wait_ge(b_od[qh], 16 * BG * H)

            @block.tensor
            def _(pe):
                def s1_group(n, head_slot, qh, kc, g):
                    if not isinstance(n, int) or n >= 2:
                        pe.wait_ge(b_red, n - 1)
                    for c in range(BG):
                        tok = (BG * g + c) * S
                        ins = nc.tensor.matmul(pA[:, g % 2, c, :],
                                               qk[:, head_slot, 1, tok + kc * P:tok + kc * P + P],
                                               qk[:, head_slot, 0, tok + qh * P:tok + qh * P + P],
                                               start=True, stop=True)
                    ins.then_inc(b_s1, 1)

                def s2_group(n, u, s, j, g):
                    qh, kc = j // 2, j % 2
                    if not isinstance(n, int) or n >= 2:
                        pe.wait_ge(b_exp, n - 1)
                    for k in range(2):
                        for i, m in enumerate((mh, ml)):
                            nc.tensor.matmul(pB[:, g % 2, k, :, :], identb[:],
                                             m[:, j % 2, :].unsqueeze(1).broadcast_to([P, BG, P]),
                                             start=(i == 0), stop=False, skip_group_check=True)
                        for c in range(BG):
                            tok = (2 * BG * g + BG * k + c) * S
                            ins = nc.tensor.matmul(pB[:, g % 2, k, c, :],
                                                   qk[:, s, 1, tok + kc * P:tok + kc * P + P],
                                                   qk[:, s, 0, tok + qh * P:tok + qh * P + P],
                                                   start=False, stop=(c == BG - 1), skip_group_check=True)
                    ins.then_inc(b_s2, 1)

                def pv_group(v, s, j, g):
                    kc = j % 2
                    for k in range(2):
                        for c in range(BG):
                            b = 2 * BG * g + BG * k + c
                            ins = nc.tensor.matmul(pO[32 * c:32 * c + DK, b // BG, :],
                                                   Vh[:, s, 2 * b + kc, :], Ex[:, j, b, :],
                                                   start=(kc == 0 and (b // BG) % 4 == 0), stop=(kc == 1),
                                                   skip_group_check=True)
                    if g == 3:
                        ins.then_inc(b_pv, 1)

                def pv_waits(v, h, j):
                    pe.wait_ge(b_norm, v + 1)
                    if j == 0:
                        pe.wait_ge(b_vh, h + 1)
                    if j % 2 == 0:
                        if not isinstance(h, int) or 2 * h + j // 2 > 0:
                            pe.wait_ge(b_oev, 2 * h + j // 2)

                def body(h, s):
                    for j in range(4):
                        u = 4 * h + j
                        first_pv = started(h, 1) or j >= 2
                        lag_j, lag_s = (j - 2, s) if j >= 2 else (j + 2, 1 - s)
                        for g in range(NBG):
                            if j < 3:
                                s1_group(8 * (u + 1) + g, s, (j + 1) // 2, (j + 1) % 2, g)
                            elif not is_last(h, H):
                                if g == 0:
                                    pe.wait_ge(b_qk[1 - s], (h + 1 - (1 - s)) * (LOADS // 2) + LOADS)
                                s1_group(8 * (u + 1) + g, 1 - s, 0, 0, g)
                            if g % 2 == 1:
                                if g == 1:
                                    pe.wait_ge(b_m, u + 1)
                                s2_group(4 * u + g // 2, u, s, j, g // 2)
                                if first_pv:
                                    if g == 1:
                                        pv_waits(u - 2, h if j >= 2 else h - 1, lag_j)
                                    pv_group(u - 2, lag_s, lag_j, g // 2)

                pe.wait_ge(b_z, 1)
                pe.wait_ge(b_qk[0], LOADS)
                for g in range(NBG):
                    s1_group(g, 0, 0, 0, g)
                sweep(pe, H, body)
                for j in (2, 3):
                    pv_waits(4 * (H - 1) + j, H - 1, j)
                    for g in range(4):
                        pv_group(4 * (H - 1) + j, 1, j, g)

            @block.vector
            def _(dve):
                def group_max(u, g):
                    dve.wait_ge(b_s1, 8 * u + g + 1)
                    dve.tensor_reduce(mg[:, :, g], pA[:, g % 2, :, :].rearrange("p b q -> p q b"),
                                      AX.X, ALU.max).then_inc(b_red, 1)

                def unit_max(u, m):
                    dve.wait_ge(b_red, 8 * u + 8)
                    if not isinstance(u, int) or u >= 1:
                        dve.wait_ge(b_m, u)
                    dve.tensor_reduce(negm[:], mg[:], AX.X, ALU.max, negate=True).then_inc(b_nm, 1)
                    dve.wait_ge(b_nm, u + 1)
                    if not isinstance(u, int) or u >= 2:
                        dve.wait_ge(b_s2, 4 * (u - 1))
                    dve.tensor_copy(mh[:, m, :], negm[:]).then_inc(b_mh, 1)
                    dve.wait_ge(b_mh, u + 1)
                    dve.tensor_tensor(ml[:, m, :], negm[:], mh[:, m, :], ALU.subtract).then_inc(b_m, 1)

                def part_sum(rows, g):
                    dve.tensor_reduce(Zg[:, :, g], rows.rearrange("p b q -> p q b"),
                                      AX.X, ALU.add).then_inc(b_part, 1)

                def group_sum(u, j, g):
                    if g == 0:
                        if not isinstance(u, int) or u >= 1:
                            dve.wait_ge(b_sum, u)
                        dve.wait_ge(b_pair, u + 1)
                        part_sum(pairs[:], 0)
                    else:
                        dve.wait_ge(b_exp, 4 * u + g + 1)
                        part_sum(Ex[:, j, 2 * BG * g:2 * BG * (g + 1), :], g)

                def unit_sum(u, j):
                    dve.wait_ge(b_part, 4 * u + 4)
                    if not isinstance(u, int) or u >= 1:
                        dve.wait_ge(b_r, u)
                    dve.tensor_reduce(Z[:], Zg[:], AX.X, ALU.add).then_inc(b_sum, 1)
                    dve.wait_ge(b_sum, u + 1)
                    if not isinstance(u, int) or u >= 2:
                        dve.wait_ge(b_norm, u - 1)
                    dve.reciprocal(R[:, j % 2, :], Z[:]).then_inc(b_r, 1)

                def body(h, s):
                    if started(h, 2):
                        dve.wait_ge(b_sc[s], 32 * (h - s))
                    dve.tensor_copy(idx[:, s, :], row0[:, bass.ds(h * SUB, SUB)]).then_inc(b_idx, 1)
                    for j in range(4):
                        u = 4 * h + j
                        more = not (is_last(h, H) and j == 3)
                        much_more = not (is_last(h, H) and j >= 2)
                        for g in range(1, 4):
                            if more:
                                group_max(u + 1, 2 * g)
                                group_max(u + 1, 2 * g + 1)
                            group_sum(u, j, g - 1)
                        if more:
                            unit_max(u + 1, (j + 1) % 2)
                        if much_more:
                            group_max(u + 2, 0)
                        group_sum(u, j, 3)
                        if much_more:
                            group_max(u + 2, 1)
                        unit_sum(u, j)

                dve.memset(pO[:], 0.0).then_inc(b_z, 1)
                for g in range(NBG):
                    group_max(0, g)
                unit_max(0, 0)
                group_max(1, 0)
                group_max(1, 1)
                sweep(dve, H, body)

            @block.scalar
            def _(act):
                def evac(h, qh):
                    w = 2 * h + qh
                    act.wait_ge(b_pv, 2 * w + 2)
                    if started(h, 1):
                        act.wait_ge(b_od[qh], 16 * BG * h)
                    act.copy(Oev[:, qh, :, :], pO[:]).then_inc(b_oev, 1)

                def body(h, s):
                    if started(h, 2):
                        act.wait_ge(b_pv, 4 * (h - 1))
                    act.copy(Vh[:, s, :, :], V[:, :, bass.ds(h * DK, DK)]).then_inc(b_vh, 1)
                    for j in range(4):
                        u = 4 * h + j
                        if started(h, 1):
                            act.wait_ge(b_pv, u - 3)
                        for g in range(4):
                            act.wait_ge(b_s2, 4 * u + g + 1)
                            act.activation(Ex[:, j, 2 * BG * g:2 * BG * (g + 1), :],
                                           pB[:, g % 2, :, :, :].rearrange("p k b q -> p (k b) q"),
                                           ACT.Exp).then_inc(b_exp, 1)
                        if j == 1 and started(h, 1):
                            evac(h - 1, 1)
                        if j == 3:
                            evac(h, 0)
                sweep(act, H, body)
                evac(H - 1, 1)

            @block.gpsimd
            def _(pool):
                def add_pairs(u, j):
                    pool.wait_ge(b_exp, 4 * u + 1)
                    if not isinstance(u, int) or u >= 1:
                        pool.wait_ge(b_part, 4 * u - 3)
                    pool.tensor_tensor(pairs[:], Ex[:, j, 0:PAIRS, :], Ex[:, j, PAIRS:2 * PAIRS, :],
                                       ALU.add).then_inc(b_pair, 1)

                def body(h, s):
                    for j in range(4):
                        u = 4 * h + j
                        if not (is_last(h, H) and j == 3):
                            add_pairs(u + 1, (j + 1) % 4)
                        pool.wait_ge(b_r, u + 1)
                        pool.tensor_tensor(Ex[:, j, :, :], Ex[:, j, :, :],
                                           R[:, j % 2, :].unsqueeze(1).broadcast_to([P, B, P]),
                                           ALU.mult).then_inc(b_norm, 1)
                        if j == 0:
                            pool.wait_ge(b_xr[s], 8 * (h - s) + 16)
                            pool.wait_ge(b_idx, h + 1)
                            settle(pool, settled)
                        pool.indirect_dma_start(
                            out=xs0_d, out_offset=bass.IndirectOffsetOnAxis(idx[:, s, j:j + 1], 0),
                            in_=xr[:, s, j, :], in_offset=None).then_inc(b_sc[s], 16)
                add_pairs(0, 0)
                sweep(pool, H, body)
                for s in range(2):
                    pool.wait_ge(b_sc[s], 16 * SUB * NT // 2)

        vstack.close()

        w1T = sb("w1T", [P, 2 * E + 1, HID])
        w2T = sb("w2T", [P, 2 * E + 1, HC, D])
        b1c = sb("b1c", [P, E * HC])
        b2x = sb("b2x", [P, E, D])
        wqkv = sb("wqkv", [P, 3 * D])
        bqk1 = sb("bqk1", [P, 2])
        bv1 = sb("bv1", [P, D])
        lnw = sb("lnw", [P, D])
        lnb = sb("lnb", [P, D])
        mdiag = sb("mdiag", [P, P])
        mcross = sb("mcross", [P, P])

        with ExitStack() as ph:
            bo_bc = sb("bo_bc", [P, D], F32, ph)
            w1l = sb("w1l", [P, 4, HC, D], F32, ph)
            w2l = sb("w2l", [P, 4, HID], F32, ph)
            p1 = pb("p1", [P, 2, HID], ph)
            p2 = pb("p2", [P, 2, HC, D], ph)
            b1l = sb("b1l", [E * HC, P], F32, ph)
            pB1 = pb("pB1", [P, E * HC], ph)
            c_w = [sem(f"c_w{i}") for i in range(4)]
            c_b1 = sem("c_b1")
            c_b1T = sem("c_b1T")
            c_s = sem("c_s")
            c_tr = sem("c_tr")
            c_ev1 = sem("c_ev1")
            c_ev2 = sem("c_ev2")
            c_m = sem("c_m")
            SMALL = 8

            block = ph.enter_context(nc.Block())

            pad_steps, table_steps = blocks("r0", 0, rows0, T, xs0_d, eb0, bs0, NB0, ph)

            def groups(eng, one):
                for e in range(E):
                    one(e, e % 4, w1_0, w2_0, e)
                with eng.Fori(0, E // 4) as i:
                    for j in range(4):
                        one(E + 4 * i + j, j, w1_1, w2_1, 4 * i + j)
                one(2 * E, 0, None, None, 0)

            @block.sync
            def _(sp):
                sp.dma_start(b1l[:], b1_0.rearrange("e (c p) -> (e c) p", p=P)).then_inc(c_b1, 16)

                def one(k, s, w1, w2, e):
                    if started(k, 4):
                        sp.wait_ge(c_tr, k - 3)
                    a = sh_w1 if w1 is None else w1[e, :, :]
                    b = sh_w2 if w2 is None else w2[e, :, :]
                    sp.dma_start(w1l[:, s, :, :], a.rearrange("(c p) d -> p c d", p=P)).then_inc(c_w[s], 16)
                    sp.dma_start(w2l[:, s, :], b).then_inc(c_w[s], 16)
                groups(sp, one)

            @block.tensor
            def _(pe):
                def one(k, s, w1, w2, e):
                    pe.wait_ge(c_w[s], 8 * (k - s) + 32)
                    if started(k, 2):
                        pe.wait_ge(c_ev1, k - 1)
                        pe.wait_ge(c_ev2, k - 1)
                    for c in range(HC):
                        nc.tensor.transpose(p1[:, s % 2, c * P:(c + 1) * P], w1l[:, s, c, :], ident[:])
                        ins = nc.tensor.transpose(p2[:, s % 2, c, :], w2l[:, s, c * P:(c + 1) * P], ident[:])
                    ins.then_inc(c_tr, 1)
                groups(pe, one)
                pe.wait_ge(c_b1, 16)
                nc.tensor.transpose(pB1[:], b1l[:], ident[0:E * HC, 0:E * HC]).then_inc(c_b1T, 1)

            @block.scalar
            def _(act):
                act.dma_start(b2x[:], b2_0.partition_broadcast(P)).then_inc(c_s, 16)
                act.dma_start(bo_bc[:], bo.partition_broadcast(P)).then_inc(c_s, 16)
                act.dma_start(wqkv[:], W_qkv).then_inc(c_s, 16)
                act.dma_start(bqk1[:, 0:1], b_qkv[0:D].rearrange("(p a) -> p a", a=1)).then_inc(c_s, 16)
                act.dma_start(bqk1[:, 1:2], b_qkv[D:2 * D].rearrange("(p a) -> p a", a=1)).then_inc(c_s, 16)
                act.dma_start(bv1[:], b_qkv[2 * D:3 * D].partition_broadcast(P)).then_inc(c_s, 16)
                act.dma_start(lnw[:], ln_w.partition_broadcast(P)).then_inc(c_s, 16)
                act.dma_start(lnb[:], ln_b.partition_broadcast(P)).then_inc(c_s, 16)

                def one(k, s, w1, w2, e):
                    act.wait_ge(c_tr, k + 1)
                    act.copy(w1T[:, bass.ds(k, 1), :], p1[:, s % 2, :].unsqueeze(1)).then_inc(c_ev1, 1)
                groups(act, one)
                act.wait_ge(c_b1T, 1)
                act.copy(b1c[:], pB1[:])

            @block.vector
            def _(dve):
                table_steps(dve)

                def one(k, s, w1, w2, e):
                    dve.wait_ge(c_tr, k + 1)
                    dve.tensor_copy(w2T[:, bass.ds(k, 1), :, :], p2[:, s % 2, :, :].unsqueeze(1)).then_inc(c_ev2, 1)
                groups(dve, one)
                dve.wait_ge(c_s, 16 * SMALL)
                dve.tensor_tensor(b2x[:], b2x[:], bo_bc[:].unsqueeze(1).broadcast_to([P, E, D]), ALU.add)

            @block.gpsimd
            def _(pool):
                pad_steps(pool)
                link = chain(pool, c_m, 0)
                link(pool.memset(mdiag[:], 1.0))
                link(pool.memset(mcross[:], 1.0))
                link(pool.affine_select(out=mdiag[:], in_=mdiag[:], compare_op=ALU.is_ge, fill=0.0, base=0,
                                        pattern=[[1, P]], channel_multiplier=-1))
                link(pool.affine_select(out=mdiag[:], in_=mdiag[:], compare_op=ALU.is_ge, fill=0.0,
                                        base=SPAN - 1, pattern=[[-1, P]], channel_multiplier=1))
                link(pool.affine_select(out=mcross[:], in_=mcross[:], compare_op=ALU.is_ge, fill=0.0,
                                        base=SPAN - 1 - P, pattern=[[-1, P]], channel_multiplier=1))

        e_x = [sem(f"e_x{i}") for i in range(RND)]
        e_xp = sem("e_xp")
        e_xT = sem("e_xT")
        e_u = sem("e_u")
        e_hb = sem("e_hb")
        e_hp = sem("e_hp")
        e_hT = sem("e_hT")
        e_y = sem("e_y")
        e_yb = sem("e_yb")
        e_st = [sem(f"e_st{i}") for i in range(RND)]

        def experts(pre, layer, xs, y, eb, bs, nb, k0):
            with ExitStack() as ph:
                xb = sb(pre + "xb", [P, RND, DR], F32, ph)
                xT = sb(pre + "xT", [P, 2, P], F32, ph)
                hb = sb(pre + "hb", [P, 2, HID], F32, ph)
                hT = sb(pre + "hT", [P, 2, HC, P], F32, ph)
                yb = sb(pre + "yb", [P, RND, D], F32, ph)
                pX = [pb(f"{pre}pX{i}", [P, P], ph) for i in range(2)]
                pU = [pb(f"{pre}pU{i}", [P, HID], ph) for i in range(2)]
                pT = [pb(f"{pre}pT{i}", [P, HC, P], ph) for i in range(2)]
                pY = [pb(f"{pre}pY{i}", [P, D], ph) for i in range(2)]
                w1L = w1T[:, layer * E:(layer + 1) * E, :]
                w2L = w2T[:, layer * E:(layer + 1) * E, :, :]
                block = ph.enter_context(nc.Block())

                loads = [0]

                def experts_of(eng, k):
                    loads[0] += 1
                    regs = [eng.alloc_register(f"{pre}e{loads[0]}_{j}") for j in range(RND + 2)]
                    eng.load(regs, eb[0:1, bass.ds(k, RND + 2)])
                    return [eng.snap(reg, donate=True, min_val=0, max_val=E - 1) for reg in regs]

                @block.sync
                def _(sp):
                    def body(k, q):
                        first = sp.value_load(bs[0:1, bass.ds(k, 1)], min_val=0, max_val=E * REG + (SPARE - 1) * P)
                        if started(k, RND):
                            sp.wait_ge(e_st[q], 16 // RND * (k0 + k - q))
                            settle(sp, settled)
                        sp.dma_start(xb[:, q, :], xs[bass.ds(first, P), :]).then_inc(e_x[q], 16)
                    sweep(sp, nb, body, RND)

                @block.gpsimd
                def _(pool):
                    def body(k, q):
                        pool.wait_ge(e_yb, k0 + k + 1)
                        settle(pool, settled)
                        pool.indirect_dma_start(
                            out=y, out_offset=bass.IndirectOffsetOnAxis(xb[:, q, D:DR].bitcast(U32), 0),
                            in_=yb[:, q, :], in_offset=None).then_inc(e_st[q], 16)
                    sweep(pool, nb, body, RND)
                    for q in range(RND):
                        pool.wait_ge(e_st[q], 16 // RND * (k0 + nb))

                @block.tensor
                def _(pe):
                    def transpose_x(k, q):
                        pe.wait_ge(e_x[q], 16 // RND * (k0 + k - q) + 16)
                        if started(k, 2):
                            pe.wait_ge(e_xT, k0 + k - 1)
                        nc.tensor.transpose(pX[q % 2][:], xb[:, q, 0:D], ident[:]).then_inc(e_xp, 1)

                    def up(k, q, e):
                        pe.wait_ge(e_xT, k0 + k + 1)
                        if started(k, 2):
                            pe.wait_ge(e_hb, k0 + k - 1)
                        nc.tensor.matmul(pU[q % 2][:].unsqueeze(1), xT[:, q % 2, :], w1L[:, bass.ds(e, 1), :],
                                         start=True, stop=True).then_inc(e_u, 1)

                    def transpose_h(k, q):
                        pe.wait_ge(e_hb, k0 + k + 1)
                        if started(k, 2):
                            pe.wait_ge(e_hT, k0 + k - 1)
                        for c in range(HC):
                            ins = nc.tensor.transpose(pT[q % 2][:, c, :], hb[:, q % 2, c * P:(c + 1) * P],
                                                      ident[:])
                        ins.then_inc(e_hp, 1)

                    def down(k, q, e):
                        pe.wait_ge(e_hT, k0 + k + 1)
                        if started(k, 2):
                            pe.wait_ge(e_yb, k0 + k - 1)
                        for c in range(HC):
                            ins = nc.tensor.matmul(pY[q % 2][:].unsqueeze(1), hT[:, q % 2, c, :],
                                                   w2L[:, bass.ds(e, 1), c, :],
                                                   start=(c == 0), stop=(c == HC - 1))
                        ins.then_inc(e_y, 1)

                    def body(k, q):
                        if q == 0:
                            es[:] = experts_of(pe, k)
                        if not beyond(k, 2, nb):
                            up(k + 2, (q + 2) % RND, es[q + 2])
                        if not beyond(k, 3, nb):
                            transpose_x(k + 3, (q + 3) % RND)
                        if not beyond(k, 1, nb):
                            transpose_h(k + 1, (q + 1) % RND)
                        down(k, q, es[q])
                    es = experts_of(pe, 0)
                    transpose_x(0, 0)
                    transpose_x(1, 1)
                    up(0, 0, es[0])
                    transpose_x(2, 2)
                    up(1, 1, es[1])
                    transpose_h(0, 0)
                    sweep(pe, nb, body, RND)

                @block.scalar
                def _(act):
                    def copy_x(k, q):
                        act.wait_ge(e_xp, k0 + k + 1)
                        if started(k, 2):
                            act.wait_ge(e_u, k0 + k - 1)
                        act.copy(xT[:, q % 2, :], pX[q % 2][:]).then_inc(e_xT, 1)

                    def leave_up(k, q):
                        act.wait_ge(e_u, k0 + k + 1)
                        if started(k, 2):
                            act.wait_ge(e_hp, k0 + k - 1)
                        if layer == 0:
                            ins = act.copy(hb[:, q % 2, :], pU[q % 2][:])
                        else:
                            ins = act.activation(hb[:, q % 2, :], pU[q % 2][:], ACT.Silu)
                        ins.then_inc(e_hb, 1)

                    def body(k, q):
                        if not beyond(k, 2, nb):
                            leave_up(k + 2, (q + 2) % RND)
                        if not beyond(k, 3, nb):
                            copy_x(k + 3, (q + 3) % RND)
                    copy_x(0, 0)
                    copy_x(1, 1)
                    leave_up(0, 0)
                    copy_x(2, 2)
                    leave_up(1, 1)
                    sweep(act, nb, body, RND)

                @block.vector
                def _(dve):
                    def leave_h(k, q, e):
                        dve.wait_ge(e_hp, k0 + k + 1)
                        if started(k, 2):
                            dve.wait_ge(e_y, k0 + k - 1)
                        if layer == 0:
                            for c in range(HC):
                                ins = dve.tensor_scalar(hT[:, q % 2, c, :], pT[q % 2][:, c, :],
                                                        b1c[:, bass.ds(e * HC + c, 1)], 0.0, ALU.add, ALU.max)
                        else:
                            ins = dve.tensor_copy(hT[:, q % 2, :, :], pT[q % 2][:])
                        ins.then_inc(e_hT, 1)

                    def finish(k, q, e):
                        dve.wait_ge(e_y, k0 + k + 1)
                        if started(k, RND):
                            dve.wait_ge(e_st[q], 16 // RND * (k0 + k - q))
                        if layer == 0:
                            ins = dve.tensor_tensor(yb[:, q, :].unsqueeze(1), pY[q % 2][:].unsqueeze(1),
                                                    b2x[:, bass.ds(e, 1), :], ALU.add)
                        else:
                            ins = dve.tensor_copy(yb[:, q, :], pY[q % 2][:])
                        ins.then_inc(e_yb, 1)

                    def body(k, q):
                        if layer == 0 and q == 0:
                            es[:] = experts_of(dve, k)
                        if not beyond(k, 1, nb):
                            leave_h(k + 1, (q + 1) % RND, es[q + 1])
                        finish(k, q, es[q])
                    es = [None] * (RND + 1) if layer == 1 else experts_of(dve, 0)
                    leave_h(0, 0, es[0])
                    sweep(dve, nb, body, RND)

        experts("x0", 0, xs0_d, y0_d, eb0, bs0, NB0, 0)

        with ExitStack() as ph:
            rt = routing_tiles("d", ph, TOPK)
            idx = sb("d_idx", [P, 4, TOPK, SUB], U32, ph)
            oT = sb("d_oT", [P, 2, TT], F32, ph)
            ye = sb("d_ye", [P, 2, SUB, D], F32, ph)
            acc = sb("d_acc", [P, 4, SUB, D], F32, ph)
            xn = sb("d_xn", [P, 4, TOPK, SUB, DR], F32, ph)
            xnT = sb("d_xnT", [P, 2, TT], F32, ph)
            st = sb("d_st", [P, SUB, 6], F32, ph)
            mv = sb("d_mv", [P, SUB, 2], F32, ph)
            rs = sb("d_rs", [P, SUB], F32, ph)
            st2 = sb("d_st2", [P, SUB, 6], F32, ph)
            mv2 = sb("d_mv2", [P, SUB, 2], F32, ph)
            rs2 = sb("d_rs2", [P, SUB], F32, ph)
            qkT = sb("d_qkT", [P, 2, TT], F32, ph)
            v = sb("d_v", [P, SUB, D], F32, ph)
            sm = sb("d_sm", [P, 2, 3, P], F32, ph)
            o = sb("d_o", [P, SUB, D], F32, ph)
            hT = sb("d_hT", [P, HC, TT], F32, ph)
            pC = pb("d_pC", [P, SUB, D], ph)
            pL = pb("d_pL", [P, SUB, E], ph)
            pH = pb("d_pH", [P, 2, TT], ph)
            pM = pb("d_pM", [P, 2, TT], ph)
            pG = pM[:, 1, 3 * P:4 * P].rearrange("p (a b n) -> p a b n", a=2, b=2)
            pV = pb("d_pV", [P, SUB, D], ph)
            pY = pb("d_pY", [P, SUB, D], ph)

            d_x = [sem(f"d_x{i}") for i in range(4)]
            d_agg = sem("d_agg")
            d_agg2 = sem("d_agg2")
            d_st2 = sem("d_st2s")
            d_copy = sem("d_copy")
            d_hit = sem("d_hit")
            d_cnt = sem("d_cnt")
            d_route = sem("d_route")
            d_sc = [sem(f"d_sc{i}") for i in range(4)]
            d_wo = sem("d_wo")
            d_sum = sem("d_sum")
            d_x1 = sem("d_x1s")
            d_st = sem("d_sts")
            d_ve = sem("d_ve")
            d_rs = sem("d_rss")
            d_xn = sem("d_xns")
            d_tr = sem("d_tr")
            d_xT = sem("d_xTs")
            d_lg = sem("d_lg")
            d_lgs = sem("d_lgs")
            d_up = sem("d_up")
            d_h = sem("d_h")
            d_y = sem("d_y")
            d_qk = sem("d_qk")
            d_qks = sem("d_qks")
            d_v = sem("d_vp")
            d_vs = sem("d_vs")
            d_s = sem("d_s")
            d_sm = sem("d_sms")
            d_o = sem("d_op")
            d_os = sem("d_os")
            d_ve2 = sem("d_ve2")
            d_rs2 = sem("d_rs2s")
            d_ln = sem("d_ln")
            d_ys = sem("d_ys")
            d_acc = sem("d_accs")
            d_x2 = [sem(f"d_x2{i}") for i in range(4)]
            WS = 2 * E
            LINKS = 3
            LINKS1 = 2 * 5 + 3 + 2 * SUB + 1 + 3 * TOPK

            block = ph.enter_context(nc.Block())

            @block.sync
            def _(sp):
                def store(t, q):
                    sp.wait_ge(d_acc, t + 1)
                    settle(sp, settled)
                    sp.dma_start(x2_d[:, bass.ds(t * SUB, SUB), :], acc[:, q, :, :]).then_inc(d_x2[q], 16)

                def body(t, q):
                    if started(t, 4):
                        sp.wait_ge(d_x2[q], 4 * (t - q))
                        settle(sp, settled)
                    if started(t, 2):
                        sp.wait_ge(d_wo, t - 1)
                        settle(sp, settled)
                        sp.wait_ge(d_sum, t - 1)
                        settle(sp, settled)
                    sp.dma_start(oT[:, q % 2, :], oT_d[:, bass.ds(t * TT, TT)]).then_inc(d_x[q], 16)
                    sp.dma_start(ye[:, q % 2, :, :], y0_v[:, bass.ds(t * SUB, SUB), :]).then_inc(d_x[q], 16)
                    sp.dma_start(acc[:, q, :, :], x_v[:, bass.ds(t * SUB, SUB), :]).then_inc(d_x[q], 16)
                    if started(t, 3):
                        store(t - 3, (q + 1) % 4)
                sweep(sp, NT, body, 4)
                for t in range(NT - 3, NT):
                    store(t, t % 4)
                for q in range(4):
                    sp.wait_ge(d_x2[q], 4 * NT)

            @block.tensor
            def _(pe):
                def project(t, q):
                    s = q % 2
                    pe.wait_ge(d_x[q], 12 * (t - q) + 48)
                    if started(t, 1):
                        pe.wait_ge(d_xT, t)
                    for j in range(SUB):
                        ins = nc.tensor.matmul(pC[:, j, :], oT[:, s, j * P:(j + 1) * P], wT[:, 3, :],
                                               start=True, stop=True)
                    ins.then_inc(d_wo, 1)

                def transpose(t, q):
                    pe.wait_ge(d_xn, t + 1)
                    for j in range(SUB):
                        ins = nc.tensor.transpose(pC[:, j, :], xn[:, q, 0, j, 0:D], ident[:])
                    ins.then_inc(d_tr, 1)

                def logits(t, s):
                    pe.wait_ge(d_xT, t + 1)
                    if started(t, 1):
                        pe.wait_ge(d_lgs, t)
                    for j in range(SUB):
                        ins = nc.tensor.matmul(pL[:, j, :], xnT[:, s, j * P:(j + 1) * P], g1T[:],
                                               start=True, stop=True)
                    ins.then_inc(d_lg, 1)

                def up(t, s, c):
                    if c >= 2:
                        pe.wait_ge(d_h, HC * t + c - 1)
                    elif started(t, 1):
                        pe.wait_ge(d_h, HC * t)
                    nc.tensor.matmul(pH[:, c % 2, :], w1T[:, WS, c * P:(c + 1) * P], xnT[:, s, :],
                                     start=True, stop=True).then_inc(d_up, 1)

                def body(t, q):
                    s = q % 2
                    if not is_last(t, NT):
                        project(t + 1, (q + 1) % 4)
                    up(t, s, 0)
                    up(t, s, 1)
                    if started(t, 1):
                        pe.wait_ge(d_os, t)
                        pe.wait_ge(d_route, LINKS1 * t)
                    for n in range(2):
                        nc.tensor.matmul(pM[:, n, :], wqkv[:, n * D:(n + 1) * D], xnT[:, s, :],
                                         start=True, stop=True).then_inc(d_qk, 1)
                    up(t, s, 2)
                    up(t, s, 3)
                    if started(t, 1):
                        pe.wait_ge(d_vs, t)
                    for j in range(SUB):
                        ins = nc.tensor.matmul(pV[:, j, :], xnT[:, s, j * P:(j + 1) * P],
                                               wqkv[:, 2 * D:3 * D], start=True, stop=True)
                    ins.then_inc(d_v, 1)
                    pe.wait_ge(d_qks, 2 * t + 2)
                    for b in range(2):
                        for n, (key, query) in enumerate(((0, 0), (1, 1), (0, 1))):
                            ins = nc.tensor.matmul(pM[:, b, n * P:(n + 1) * P],
                                                   qkT[:, 1, (2 * b + key) * P:(2 * b + key + 1) * P],
                                                   qkT[:, 0, (2 * b + query) * P:(2 * b + query + 1) * P],
                                                   start=True, stop=True)
                        ins.then_inc(d_s, 1)
                    pe.wait_ge(d_h, HC * (t + 1))
                    if started(t, 1):
                        pe.wait_ge(d_ys, t)
                    for j in range(SUB):
                        for c in range(HC):
                            ins = nc.tensor.matmul(pY[:, j, :], hT[:, c, j * P:(j + 1) * P],
                                                   w2T[:, WS, c, :], start=(c == 0), stop=(c == HC - 1))
                    ins.then_inc(d_y, 1)
                    if not is_last(t, NT):
                        transpose(t + 1, (q + 1) % 4)
                    pe.wait_ge(d_sm, 4 * t + 4)
                    count_rows(pe, d_hit, d_cnt, d_route, LINKS1, t, rt, pG)
                    for b in range(2):
                        nc.tensor.matmul(pM[:, 0, 2 * b * P:(2 * b + 1) * P], sm[:, b, 0, :],
                                         v[:, 2 * b, :], start=True, stop=True)
                        nc.tensor.matmul(pM[:, 0, (2 * b + 1) * P:(2 * b + 2) * P], sm[:, b, 1, :],
                                         v[:, 2 * b + 1, :], start=True, stop=False)
                        ins = nc.tensor.matmul(pM[:, 0, (2 * b + 1) * P:(2 * b + 2) * P], sm[:, b, 2, :],
                                               v[:, 2 * b, :], start=False, stop=True)
                    ins.then_inc(d_o, 1)
                    if not is_last(t, NT):
                        logits(t + 1, 1 - s)
                project(0, 0)
                transpose(0, 0)
                logits(0, 0)
                sweep(pe, NT, body, 4)

            @block.scalar
            def _(act):
                def copy_xT(t, q):
                    s = q % 2
                    act.wait_ge(d_tr, t + 1)
                    if started(t, 2):
                        act.wait_ge(d_v, t - 1)
                        act.wait_ge(d_lg, t - 1)
                    act.copy(xnT[:, s, :], pC[:].rearrange("p j n -> p (j n)")).then_inc(d_xT, 1)
                    act.copy(xn[:, q, 1, :, 0:D], xn[:, q, 0, :, 0:D]).then_inc(d_copy, 1)

                def silu(t, c):
                    if started(t, 1) and c == 0:
                        act.wait_ge(d_y, t)
                    act.wait_ge(d_up, HC * t + c + 1)
                    act.activation(hT[:, c, :], pH[:, c % 2, :], ACT.Silu).then_inc(d_h, 1)

                def body(t, q):
                    silu(t, 0)
                    silu(t, 1)
                    if started(t, 1):
                        act.wait_ge(d_s, 2 * t)
                    for i in range(2):
                        act.wait_ge(d_qk, 2 * t + i + 1)
                        act.activation(qkT[:, i, :], pM[:, i, :], ACT.Identity,
                                       bias=bqk1[:, i:i + 1]).then_inc(d_qks, 1)
                    silu(t, 2)
                    silu(t, 3)
                    if not is_last(t, NT):
                        copy_xT(t + 1, (q + 1) % 4)
                copy_xT(0, 0)
                sweep(act, NT, body, 4)

            @block.vector
            def _(dve):
                def first_sum(t, q):
                    s = q % 2
                    dve.wait_ge(d_x[q], 12 * (t - q) + 48)
                    dve.tensor_tensor(acc[:, q, :, :], acc[:, q, :, :], ye[:, s, :, :], ALU.add).then_inc(d_sum, 1)
                    dve.wait_ge(d_wo, t + 1)
                    dve.wait_ge(d_sum, t + 1)
                    dve.tensor_tensor(acc[:, q, :, :], pC[:], acc[:, q, :, :], ALU.add).then_inc(d_x1, 1)
                    dve.wait_ge(d_x1, t + 1)
                    row_statistics(dve, st[:], mv[:], acc[:, q, :, :], d_st, t, settled).then_inc(d_agg, 1)

                def norm(t, q):
                    dve.wait_ge(d_rs, t + 1)
                    if started(t, 4):
                        dve.wait_ge(d_sc[q], 4 * TOPK * SUB * (t - q))
                    for i in range(TOPK):
                        dve.tensor_copy(xn[:, q, i, :, D:DR].bitcast(U32),
                                        dest1[:, i, bass.ds(t * SUB, SUB)].unsqueeze(2))
                    for j in range(SUB):
                        ins = dve.tensor_scalar(xn[:, q, 0, j, 0:D], acc[:, q, j, :], mv[:, j, 0:1], rs[:, j:j + 1],
                                                ALU.subtract, ALU.mult)
                    ins.then_inc(d_xn, 1)

                def choose(t):
                    link = chain(dve, d_route, LINKS1 * t)
                    dve.wait_ge(d_lg, t + 1)
                    dve.tensor_copy(rt.lg[:], pL[:]).then_inc(d_lgs, 1)
                    dve.wait_ge(d_lgs, t + 1)
                    first_of_largest(dve, link, rt.lg, rt.oh[0], rt.m[0][:], rt.c[0], SUB)
                    link(dve.tensor_scalar(rt.lg2[:], rt.oh[0][:], PRIO_NONE, None, ALU.mult))
                    link(dve.tensor_tensor(rt.lg2[:], rt.lg2[:], rt.lg[:], ALU.add))
                    first_of_largest(dve, link, rt.lg2, rt.oh[1], rt.m[1][:], rt.c[1], SUB)
                    link(dve.tensor_tensor(rt.hit[:], rt.oh[0][:], rt.oh[1][:], ALU.add))
                    dve.sem_inc(d_hit, 1)
                    for i in range(TOPK):
                        dve.tensor_copy(top1[:, i, bass.ds(t * SUB, SUB)], rt.m[i][:])

                def assign(t, q):
                    dve.wait_ge(d_cnt, t + 1)
                    assign_rows(dve, chain(dve, d_route, LINKS1 * t + 13), rt, pG, rows1,
                                [idx[:, q, i, :] for i in range(TOPK)])

                def finish(t, q):
                    link = chain(dve, d_ln, t * LINKS)
                    dve.wait_ge(d_rs2, t + 1)
                    for j in range(SUB):
                        ins = dve.tensor_scalar(o[:, j, :], o[:, j, :], mv2[:, j, 0:1], rs2[:, j:j + 1],
                                                ALU.subtract, ALU.mult)
                    link(ins)
                    link(dve.tensor_tensor(o[:], o[:], lnw[:].unsqueeze(1).broadcast_to([P, SUB, D]), ALU.mult))
                    link(dve.tensor_tensor(o[:], o[:], lnb[:].unsqueeze(1).broadcast_to([P, SUB, D]), ALU.add))
                    dve.wait_ge(d_ys, t + 1)
                    dve.tensor_tensor(acc[:, q, :, :], acc[:, q, :, :], o[:], ALU.add).then_inc(d_acc, 1)

                def body(t, q):
                    s = q % 2
                    if not is_last(t, NT):
                        first_sum(t + 1, (q + 1) % 4)
                    choose(t)
                    if not is_last(t, NT):
                        norm(t + 1, (q + 1) % 4)
                    dve.wait_ge(d_v, t + 1)
                    if started(t, 1):
                        dve.wait_ge(d_o, t)
                    dve.tensor_tensor(v[:], pV[:], bv1[:].unsqueeze(1).broadcast_to([P, SUB, D]),
                                      ALU.add).then_inc(d_vs, 1)
                    for b in range(2):
                        dve.wait_ge(d_s, 2 * t + b + 1)
                        sc = pM[:, b, :].rearrange("p (n q) -> p n q", q=P)
                        dve.scalar_tensor_tensor(
                            sm[:, b, 0:2, :], sc[:, 0:2, :], SCALE1,
                            mdiag[:].unsqueeze(1).broadcast_to([P, 2, P]),
                            ALU.mult, ALU.mult).then_inc(d_sm, 1)
                        dve.scalar_tensor_tensor(sm[:, b, 2, :], sc[:, 2, :], SCALE1, mcross[:],
                                                 ALU.mult, ALU.mult).then_inc(d_sm, 1)
                    if started(t, 1):
                        finish(t - 1, (q + 3) % 4)
                    dve.wait_ge(d_y, t + 1)
                    dve.tensor_tensor(acc[:, q, :, :], pY[:], acc[:, q, :, :], ALU.add).then_inc(d_ys, 1)
                    dve.wait_ge(d_o, t + 1)
                    if started(t, 1):
                        dve.wait_ge(d_acc, t)
                    dve.tensor_copy(o[:], pM[:, 0, :].rearrange("p (j d) -> p j d", d=D)).then_inc(d_os, 1)
                    assign(t, q)
                    dve.wait_ge(d_os, t + 1)
                    row_statistics(dve, st2[:], mv2[:], o[:], d_st2, t, settled).then_inc(d_agg2, 1)

                first_sum(0, 0)
                norm(0, 0)
                sweep(dve, NT, body, 4)
                finish(NT - 1, 3)

            @block.gpsimd
            def _(pool):
                def first_norm(t):
                    pool.wait_ge(d_agg, t + 1)
                    inverse_deviation(pool, mv[:], rs[:], eps, mhalf, d_ve, t).then_inc(d_rs, 1)

                def scatter(t, q):
                    pool.wait_ge(d_copy, t + 1)
                    pool.wait_ge(d_route, LINKS1 * (t + 1))
                    settle(pool, settled)
                    for i in range(TOPK):
                        for j in range(SUB):
                            pool.indirect_dma_start(
                                out=xs1_d, out_offset=bass.IndirectOffsetOnAxis(idx[:, q, i, j:j + 1], 0),
                                in_=xn[:, q, i, j, :], in_offset=None).then_inc(d_sc[q], 16)

                def body(t, q):
                    if not is_last(t, NT):
                        first_norm(t + 1)
                    if started(t, 1):
                        scatter(t - 1, (q + 3) % 4)
                    pool.wait_ge(d_agg2, t + 1)
                    inverse_deviation(pool, mv2[:], rs2[:], eps, mhalf, d_ve2, t).then_inc(d_rs2, 1)
                first_norm(0)
                sweep(pool, NT, body, 4)
                scatter(NT - 1, 3)
                for q in range(4):
                    pool.wait_ge(d_sc[q], 4 * TOPK * SUB * NT)

        with ExitStack() as ph:
            pad_steps, table_steps = blocks("r1", 1, rows1, TOPK * T, xs1_d, eb1, bs1, NB1, ph)
            block = ph.enter_context(nc.Block())

            @block.gpsimd
            def _(pool):
                pad_steps(pool)

            @block.vector
            def _(dve):
                table_steps(dve)
        experts("x1", 1, xs1_d, y1_d, eb1, bs1, NB1, NB0)

        with ExitStack() as ph:
            gate = sb("f_gate", [P, TOPK, NS], F32, ph)
            low = sb("f_low", [P, NS], F32, ph)
            gt = sb("f_gt", [P, 4, TOPK, SUB], F32, ph)
            ye = sb("f_ye", [P, 4, SUB, TOPK, D], F32, ph)
            acc = sb("f_acc", [P, 4, SUB, D], F32, ph)
            f_x = [sem(f"f_x{i}") for i in range(4)]
            f_i = sem("f_i")
            f_gate = sem("f_gate_s")
            f_exp = sem("f_exp")
            f_1 = sem("f_1")
            f_2 = sem("f_2")
            f_out = [sem(f"f_out{i}") for i in range(4)]

            block = ph.enter_context(nc.Block())

            @block.sync
            def _(sp):
                def body(t, s):
                    if started(t, 4):
                        sp.wait_ge(f_out[s], 4 * (t - s))
                    settle(sp, settled)
                    sp.dma_start(acc[:, s, :, :], x2_d[:, bass.ds(t * SUB, SUB), :]).then_inc(f_x[s], 16)
                    sp.dma_start(ye[:, s, :, :, :], y1_v[:, bass.ds(t * SUB, SUB), :, :]).then_inc(f_x[s], 16)
                sweep(sp, NT, body, 4)

            @block.vector
            def _(dve):
                def gates_of(t, s):
                    if started(t, 4):
                        dve.wait_ge(f_2, t - 3)
                    for i in range(TOPK):
                        ins = dve.tensor_copy(gt[:, s, i, :], gate[:, i, bass.ds(t * SUB, SUB)])
                    ins.then_inc(f_i, 1)

                def body(t, s):
                    dve.wait_ge(f_i, t + 1)
                    dve.wait_ge(f_x[s], 8 * (t - s) + 32)
                    for i, done in enumerate((f_1, f_2)):
                        for j in range(SUB):
                            ins = dve.scalar_tensor_tensor(acc[:, s, j, :], ye[:, s, j, i, :],
                                                           gt[:, s, i, j:j + 1], acc[:, s, j, :],
                                                           ALU.mult, ALU.add)
                        ins.then_inc(done, 1)
                        if i == 0:
                            dve.wait_ge(f_1, t + 1)
                    if not beyond(t, 2, NT):
                        gates_of(t + 2, (s + 2) % 4)
                link = chain(dve, f_gate, 0)
                link(dve.tensor_tensor(low[:], top1[:, 1, :], top1[:, 0, :], ALU.subtract))
                dve.wait_ge(f_exp, 1)
                link(dve.tensor_scalar(gate[:, 1, :], low[:], 1.0, None, ALU.add))
                link(dve.reciprocal(gate[:, 0, :], gate[:, 1, :]))
                link(dve.tensor_tensor(gate[:, 1, :], low[:], gate[:, 0, :], ALU.mult))
                gates_of(0, 0)
                gates_of(1, 1)
                sweep(dve, NT, body, 4)

            @block.scalar
            def _(act):
                def body(t, s):
                    act.wait_ge(f_2, t + 1)
                    act.dma_start(out_v[:, bass.ds(t * SUB, SUB), :], acc[:, s, :, :]).then_inc(f_out[s], 16)
                act.wait_ge(f_gate, 1)
                act.activation(low[:], low[:], ACT.Exp).then_inc(f_exp, 1)
                sweep(act, NT, body, 4)
                for s in range(4):
                    act.wait_ge(f_out[s], 4 * NT)


_INS = ['L0_attn_x', 'L0_attn_Wq', 'L0_attn_bq', 'L0_attn_Wk', 'L0_attn_bk', 'L0_attn_Wv', 'L0_attn_bv',
        'L0_attn_Wo', 'L0_attn_bo', 'L0_ffn_gate_w', 'L0_ffn_gate_b', 'L0_ffn_w1', 'L0_ffn_b1', 'L0_ffn_w2',
        'L0_ffn_b2', 'L1_attn_W_qkv', 'L1_attn_b_qkv', 'L1_attn_ln_w', 'L1_attn_ln_b', 'L1_ffn_shared_w1',
        'L1_ffn_shared_w2', 'L1_ffn_experts_w1', 'L1_ffn_experts_w2', 'L1_ffn_gate_w']


def kernel(**inputs):
    import numpy as _np
    import concourse.bacc as _bacc
    from concourse import mybir as _mybir
    from concourse.bass_utils import run_bass_kernel_spmd as _run

    nc = _bacc.Bacc("TRN2", target_bir_lowering=False, num_devices=1)
    arrays, args = {}, []
    for name in _INS:
        a = _np.ascontiguousarray(inputs[name])
        arrays[f"in_{name}_dram"] = a
        args.append(nc.dram_tensor(f"in_{name}_dram", a.shape, _mybir.dt.from_np(a.dtype),
                                   kind="ExternalInput").ap())
    args.append(nc.dram_tensor("out_0_dram", (B, S, D), _mybir.dt.float32, kind="ExternalOutput").ap())
    layer_kernel(nc, *args)
    r = _run(nc, [arrays], core_ids=[0])
    return r.results[0]["out_0_dram"]
```
